# Optimizing a Trainium2 kernel written in Bass

```python
import numpy as np
import jax
import jax.numpy as jnp

def _softmax(x, axis=-1):
    return jax.nn.softmax(x, axis=axis)

def _gelu(x):
    return jax.nn.gelu(x, approximate=True)

def _silu(x):
    return jax.nn.silu(x)

def _sigmoid(x):
    return jax.nn.sigmoid(x)

def _layernorm(x, axis=-1, eps=1e-05):
    m = jnp.mean(x, axis=axis, keepdims=True)
    v = jnp.var(x, axis=axis, keepdims=True)
    return (x - m) / jnp.sqrt(v + eps)

def _scatter_add(tgt, idx, src, axis=0):
    return tgt.at[idx].add(src)

def _segment_sum(src, seg, n):
    return jax.ops.segment_sum(src, seg, n)
kernel_name = 'mk_sandwich_d2_jaxref_r8_f2eb36'

def setup_inputs(seed: int=0):
    np.random.seed(seed)
    _w = jnp.asarray

    def _L0_attn_setup():
        import jax, jax.numpy as jnp
        import numpy as np
        H = 128
        D = 32
        CHUNK = 64
        LR = 0.1
        GRAD_SCALE = 0.1
        MAX_GRAD_NORM = 1.0
        EPS = 1e-06
        P = 2 * D * D

        def _xavier(k, shape, gain=0.1):
            fan_out, fan_in = shape
            a = gain * np.sqrt(6.0 / (fan_in + fan_out))
            return jax.random.uniform(k, shape, jnp.float32, -a, a)

        def _causal_dwconv(x, w, b):
            T = x.shape[1]
            xp = jnp.pad(x, ((0, 0), (3, 0), (0, 0)))
            y = b
            for j in range(4):
                y = y + xp[:, j:j + T, :] * w[:, j]
            return y

        def _mem_loss(p, k_t, v_t):
            W1 = p[:D * D].reshape(D, D)
            W2 = p[D * D:].reshape(D, D)
            pred = jax.nn.silu(k_t @ W1.T) @ W2.T
            return jnp.sum((pred - v_t) ** 2)
        _grad_fn = jax.vmap(jax.vmap(jax.grad(_mem_loss), in_axes=(None, 0, 0)), in_axes=(0, 0, 0))

        def _forward(hidden, Wk, Wv, Wq, Wo, ckw, ckb, cvw, cvb, cqw, cqb, mW1, mW2, aW, ab, eW, eb, tW, tb, norm_g, gW, gb):
            B, S, _ = hidden.shape
            k = _causal_dwconv(hidden @ Wk.T, ckw, ckb)
            v = _causal_dwconv(hidden @ Wv.T, cvw, cvb)
            q = _causal_dwconv(hidden @ Wq.T, cqw, cqb)
            alpha = (jax.nn.sigmoid(hidden @ aW.T + ab) * 0.1).mean(-1)
            eta = (jax.nn.sigmoid(hidden @ eW.T + eb) * 0.9 + 0.05).mean(-1)
            theta = (jax.nn.softplus(hidden @ tW.T + tb) * LR).mean(-1)
            W_state = jnp.tile(jnp.concatenate([mW1.ravel(), mW2.ravel()])[None], (B, 1))
            S_state = jnp.zeros_like(W_state)

            def step(carry, xs):
                Sm, Wm = carry
                gt, et, tt, at = xs
                Sm = et[:, None] * Sm - tt[:, None] * gt
                Wm = (1.0 - at[:, None]) * Wm + Sm
                return ((Sm, Wm), Wm)
            outs = []
            for c0 in range(0, S, CHUNK):
                sl = slice(c0, c0 + CHUNK)
                g = _grad_fn(W_state, k[:, sl], v[:, sl]) * GRAD_SCALE
                gn = jnp.maximum(jnp.linalg.norm(g, axis=-1, keepdims=True), EPS)
                g = g * jnp.minimum(MAX_GRAD_NORM / gn, 1.0)
                g = jax.lax.stop_gradient(g)
                xs = (jnp.swapaxes(g, 0, 1), eta[:, sl].T, theta[:, sl].T, alpha[:, sl].T)
                (S_state, W_state), Wtraj = jax.lax.scan(step, (S_state, W_state), xs)
                Wtraj = jnp.swapaxes(Wtraj, 0, 1)
                T = Wtraj.shape[1]
                W1t = Wtraj[..., :D * D].reshape(B, T, D, D)
                W2t = Wtraj[..., D * D:].reshape(B, T, D, D)
                h = jax.nn.silu(jnp.einsum('btd,btod->bto', q[:, sl], W1t))
                outs.append(jnp.einsum('bto,btpo->btp', h, W2t))
            retrieved = jnp.concatenate(outs, axis=1)
            out = retrieved @ Wo.T
            out = out * jax.lax.rsqrt(jnp.mean(out * out, -1, keepdims=True) + EPS) * norm_g
            gate = hidden @ gW.T + gb
            return out * gate
        key = jax.random.key(seed)
        ks = jax.random.split(key, 24)
        B, S = (1, 128)
        return {'hidden': jax.random.normal(ks[0], (B, S, H), jnp.float32), 'Wk': _xavier(ks[1], (D, H)), 'Wv': _xavier(ks[2], (D, H)), 'Wq': _xavier(ks[3], (D, H)), 'Wo': _xavier(ks[4], (H, D)), 'ckw': jax.random.normal(ks[5], (D, 4), jnp.float32) * 0.05, 'ckb': jnp.zeros((D,), jnp.float32), 'cvw': jax.random.normal(ks[6], (D, 4), jnp.float32) * 0.05, 'cvb': jnp.zeros((D,), jnp.float32), 'cqw': jax.random.normal(ks[7], (D, 4), jnp.float32) * 0.05, 'cqb': jnp.zeros((D,), jnp.float32), 'mW1': _xavier(ks[8], (D, D)), 'mW2': _xavier(ks[9], (D, D)), 'aW': jax.random.normal(ks[10], (D, H), jnp.float32) * 0.02, 'ab': jnp.zeros((D,), jnp.float32), 'eW': jax.random.normal(ks[11], (D, H), jnp.float32) * 0.02, 'eb': jnp.zeros((D,), jnp.float32), 'tW': jax.random.normal(ks[12], (D, H), jnp.float32) * 0.02, 'tb': jnp.zeros((D,), jnp.float32), 'norm_g': jnp.ones((H,), jnp.float32), 'gW': jnp.zeros((H, H), jnp.float32), 'gb': jnp.ones((H,), jnp.float32)}
    _L0_attn_in = _L0_attn_setup()

    def _L0_ffn_setup():
        import jax, jax.numpy as jnp
        import numpy as np
        E = 8
        H = 128
        M = 256
        K = 2
        SE = 1
        BSZ, SEQ = (2, 128)
        W_SCALE = 0.02
        key = jax.random.key(seed)
        ks = jax.random.split(key, 9)
        return {'x': jax.random.normal(ks[0], (BSZ, SEQ, H), jnp.float32), 'gate_w': jax.random.normal(ks[1], (E, H), jnp.float32) * W_SCALE, 'beta': jnp.zeros((E,), jnp.float32), 'gate_proj_w': jax.random.normal(ks[2], (E, H, M), jnp.float32) * W_SCALE, 'up_proj_w': jax.random.normal(ks[3], (E, H, M), jnp.float32) * W_SCALE, 'down_proj_w': jax.random.normal(ks[4], (E, M, H), jnp.float32) * W_SCALE, 'shared_gate_w': jax.random.normal(ks[5], (SE, H, M), jnp.float32) * W_SCALE, 'shared_up_w': jax.random.normal(ks[6], (SE, H, M), jnp.float32) * W_SCALE, 'shared_down_w': jax.random.normal(ks[7], (SE, M, H), jnp.float32) * W_SCALE}
    _L0_ffn_in = _L0_ffn_setup()

    def _L1_attn_setup():
        import jax, jax.numpy as jnp
        import numpy as np
        B, L, DIM, S, K = (2, 256, 128, 16, 3)
        INNER = DIM
        key = jax.random.key(seed)
        ks = jax.random.split(key, 10)
        f = lambda k, shape, s=0.02: jax.random.normal(k, shape, jnp.float32) * s
        return {'x': jax.random.normal(ks[0], (B, L, DIM), jnp.float32), 'gamma': jnp.ones((DIM,), jnp.float32), 'beta': jnp.zeros((DIM,), jnp.float32), 'W_in': f(ks[1], (2 * INNER, DIM)), 'conv_w': f(ks[2], (INNER, 1, K), 0.2), 'W_x': f(ks[3], (2 * S, INNER)), 'W_dt': f(ks[4], (INNER, DIM)), 'b_dt': f(ks[5], (INNER,), 0.1), 'A_log': jax.random.normal(ks[6], (INNER, S), jnp.float32), 'D_param': jnp.ones((INNER,), jnp.float32), 'W_out': f(ks[7], (DIM, INNER))}
    _L1_attn_in = _L1_attn_setup()

    def _L1_ffn_setup():
        import jax, jax.numpy as jnp
        import numpy as np
        D_MODEL = 128
        D_FF = 256
        N_EXPERTS = 8
        TOP_K = 2
        CLAMP = 10000.0
        ROUTER_EPS = 1e-08
        LN_EPS = 1e-05

        def _layernorm(x, g, b):
            mu = jnp.mean(x, axis=-1, keepdims=True)
            var = jnp.mean(jnp.square(x - mu), axis=-1, keepdims=True)
            return (x - mu) * jax.lax.rsqrt(var + LN_EPS) * g + b
        key = jax.random.key(seed)
        k1, k2, k3, k4 = jax.random.split(key, 4)
        B, S = (8, 128)
        x = jax.random.normal(k1, (B, S, D_MODEL), dtype=jnp.float32)
        ln_gamma = jnp.ones((D_MODEL,), jnp.float32)
        ln_beta = jnp.zeros((D_MODEL,), jnp.float32)
        bound = 0.02 * float(np.sqrt(3.0))
        router_w = jax.random.uniform(k2, (N_EXPERTS, D_MODEL), jnp.float32, -bound, bound)
        gate_up_w = jax.random.normal(k3, (N_EXPERTS, 2 * D_FF, D_MODEL), jnp.float32) * (1.0 / np.sqrt(D_MODEL))
        down_w = jax.random.normal(k4, (N_EXPERTS, D_MODEL, D_FF), jnp.float32) * (1.0 / np.sqrt(D_FF))
        return {'x': x, 'ln_gamma': ln_gamma, 'ln_beta': ln_beta, 'router_w': router_w, 'gate_up_w': gate_up_w, 'down_w': down_w}
    _L1_ffn_in = _L1_ffn_setup()
    _d = {'L0_attn_hidden': _L0_attn_in['hidden'], 'L0_attn_Wk': _L0_attn_in['Wk'], 'L0_attn_Wv': _L0_attn_in['Wv'], 'L0_attn_Wq': _L0_attn_in['Wq'], 'L0_attn_Wo': _L0_attn_in['Wo'], 'L0_attn_ckw': _L0_attn_in['ckw'], 'L0_attn_ckb': _L0_attn_in['ckb'], 'L0_attn_cvw': _L0_attn_in['cvw'], 'L0_attn_cvb': _L0_attn_in['cvb'], 'L0_attn_cqw': _L0_attn_in['cqw'], 'L0_attn_cqb': _L0_attn_in['cqb'], 'L0_attn_mW1': _L0_attn_in['mW1'], 'L0_attn_mW2': _L0_attn_in['mW2'], 'L0_attn_aW': _L0_attn_in['aW'], 'L0_attn_ab': _L0_attn_in['ab'], 'L0_attn_eW': _L0_attn_in['eW'], 'L0_attn_eb': _L0_attn_in['eb'], 'L0_attn_tW': _L0_attn_in['tW'], 'L0_attn_tb': _L0_attn_in['tb'], 'L0_attn_norm_g': _L0_attn_in['norm_g'], 'L0_attn_gW': _L0_attn_in['gW'], 'L0_attn_gb': _L0_attn_in['gb'], 'L0_ffn_gate_w': _L0_ffn_in['gate_w'], 'L0_ffn_beta': _L0_ffn_in['beta'], 'L0_ffn_gate_proj_w': _L0_ffn_in['gate_proj_w'], 'L0_ffn_up_proj_w': _L0_ffn_in['up_proj_w'], 'L0_ffn_down_proj_w': _L0_ffn_in['down_proj_w'], 'L0_ffn_shared_gate_w': _L0_ffn_in['shared_gate_w'], 'L0_ffn_shared_up_w': _L0_ffn_in['shared_up_w'], 'L0_ffn_shared_down_w': _L0_ffn_in['shared_down_w'], 'L1_attn_gamma': _L1_attn_in['gamma'], 'L1_attn_beta': _L1_attn_in['beta'], 'L1_attn_W_in': _L1_attn_in['W_in'], 'L1_attn_conv_w': _L1_attn_in['conv_w'], 'L1_attn_W_x': _L1_attn_in['W_x'], 'L1_attn_W_dt': _L1_attn_in['W_dt'], 'L1_attn_b_dt': _L1_attn_in['b_dt'], 'L1_attn_A_log': _L1_attn_in['A_log'], 'L1_attn_D_param': _L1_attn_in['D_param'], 'L1_attn_W_out': _L1_attn_in['W_out'], 'L1_ffn_ln_gamma': _L1_ffn_in['ln_gamma'], 'L1_ffn_ln_beta': _L1_ffn_in['ln_beta'], 'L1_ffn_router_w': _L1_ffn_in['router_w'], 'L1_ffn_gate_up_w': _L1_ffn_in['gate_up_w'], 'L1_ffn_down_w': _L1_ffn_in['down_w']}
    _x0 = _d['L0_attn_hidden']
    _d['L0_attn_hidden'] = jax.random.normal(jax.random.fold_in(jax.random.key(seed), 1), (8, 512, 128), dtype=_x0.dtype)
    del _x0
    return _d

def reference(L0_attn_hidden, L0_attn_Wk, L0_attn_Wv, L0_attn_Wq, L0_attn_Wo, L0_attn_ckw, L0_attn_ckb, L0_attn_cvw, L0_attn_cvb, L0_attn_cqw, L0_attn_cqb, L0_attn_mW1, L0_attn_mW2, L0_attn_aW, L0_attn_ab, L0_attn_eW, L0_attn_eb, L0_attn_tW, L0_attn_tb, L0_attn_norm_g, L0_attn_gW, L0_attn_gb, L0_ffn_gate_w, L0_ffn_beta, L0_ffn_gate_proj_w, L0_ffn_up_proj_w, L0_ffn_down_proj_w, L0_ffn_shared_gate_w, L0_ffn_shared_up_w, L0_ffn_shared_down_w, L1_attn_gamma, L1_attn_beta, L1_attn_W_in, L1_attn_conv_w, L1_attn_W_x, L1_attn_W_dt, L1_attn_b_dt, L1_attn_A_log, L1_attn_D_param, L1_attn_W_out, L1_ffn_ln_gamma, L1_ffn_ln_beta, L1_ffn_router_w, L1_ffn_gate_up_w, L1_ffn_down_w):

    def _L0_attn_ref(hidden, Wk, Wv, Wq, Wo, ckw, ckb, cvw, cvb, cqw, cqb, mW1, mW2, aW, ab, eW, eb, tW, tb, norm_g, gW, gb):
        import jax, jax.numpy as jnp
        import numpy as np
        H = 128
        D = 32
        CHUNK = 64
        LR = 0.1
        GRAD_SCALE = 0.1
        MAX_GRAD_NORM = 1.0
        EPS = 1e-06
        P = 2 * D * D

        def _xavier(k, shape, gain=0.1):
            fan_out, fan_in = shape
            a = gain * np.sqrt(6.0 / (fan_in + fan_out))
            return jax.random.uniform(k, shape, jnp.float32, -a, a)

        def _causal_dwconv(x, w, b):
            T = x.shape[1]
            xp = jnp.pad(x, ((0, 0), (3, 0), (0, 0)))
            y = b
            for j in range(4):
                y = y + xp[:, j:j + T, :] * w[:, j]
            return y

        def _mem_loss(p, k_t, v_t):
            W1 = p[:D * D].reshape(D, D)
            W2 = p[D * D:].reshape(D, D)
            pred = jax.nn.silu(k_t @ W1.T) @ W2.T
            return jnp.sum((pred - v_t) ** 2)
        _grad_fn = jax.vmap(jax.vmap(jax.grad(_mem_loss), in_axes=(None, 0, 0)), in_axes=(0, 0, 0))

        def _forward(hidden, Wk, Wv, Wq, Wo, ckw, ckb, cvw, cvb, cqw, cqb, mW1, mW2, aW, ab, eW, eb, tW, tb, norm_g, gW, gb):
            B, S, _ = hidden.shape
            k = _causal_dwconv(hidden @ Wk.T, ckw, ckb)
            v = _causal_dwconv(hidden @ Wv.T, cvw, cvb)
            q = _causal_dwconv(hidden @ Wq.T, cqw, cqb)
            alpha = (jax.nn.sigmoid(hidden @ aW.T + ab) * 0.1).mean(-1)
            eta = (jax.nn.sigmoid(hidden @ eW.T + eb) * 0.9 + 0.05).mean(-1)
            theta = (jax.nn.softplus(hidden @ tW.T + tb) * LR).mean(-1)
            W_state = jnp.tile(jnp.concatenate([mW1.ravel(), mW2.ravel()])[None], (B, 1))
            S_state = jnp.zeros_like(W_state)

            def step(carry, xs):
                Sm, Wm = carry
                gt, et, tt, at = xs
                Sm = et[:, None] * Sm - tt[:, None] * gt
                Wm = (1.0 - at[:, None]) * Wm + Sm
                return ((Sm, Wm), Wm)
            outs = []
            for c0 in range(0, S, CHUNK):
                sl = slice(c0, c0 + CHUNK)
                g = _grad_fn(W_state, k[:, sl], v[:, sl]) * GRAD_SCALE
                gn = jnp.maximum(jnp.linalg.norm(g, axis=-1, keepdims=True), EPS)
                g = g * jnp.minimum(MAX_GRAD_NORM / gn, 1.0)
                g = jax.lax.stop_gradient(g)
                xs = (jnp.swapaxes(g, 0, 1), eta[:, sl].T, theta[:, sl].T, alpha[:, sl].T)
                (S_state, W_state), Wtraj = jax.lax.scan(step, (S_state, W_state), xs)
                Wtraj = jnp.swapaxes(Wtraj, 0, 1)
                T = Wtraj.shape[1]
                W1t = Wtraj[..., :D * D].reshape(B, T, D, D)
                W2t = Wtraj[..., D * D:].reshape(B, T, D, D)
                h = jax.nn.silu(jnp.einsum('btd,btod->bto', q[:, sl], W1t))
                outs.append(jnp.einsum('bto,btpo->btp', h, W2t))
            retrieved = jnp.concatenate(outs, axis=1)
            out = retrieved @ Wo.T
            out = out * jax.lax.rsqrt(jnp.mean(out * out, -1, keepdims=True) + EPS) * norm_g
            gate = hidden @ gW.T + gb
            return out * gate
        return _forward(hidden, Wk, Wv, Wq, Wo, ckw, ckb, cvw, cvb, cqw, cqb, mW1, mW2, aW, ab, eW, eb, tW, tb, norm_g, gW, gb)

    def _L0_ffn_ref(x, gate_w, beta, gate_proj_w, up_proj_w, down_proj_w, shared_gate_w, shared_up_w, shared_down_w):
        import jax, jax.numpy as jnp
        import numpy as np
        E = 8
        H = 128
        M = 256
        K = 2
        SE = 1
        BSZ, SEQ = (2, 128)
        W_SCALE = 0.02
        B0, S0, H0 = x.shape
        xt = x.reshape(-1, H0)
        B = xt.shape[0]
        logits = xt @ gate_w.T
        _, idx = jax.lax.top_k(logits + beta, K)
        probs = jax.nn.sigmoid(jnp.take_along_axis(logits, idx, axis=-1))
        c = jnp.zeros((B, E), xt.dtype).at[jnp.arange(B)[:, None], idx].add(probs)
        g = jnp.einsum('bh,ehm->bem', xt, gate_proj_w)
        u = jnp.einsum('bh,ehm->bem', xt, up_proj_w)
        h = jax.nn.silu(g) * u
        eo = jnp.einsum('bem,emh->beh', h, down_proj_w)
        combined = jnp.einsum('beh,be->bh', eo, c)
        sg = jnp.einsum('bh,ehm->bem', xt, shared_gate_w)
        su = jnp.einsum('bh,ehm->bem', xt, shared_up_w)
        sh = jax.nn.silu(sg) * su
        shared_out = jnp.einsum('bem,emh->beh', sh, shared_down_w).sum(axis=1)
        return (combined + shared_out).reshape(B0, S0, H0)

    def _L1_attn_ref(x, gamma, beta, W_in, conv_w, W_x, W_dt, b_dt, A_log, D_param, W_out):
        import jax, jax.numpy as jnp
        import numpy as np
        B, L, DIM, S, K = (2, 256, 128, 16, 3)
        INNER = DIM
        residual = x
        mu = jnp.mean(x, axis=-1, keepdims=True)
        var = jnp.var(x, axis=-1, keepdims=True)
        h = (x - mu) / jnp.sqrt(var + 1e-05) * gamma + beta
        xz = jnp.einsum('bld,ed->ble', h, W_in)
        inner = W_in.shape[0] // 2
        xx, z = (xz[..., :inner], xz[..., inner:])
        k = conv_w.shape[-1]
        pad = (k - 1) // 2
        xc = jax.lax.conv_general_dilated(xx.transpose(0, 2, 1), conv_w, window_strides=(1,), padding=[(pad, pad)], dimension_numbers=('NCL', 'OIL', 'NCL'), feature_group_count=inner).transpose(0, 2, 1)
        xc = jax.nn.silu(xc)
        dt = jnp.einsum('bld,ed->ble', xc, W_dt) + b_dt
        BC = jnp.einsum('bld,ed->ble', xc, W_x)
        s = A_log.shape[-1]
        Bm, Cm = (BC[..., :s], BC[..., s:])
        A = -jnp.exp(A_log)
        dt = jax.nn.softplus(dt)
        dA = jnp.exp(jnp.einsum('bld,ds->blds', dt, A))
        dB = jnp.einsum('bld,bls->blds', dt, Bm)

        def step(state, inputs):
            dA_t, dB_t, C_t = inputs
            state = state * dA_t + dB_t
            y_t = jnp.einsum('bds,bs->bd', state, C_t)
            return (state, y_t)
        init = jnp.zeros((x.shape[0], inner, s), xc.dtype)
        _, ys = jax.lax.scan(step, init, (dA.transpose(1, 0, 2, 3), dB.transpose(1, 0, 2, 3), Cm.transpose(1, 0, 2)))
        y = ys.transpose(1, 0, 2)
        y = y + D_param * xc
        y = y * jax.nn.silu(z)
        out = jnp.einsum('bld,ed->ble', y, W_out)
        return out + residual

    def _L1_ffn_ref(x, ln_gamma, ln_beta, router_w, gate_up_w, down_w):
        import jax, jax.numpy as jnp
        import numpy as np
        D_MODEL = 128
        D_FF = 256
        N_EXPERTS = 8
        TOP_K = 2
        CLAMP = 10000.0
        ROUTER_EPS = 1e-08
        LN_EPS = 1e-05

        def _layernorm(x, g, b):
            mu = jnp.mean(x, axis=-1, keepdims=True)
            var = jnp.mean(jnp.square(x - mu), axis=-1, keepdims=True)
            return (x - mu) * jax.lax.rsqrt(var + LN_EPS) * g + b
        B, S, D = x.shape
        xn = _layernorm(x, ln_gamma, ln_beta)
        xf = xn.reshape(-1, D)
        N = xf.shape[0]
        logits = jnp.clip(xf @ router_w.T, -CLAMP, CLAMP)
        m = jnp.max(logits, axis=-1, keepdims=True)
        e = jnp.exp(logits - m)
        probs = e / (jnp.sum(e, axis=-1, keepdims=True) + ROUTER_EPS)
        probs = jnp.clip(probs, ROUTER_EPS, 1.0)
        topk_p, topk_i = jax.lax.top_k(probs, TOP_K)
        dense_gate = jnp.zeros((N, N_EXPERTS), probs.dtype).at[jnp.arange(N)[:, None], topk_i].add(topk_p)
        out = jnp.zeros_like(xf)
        for eid in range(N_EXPERTS):
            xe = xf * dense_gate[:, eid:eid + 1]
            gu = xe @ gate_up_w[eid].T
            gate, up = jnp.split(gu, 2, axis=-1)
            hidden = jax.nn.silu(gate) * up
            out = out + hidden @ down_w[eid].T
        return x + out.reshape(B, S, D)
    x = L0_attn_hidden
    x = x + _layernorm(_L0_attn_ref(_layernorm(x, axis=-1), L0_attn_Wk, L0_attn_Wv, L0_attn_Wq, L0_attn_Wo, L0_attn_ckw, L0_attn_ckb, L0_attn_cvw, L0_attn_cvb, L0_attn_cqw, L0_attn_cqb, L0_attn_mW1, L0_attn_mW2, L0_attn_aW, L0_attn_ab, L0_attn_eW, L0_attn_eb, L0_attn_tW, L0_attn_tb, L0_attn_norm_g, L0_attn_gW, L0_attn_gb), axis=-1)
    x = x + _layernorm(_L0_ffn_ref(_layernorm(x, axis=-1), L0_ffn_gate_w, L0_ffn_beta, L0_ffn_gate_proj_w, L0_ffn_up_proj_w, L0_ffn_down_proj_w, L0_ffn_shared_gate_w, L0_ffn_shared_up_w, L0_ffn_shared_down_w), axis=-1)
    x = x + _layernorm(_L1_attn_ref(_layernorm(x, axis=-1), L1_attn_gamma, L1_attn_beta, L1_attn_W_in, L1_attn_conv_w, L1_attn_W_x, L1_attn_W_dt, L1_attn_b_dt, L1_attn_A_log, L1_attn_D_param, L1_attn_W_out), axis=-1)
    x = x + _layernorm(_L1_ffn_ref(_layernorm(x, axis=-1), L1_ffn_ln_gamma, L1_ffn_ln_beta, L1_ffn_router_w, L1_ffn_gate_up_w, L1_ffn_down_w), axis=-1)
    return x

_drawn_inputs = setup_inputs


def setup_inputs(seed=0):
    import zlib

    import numpy as np

    out = dict(_drawn_inputs(seed))
    spreads = {'L0_attn_ckb': (0.0, 0.1),
     'L0_attn_cvb': (0.0, 0.1),
     'L0_attn_cqb': (0.0, 0.1),
     'L0_attn_ab': (0.0, 2.0),
     'L0_attn_eb': (0.0, 0.8),
     'L0_attn_tb': (0.0, 0.8),
     'L0_attn_norm_g': (1.0, 0.2),
     'L0_attn_gW': (0.0, 0.1),
     'L0_attn_gb': (1.0, 0.2),
     'L0_ffn_beta': (0.0, 0.1),
     'L1_attn_gamma': (1.0, 0.6),
     'L1_attn_beta': (0.0, 0.8),
     'L1_attn_D_param': (1.0, 0.6),
     'L1_ffn_ln_gamma': (1.0, 0.6),
     'L1_ffn_ln_beta': (0.0, 0.8)}
    factors = {'L0_attn_Wk': 8.0,
     'L0_attn_Wv': 8.0,
     'L0_attn_ckw': 8.0,
     'L0_attn_cvw': 8.0,
     'L0_attn_aW': 8.0,
     'L0_attn_eW': 8.0,
     'L0_attn_tW': 8.0,
     'L1_attn_W_in': 8.0,
     'L1_attn_conv_w': 8.0,
     'L1_attn_W_x': 8.0,
     'L1_attn_W_dt': 8.0,
     'L1_attn_b_dt': 8.0,
     'L1_attn_A_log': 8.0,
     'L1_attn_W_out': 8.0,
     'L1_ffn_router_w': 8.0,
     'L1_ffn_gate_up_w': 8.0,
     'L1_ffn_down_w': 8.0}
    for name, (base, spread) in spreads.items():
        noise = np.random.default_rng([zlib.crc32(name.encode()), seed]).standard_normal(out[name].shape)
        drawn = base * np.exp(spread * noise) if base else spread * noise
        out[name] = jnp.asarray(drawn.astype(out[name].dtype))
    for name, factor in factors.items():
        out[name] = (out[name] * factor).astype(out[name].dtype)
    return out
```

```python
from contextlib import ExitStack, contextmanager

import numpy as np

import concourse.bass as bass
from concourse import mybir

F32 = mybir.dt.float32
BF16 = mybir.dt.bfloat16
I32 = mybir.dt.int32
ALU = mybir.AluOpType
ACT = mybir.ActivationFunctionType
AX = mybir.AxisListType.X

P = 128
BATCH, SEQ, H = 8, 512, 128
TOKENS = BATCH * SEQ
TILES = TOKENS // P
TPB = SEQ // P
GROUPS, B4 = 2, 4
D = 32
CHUNK = 64
CHUNKS = SEQ // CHUNK
EXPERTS, MID = 8, 256
SLOTS = 2 * TILES + EXPERTS
STATE = 16
EPS = 1e-5

PARTS = [
    ("proj", 6 * D), ("gate", H), ("gate_b", H), ("norm_g", H), ("wo", B4 * H),
    ("conv_w", 12), ("conv_b", 3), ("bias3", 3), ("mem", 2 * D),
    ("route0", EXPERTS), ("beta0", EXPERTS), ("route1", EXPERTS), ("ln_g", H), ("ln_b", H),
    ("w_in", 2 * H), ("w_bc", 3 * 2 * STATE), ("w_dt", H), ("w_out", H),
    ("sconv", 3), ("b_dt", 1), ("a_log", STATE), ("skip_d", 1), ("gamma", 1), ("beta", 1),
    ("ident", P), ("quad", P), ("neg_i", CHUNK), ("mean_bd", P), ("mean_sel", B4 * 64),
    ("before", P), ("ones", P), ("rank8", EXPERTS), ("edge", TILES), ("slot", SLOTS),
    ("pick", 2 * STATE),
]
AT = {}
_at = 0
for _name, _width in PARTS:
    AT[_name] = (_at, _width)
    _at += _width
PACKED = _at


class Count:

    def __init__(self):
        self.base, self.k = 0, 0

    def one(self):
        self.k += 1
        return 1

    @property
    def now(self):
        return self.base + self.k

    @contextmanager
    def loop(self, eng, n, per):
        start = self.now
        with eng.Fori(0, n) as i:
            self.base, self.k = start + i * per, 0
            yield i
            assert self.k == per, f"{self.k} increments in a round, {per} said"
        self.base, self.k = start + n * per, 0

STEPS_V = 15
SCRATCH = 20500


def build(nc, x_d, packed_d, up0_d, down0_d, up1_d, down1_d, out_d):
    ctx = ExitStack()
    with ctx:
        def sb(name, shape, dt=F32):
            return ctx.enter_context(nc.sbuf_tensor(name, shape, dt))

        def sem(name):
            return ctx.enter_context(nc.semaphore(name))

        xres = sb("xres", [P, TILES, H])
        pk = sb("pk", [P, PACKED])

        def par(name, a=0, b=None):
            at, width = AT[name]
            return pk[:, at + a:at + (width if b is None else b)]

        big = [sb(f"big{n}", [P, TOKENS]) for n in range(4)]
        experts_up = sb("experts_up", [P, EXPERTS + 1, 2 * MID])
        experts_down = sb("experts_down", [P, EXPERTS + 1, 2, H])
        scratch = sb("scratch", [P, SCRATCH])
        carved = [0]

        def carve(name, shape, dt=F32):
            n = int(np.prod(shape[1:])) // (2 if dt == BF16 else 1)
            a = scratch[:, carved[0]:carved[0] + n]
            carved[0] += n
            assert carved[0] <= SCRATCH, (name, carved[0])
            if dt != F32:
                a = a.bitcast(dt)
            axes = " ".join(f"a{k}" for k in range(1, len(shape)))
            if len(shape) == 2:
                return a
            return a.rearrange(f"p ({axes}) -> p {axes}", **{f"a{k}": shape[k] for k in range(1, len(shape))})

        ident, quad = par("ident"), par("quad")
        quad4 = quad.rearrange("p (b c) -> p b c", b=B4)
        pow_c = sb("pow_c", [P, TILES])
        st = sb("st", [P, TILES, 6])
        mean = sb("mean", [P, TILES])
        var = sb("var", [P, TILES])
        var2 = sb("var2", [P, TILES])
        rstd = sb("rstd", [P, TILES])
        rstd2 = sb("rstd2", [P, TILES])
        lnt = sb("lnt", [P, 3, TILES])

        bank = ctx.enter_context(nc.psum_tensor("bank", [P, 8, 512], F32))

        S = {}

        def sg(name):
            if name not in S:
                S[name] = sem(name)
            return S[name]

        v_step, p_step, a_step = sg("v_step"), sg("p_step"), sg("a_step")
        cv, cp, ca = Count(), Count(), Count()
        n_ln = [0]

        def moments(v, lo, hi, twice=False):
            n = hi - lo
            s = st[:, lo:hi, :]
            nc.vector.tensor_tensor(lnt[:, 0, 0:n], s[:, :, 1], s[:, :, 4], ALU.add).then_inc(v_step, cv.one())
            nc.vector.tensor_tensor(lnt[:, 1, 0:n], s[:, :, 1], s[:, :, 4], ALU.subtract).then_inc(v_step, cv.one())
            nc.vector.tensor_tensor(lnt[:, 2, 0:n], s[:, :, 2], s[:, :, 5], ALU.add).then_inc(v_step, cv.one())
            v.wait_ge(v_step, cv.now)
            nc.vector.tensor_scalar(mean[:, lo:hi], lnt[:, 0, 0:n], 0.5, None, ALU.mult).then_inc(v_step, cv.one())
            nc.vector.tensor_scalar(lnt[:, 2, 0:n], lnt[:, 2, 0:n], 1.0 / H, EPS, ALU.mult, ALU.add).then_inc(v_step, cv.one())
            nc.vector.scalar_tensor_tensor(lnt[:, 1, 0:n], lnt[:, 1, 0:n], 0.25, lnt[:, 1, 0:n],
                                           ALU.mult, ALU.mult).then_inc(v_step, cv.one())
            v.wait_ge(v_step, cv.now)
            if twice:
                nc.vector.tensor_tensor(var[:, lo:hi], lnt[:, 1, 0:n], lnt[:, 2, 0:n], ALU.add).then_inc(v_step, cv.one())
                v.wait_ge(v_step, cv.now)
                nc.vector.tensor_scalar(var2[:, lo:hi], var[:, lo:hi], 1.0 + EPS, -EPS,
                                        ALU.mult, ALU.add).then_inc(sg("var_ready"), 1)
            else:
                nc.vector.tensor_tensor(var[:, lo:hi], lnt[:, 1, 0:n], lnt[:, 2, 0:n],
                                        ALU.add).then_inc(sg("var_ready"), 1)

        n_var = [0]

        def rsqrts(lo, hi, twice=False):
            n_var[0] += 1
            nc.gpsimd.wait_ge(sg("var_ready"), n_var[0])
            i = nc.gpsimd.tensor_tensor(rstd[:, lo:hi], var[:, lo:hi], pow_c[:, lo:hi], ALU.pow)
            if twice:
                i = nc.gpsimd.tensor_tensor(rstd2[:, lo:hi], var2[:, lo:hi], pow_c[:, lo:hi], ALU.pow)
            i.then_inc(sg("rstd_ready"), 1)

        if True:
            xn = carve("xn", [P, 2, TPB, H])
            xT = carve("xT", [P, 2, SEQ])
            pre = carve("pre", [P, 3, 4 + SEQ])
            kvq = carve("kvq", [P, 3, GROUPS, SEQ])
            w_st = carve("w_st", [P, GROUPS, SEQ])
            b_st = carve("b_st", [P, GROUPS, SEQ])
            e_st = carve("e_st", [P, GROUPS, SEQ])
            gw_n = carve("gw_n", [P, H])
            gb_n = carve("gb_n", [P, H])
            gate_t = big[0][:, :].rearrange("p (t c) -> p t c", t=TILES)
            sga = big[1][:, 0:1024].rearrange("p (g n) -> p g n", g=GROUPS)
            sge = big[1][:, 1024:2048].rearrange("p (g n) -> p g n", g=GROUPS)
            tabs = big[1][:, 2048:3072].rearrange("p (g n) -> p g n", g=GROUPS)
            tlin = big[1][:, 3072:4096].rearrange("p (g n) -> p g n", g=GROUPS)
            eta_c, keep_c = big[2][:, 0:2048], big[2][:, 2048:4096]
            xco, yco = big[3][:, 0:2048], big[3][:, 2048:4096]
            init = e_st

        first = {}
        TB, GB = 0, 1

        def prep_sync(sync):
            sync.dma_start(pk[:, :], packed_d).then_inc(sg("packed_in"), 16)
            for g in range(GROUPS):
                sync.dma_start(xres[:, g * 16:g * 16 + 16, :],
                               x_d.rearrange("(t p) c -> p t c", p=P)[:, g * 16:g * 16 + 16, :]
                               ).then_inc(sg(f"x_in{g}"), 16)

        def prep_gpsimd(pool):
            nc.gpsimd.memset(zeros[:, :], 0.0).then_inc(sg("zeros_ready"), 1)
            nc.gpsimd.memset(pow_c[:, :], -0.5).then_inc(p_step, cp.one())
            pool.wait_ge(p_step, cp.now)
            rsqrts(0, 16)
            rsqrts(16, 32)

        def prep_vector(v):
            v.sem_inc(sg("gt_free"), 1)
            v.sem_inc(sg("pre_free"), 1)
            nc.vector.memset(pre[:, :, :], 0.0).then_inc(sg("pre_zero"), 1)
            v.wait_ge(sg("packed_in"), 16)
            nc.vector.tensor_tensor(gw_n[:, :], par("gate"), par("norm_g"), ALU.mult).then_inc(sg("gw_ready"), 1)
            nc.vector.tensor_tensor(gb_n[:, :], par("gate_b"), par("norm_g"), ALU.mult).then_inc(v_step, cv.one())
            for g in range(GROUPS):
                v.wait_ge(sg(f"x_in{g}"), 16)
                with cv.loop(v, 16, 1) as t:
                    nc.vector.bn_stats(st[:, g * 16 + t, :], xres[:, g * 16 + t, :]).then_inc(v_step, cv.one())
                v.wait_ge(v_step, cv.now)
                moments(v, g * 16, g * 16 + 16)

            v.wait_ge(sg("rstd_ready"), 2)
            with cv.loop(v, GROUPS, 9) as g:
                def gate_add(b4):
                    v.wait_ge(sg("gt_done"), g * B4 + b4 + 1)
                    nc.vector.tensor_tensor(
                        gate_t[:, bass.ds(g * 16 + b4 * TPB, TPB), :],
                        bank[:, GB, :].rearrange("p (j c) -> p j c", j=TPB),
                        gb_n[:, None, :].broadcast_to([P, TPB, H]), ALU.add).then_inc(sg("gt_free"), 1)

                for b4 in range(B4):
                    v.wait_ge(sg("xn_free"), g * B4 + b4 + 1)
                    for j in range(TPB):
                        t = g * 16 + b4 * TPB + j
                        i = nc.vector.tensor_scalar(xn[:, b4 % 2, j, :], xres[:, t, :], mean[:, bass.ds(t, 1)],
                                                    rstd[:, bass.ds(t, 1)], ALU.subtract, ALU.mult)
                    i.then_inc(sg("xn_ready"), 1)
                    if b4 >= 1:
                        gate_add(b4 - 1)
                gate_add(B4 - 1)
                v.wait_ge(sg("pre_ready"), g + 1)
                for tap in range(4):
                    for kind in range(3):
                        src = pre[:, kind, tap:tap + SEQ]
                        dst = kvq[:, kind, g, :]
                        w = par("conv_w", kind * 4 + tap, kind * 4 + tap + 1)
                        if tap == 0:
                            i = nc.vector.tensor_scalar(dst, src, w, par("conv_b", kind, kind + 1), ALU.mult, ALU.add)
                        else:
                            i = nc.vector.scalar_tensor_tensor(dst, src, w, dst, ALU.mult, ALU.add)
                        if tap < 3:
                            i.then_inc(v_step, cv.one())
                    if tap < 3:
                        v.wait_ge(v_step, cv.now)
                i.then_inc(sg("pre_free"), 1)

            v.wait_ge(sg("theta_parts"), 1)
            theta = tlin
            nc.vector.scalar_tensor_tensor(theta[:, :, :], tlin[:, :, :], 0.0, tabs[:, :, :],
                                           ALU.max, ALU.add).then_inc(sg("theta_ready"), 1)
            starts = lambda a: a.rearrange("p (c t) -> p c t", t=CHUNK)[:, :, 0:1]
            flat = lambda a: a[:, :, :].rearrange("p g n -> p (g n)")
            tmp = lambda k: big[2][:, k * 1024:(k + 1) * 1024]
            v.wait_ge(sg("means"), 1)
            nc.vector.tensor_scalar(tmp(0).rearrange("p (g n) -> p g n", g=2), bank[:, 0:2, :], 0.9, 0.05, ALU.mult, ALU.add).then_inc(sg("bd_read"), 1)
            nc.vector.tensor_scalar(tmp(1).rearrange("p (g n) -> p g n", g=2), bank[:, 2:4, :], -0.1, 1.0, ALU.mult, ALU.add).then_inc(sg("bd_read"), 1)
            v.wait_ge(sg("bd_read"), 2)
            nc.vector.memset(tmp(2), 0.0).then_inc(v_step, cv.one())
            nc.vector.memset(tmp(3), 0.0).then_inc(v_step, cv.one())
            v.wait_ge(v_step, cv.now)
            nc.vector.tensor_copy(starts(tmp(2)), starts(tmp(0))).then_inc(v_step, cv.one())
            nc.vector.tensor_copy(starts(tmp(3)), starts(tmp(1))).then_inc(v_step, cv.one())
            v.wait_ge(v_step, cv.now)
            nc.vector.memset(starts(tmp(0)), 0.0).then_inc(v_step, cv.one())
            nc.vector.memset(starts(tmp(1)), 0.0).then_inc(v_step, cv.one())
            v.wait_ge(v_step, cv.now)
            nc.vector.tensor_tensor_scan(flat(e_st), tmp(0), tmp(2), 0.0, ALU.mult, ALU.add).then_inc(v_step, cv.one())
            nc.vector.tensor_tensor_scan(flat(w_st), tmp(1), tmp(3), 0.0, ALU.mult, ALU.add).then_inc(v_step, cv.one())
            v.wait_ge(v_step, cv.now)
            nc.vector.tensor_tensor_scan(flat(b_st), tmp(1), flat(e_st), 0.0, ALU.mult, ALU.add).then_inc(v_step, cv.one())
            v.wait_ge(v_step, cv.now)
            v.wait_ge(sg("means"), 2)
            nc.vector.tensor_scalar(eta_c.rearrange("p (b n) -> p b n", b=4), bank[:, 4:8, :], 0.9, 0.05, ALU.mult, ALU.add).then_inc(v_step, cv.one())
            v.wait_ge(sg("means"), 3)
            nc.vector.tensor_scalar(keep_c.rearrange("p (b n) -> p b n", b=4), bank[:, 0:4, :], -0.1, 1.0, ALU.mult, ALU.add).then_inc(v_step, cv.one())
            v.wait_ge(v_step, cv.now)
            v.sem_inc(sg("bank_free"), 1)
            nc.vector.memset(starts(eta_c), 0.0).then_inc(v_step, cv.one())
            nc.vector.memset(starts(keep_c), 0.0).then_inc(v_step, cv.one())
            v.wait_ge(sg("means"), 4)
            nc.vector.scalar_tensor_tensor(
                yco.rearrange("p (c t) -> p c t", t=CHUNK),
                bank[:, 4:8, :].rearrange("p b n -> p (b n)").rearrange("p (c t) -> p c t", t=CHUNK), 0.1,
                par("neg_i")[:, None, :].broadcast_to([P, 4 * CHUNKS, CHUNK]),
                ALU.mult, ALU.mult).then_inc(v_step, cv.one())
            v.wait_ge(v_step, cv.now)
            nc.vector.tensor_tensor_scan(xco, eta_c, yco, 0.0, ALU.mult, ALU.add).then_inc(v_step, cv.one())
            v.wait_ge(v_step, cv.now)
            nc.vector.tensor_tensor_scan(yco, keep_c, xco, 0.0, ALU.mult, ALU.add).then_inc(sg("coef_ready"), 1)

        def prep_tensor(pe):
            pe.sem_inc(sg("xn_free"), 2)
            pe.sem_inc(sg("xT_free"), 2)
            pe.wait_ge(sg("packed_in"), 16)
            pe.wait_ge(sg("gw_ready"), 1)
            with pe.Fori(0, GROUPS) as g:
                for b4 in range(B4):
                    u = g * B4 + b4
                    pe.wait_ge(sg("xn_ready"), u + 1)
                    for j in range(TPB):
                        i = nc.tensor.transpose(bank[:, TB, j * P:(j + 1) * P], xn[:, b4 % 2, j, :], ident)
                    i.then_inc(sg("xn_free"), 1)
                    pe.wait_ge(sg("xT_ready"), u + 1)
                    pe.wait_ge(sg("gt_free"), u + 1)
                    for j in range(TPB):
                        i = nc.tensor.matmul(bank[:, GB, j * H:(j + 1) * H], xT[:, b4 % 2, j * P:(j + 1) * P],
                                             gw_n[:, :], start=True, stop=True)
                    i.then_inc(sg("gt_done"), 1)
                    if b4 == 0:
                        pe.wait_ge(sg("kinds_free"), g + 1)
                    for kind in range(6):
                        i = nc.tensor.matmul(bank[D * b4:D * b4 + D, 2 + kind, :], par("proj", kind * D, kind * D + D),
                                             xT[:, b4 % 2, :], start=True, stop=True)
                    i.then_inc(sg("xT_free"), 1)
            pe.wait_ge(sg("kinds_free"), 1 + GROUPS)
            pe.wait_ge(sg("gt_free"), 1 + BATCH)
            for k, s in enumerate((sge, sga)):
                for g in range(GROUPS):
                    i = nc.tensor.matmul(bank[:, 2 * k + g, :], par("mean_bd"), s[:, g, :], start=True, stop=True)
            i.then_inc(sg("means"), 1)

            def spread(s, at):
                for b4 in range(B4):
                    for g in range(GROUPS):
                        i = nc.tensor.matmul(bank[64 * g:64 * g + 64, at + b4, :], par("mean_sel", b4 * 64, b4 * 64 + 64),
                                             s[:, g, :], start=True, stop=True)
                i.then_inc(sg("means"), 1)

            spread(sge, 4)
            pe.wait_ge(sg("bd_read"), 2)
            spread(sga, 0)
            pe.wait_ge(sg("theta_ready"), 1)
            pe.wait_ge(sg("bank_free"), 1)
            spread(tlin, 4)

        def prep_scalar(act):
            act.sem_inc(sg("kinds_free"), 1)
            act.dma_start(experts_up[:, :, :], up0_d).then_inc(sg("experts_in"), 16)
            act.dma_start(experts_down[:, :, :, :], down0_d).then_inc(sg("experts_in"), 16)
            act.wait_ge(sg("zeros_ready"), 1)
            for n in range(2):
                act.dma_start(rows_d[n].rearrange("(s p) c -> p s c", p=P),
                              zeros[:, None, :].broadcast_to([P, SLOTS, H])).then_inc(sg("zeroed"), 16)
            act.wait_ge(sg("packed_in"), 16)
            act.wait_ge(sg("pre_zero"), 1)
            with act.Fori(0, GROUPS) as g:
                for b4 in range(B4):
                    u = g * B4 + b4
                    act.wait_ge(sg("xn_free"), u + 3)
                    act.wait_ge(sg("xT_free"), u + 1)
                    nc.scalar.activation(xT[:, b4 % 2, :], bank[:, TB, :], ACT.Identity).then_inc(sg("xT_ready"), 1)
                act.wait_ge(sg("xT_free"), g * B4 + B4 + 2)
                act.wait_ge(sg("pre_free"), g + 1)
                for kind in range(3):
                    i = nc.scalar.activation(pre[:, kind, 3:3 + SEQ], bank[:, 2 + kind, :], ACT.Identity)
                i.then_inc(sg("pre_ready"), 1)
                nc.scalar.activation(sga[:, g, :], bank[:, 5, :], ACT.Sigmoid, bias=par("bias3", 0, 1))
                nc.scalar.activation(sge[:, g, :], bank[:, 6, :], ACT.Sigmoid, bias=par("bias3", 1, 2))
                nc.scalar.activation(tabs[:, g, :], bank[:, 7, :], ACT.Abs, bias=par("bias3", 2, 3))
                nc.scalar.activation(tlin[:, g, :], bank[:, 7, :], ACT.Identity,
                                     bias=par("bias3", 2, 3)).then_inc(sg("kinds_free"), 1)
            act.wait_ge(sg("kinds_free"), 1 + GROUPS)
            nc.scalar.activation(tabs[:, :, :], tabs[:, :, :], ACT.Exp, scale=-1.0).then_inc(a_step, ca.one())
            act.wait_ge(a_step, ca.now)
            nc.scalar.activation(tabs[:, :, :], tabs[:, :, :], ACT.Ln, bias=1.0).then_inc(sg("theta_parts"), 1)

        ks = carve("ks", [P, 2, GROUPS, CHUNK])
        vs = carve("vs", [P, 2, GROUPS, CHUNK])
        qx = carve("qx", [P, 2, GROUPS, B4, CHUNK])
        qa = carve("qa", [P, 2, GROUPS, CHUNK])
        qb = carve("qb", [P, 2, GROUPS, CHUNK])
        kh = carve("kh", [P, 2, P])
        vt = carve("vt", [P, P])
        de = carve("de", [P, 2, P])
        dec = carve("dec", [P, 2, 2, P])
        dexy = carve("dexy", [P, 2, 2, P])
        sq = carve("sq", [P, 2, P])
        skh = carve("skh", [P, 2, B4])
        sde = carve("sde", [P, 2, B4])
        cl = carve("cl", [P, 3, B4])
        sig = carve("sig", [P, P])
        dsilu = carve("dsilu", [P, P])
        hT = carve("hT", [P, 2, GROUPS, CHUNK])
        eT = carve("eT", [P, GROUPS, CHUNK])
        p1 = carve("p1", [P, B4, CHUNK])
        p2 = carve("p2", [P, B4, CHUNK])
        sig2 = carve("sig2", [P, GROUPS, CHUNK])
        h2 = carve("h2", [P, GROUPS, CHUNK])
        h2x = carve("h2x", [P, GROUPS, B4, CHUNK])
        h2a = carve("h2a", [P, GROUPS, CHUNK])
        h2b = carve("h2b", [P, GROUPS, CHUNK])
        wc = carve("wc", [P, GROUPS, 2, D])
        sc = carve("sc", [P, GROUPS, 2, D])
        sd = carve("sd", [P, GROUPS, 2, D])
        wx = carve("wx", [P, 2, GROUPS * 2, B4, D])
        sx = carve("sx", [P, 2, GROUPS * 2, B4, D])
        w2x = carve("w2x", [P, 2, GROUPS, P])
        ret = carve("ret", [P, GROUPS, SEQ])
        A_B, KV_B, SC_B, TR_B, PD_B, G_B, W2_B = 0, 1, 2, 3, 4, 5, 7
        y5 = yco.rearrange("p (b c t) -> p b c t", b=B4, c=CHUNKS)
        x5 = xco.rearrange("p (b c t) -> p b c t", b=B4, c=CHUNKS)
        quad_t = quad4[:, :, 0:1]

        def grp(a, g):
            return a[64 * g:64 * g + 64]

        def at(i):
            return bass.ds(i * CHUNK, CHUNK)

        def expand(dst, src):
            return nc.vector.tensor_tensor(
                dst, src[:, :, :, :].rearrange("p g k d -> p (g k) d")[:, :, None, :].broadcast_to([P, 4, B4, D]),
                quad4[:, None, :, :].broadcast_to([P, 4, B4, D]), ALU.mult)

        def chunks_on(eng, step):
            step(0, 0, True, False)
            with eng.Fori(0, (CHUNKS - 2) // 2) as r:
                step(2 * r + 1, 1, True, True)
                step(2 * r + 2, 0, True, True)
            step(CHUNKS - 1, 1, True, True)
            step(CHUNKS, 0, False, True)

        def recur_gpsimd(pool):
            pool.wait_ge(sg("coef_ready"), 1)

            def stage(i, p):
                nc.gpsimd.tensor_copy(ks[:, p], kvq[:, 0, :, at(i)])
                nc.gpsimd.tensor_copy(vs[:, p], kvq[:, 1, :, at(i)])
                for g in range(GROUPS):
                    nc.gpsimd.tensor_tensor(qx[:, p, g], kvq[:, 2, g, at(i)][:, None, :].broadcast_to([P, B4, CHUNK]),
                                            quad_t.broadcast_to([P, B4, CHUNK]), ALU.mult)
                nc.gpsimd.tensor_tensor(qa[:, p], kvq[:, 2, :, at(i)], w_st[:, :, at(i)], ALU.mult)
                nc.gpsimd.tensor_tensor(qb[:, p], kvq[:, 2, :, at(i)], b_st[:, :, at(i)],
                                        ALU.mult).then_inc(sg("staged"), 1)

            def step(i, p, chain, back):
                if back:
                    pool.wait_ge(sg("h2_ready"), i)
                    nc.gpsimd.tensor_tensor(h2a[:, :, :], h2[:, :, :], w_st[:, :, at(i - 1)], ALU.mult)
                    nc.gpsimd.tensor_tensor(h2b[:, :, :], h2[:, :, :], b_st[:, :, at(i - 1)],
                                            ALU.mult).then_inc(sg("h2ab"), 1)
                if chain:
                    pool.wait_ge(sg("norm_ready"), i + 1)
                    nc.gpsimd.tensor_tensor(cl[:, 2, :], cl[:, 1, :], pow_c[:, 0:B4], ALU.pow).then_inc(sg("clip_ready"), 1)
                    pool.wait_ge(sg("dec_ready"), i + 1)
                    nc.gpsimd.tensor_tensor(
                        dexy[:, :, 0, :].rearrange("p k (b d) -> p k b d", b=B4),
                        dec[:, p].rearrange("p k (b d) -> p k b d", b=B4),
                        x5[:, :, i, CHUNK - 1:CHUNK][:, None, :, :].broadcast_to([P, 2, B4, D]),
                        ALU.mult).then_inc(sg("dx_ready"), 1)

            stage(0, 0)

            def both(i, p, chain, back):
                if chain and not (isinstance(i, int) and i == CHUNKS - 1):
                    if back:
                        pool.wait_ge(sg("r1_done"), i)
                    stage(i + 1, 1 - p)
                step(i, p, chain, back)

            chunks_on(pool, both)

        def recur_scalar(act):
            act.wait_ge(sg("coef_ready"), 1)

            def step(i, p, chain, back):
                if chain:
                    act.wait_ge(sg("a_done"), i + 1)
                    nc.scalar.activation(sig[:, :], bank[:, A_B, 0:P], ACT.Sigmoid).then_inc(sg("sig_ready"), 1)
                    act.wait_ge(sg("kv_done"), i + 1)
                    nc.scalar.activation(kh[:, 0, :], bank[:, KV_B, 0:P], ACT.Identity)
                    nc.scalar.activation(vt[:, :], bank[:, KV_B, P:2 * P], ACT.Identity).then_inc(sg("kv_ready"), 1)
                    act.wait_ge(sg("hT_done"), i + 1)
                    nc.scalar.activation(hT[:, p], bank[:, TR_B, 0:P].rearrange("p (g t) -> p g t", g=2),
                                         ACT.Identity).then_inc(sg("hT_ready"), 1)
                if chain and back:
                    act.wait_ge(sg("w2_done"), i + 1)
                    nc.scalar.activation(w2x[:, p], bank[:, W2_B, 0:2 * P].rearrange("p (g n) -> p g n", g=2),
                                         ACT.Identity).then_inc(sg("w2_ready"), 1)
                if back:
                    act.wait_ge(sg("r1_done"), i)
                    nc.scalar.activation(sig2[:, :, :], bank[:, G_B:G_B + 2, 0:CHUNK], ACT.Sigmoid).then_inc(sg("sig2_ready"), 1)
                if chain:
                    act.wait_ge(sg("eT_done"), i + 1)
                    nc.scalar.activation(eT[:, :, :], bank[:, TR_B, P:2 * P].rearrange("p (g t) -> p g t", g=2),
                                         ACT.Identity).then_inc(sg("eT_ready"), 1)
                if back:
                    act.wait_ge(sg("r3_done"), i)
                    nc.scalar.activation(ret[:, :, at(i - 1)], bank[:, G_B:G_B + 2, CHUNK:2 * CHUNK],
                                         ACT.Identity).then_inc(sg("ret_ready"), 1)
            act.wait_ge(sg("w2_done"), 1)
            nc.scalar.activation(w2x[:, 0], bank[:, W2_B, 0:2 * P].rearrange("p (g n) -> p g n", g=2),
                                 ACT.Identity).then_inc(sg("w2_ready"), 1)
            chunks_on(act, step)

        def recur_vector(v):
            for g in range(GROUPS):
                nc.vector.tensor_copy(wc[:, g], par("mem").rearrange("p (k d) -> p k d", k=2)).then_inc(v_step, cv.one())
            nc.vector.memset(sc[:, :, :, :], 0.0).then_inc(v_step, cv.one())
            v.wait_ge(v_step, cv.now)
            v.wait_ge(sg("coef_ready"), 1)
            expand(sx[:, 0], sc)
            expand(wx[:, 0], wc).then_inc(sg("wx_ready"), 1)

            def chain_a(i, p):
                v.wait_ge(sg("sig_ready"), i + 1)
                a = bank[:, A_B, 0:P]
                v.wait_ge(sg("hT_done"), i) if not (isinstance(i, int) and i == 0) else None
                nc.vector.tensor_tensor(kh[:, 1, :], a, sig[:, :], ALU.mult).then_inc(sg("h_ready"), 1)
                v.wait_ge(sg("h_ready"), i + 1)
                nc.vector.scalar_tensor_tensor(dsilu[:, :], a, 1.0, kh[:, 1, :], ALU.add, ALU.subtract).then_inc(v_step, cv.one())
                v.wait_ge(v_step, cv.now)
                nc.vector.tensor_tensor(dsilu[:, :], dsilu[:, :], sig[:, :], ALU.mult).then_inc(v_step, cv.one())
                v.wait_ge(sg("kv_ready"), i + 1)
                nc.vector.tensor_tensor(sq[:, :, :], kh[:, :, :], kh[:, :, :], ALU.mult).then_inc(v_step, cv.one())
                v.wait_ge(v_step, cv.now)
                nc.vector.tensor_reduce(skh[:, :, :], sq[:, :, :].rearrange("p k (b d) -> p k b d", b=B4), AX,
                                        ALU.add).then_inc(v_step, cv.one())
                v.wait_ge(sg("pred_done"), i + 1)
                nc.vector.tensor_tensor(de[:, 1, :], bank[:, PD_B, 0:P], vt[:, :], ALU.subtract).then_inc(sg("e_ready"), 1)

            def back_a(i):
                v.wait_ge(sg("sig2_ready"), i)
                nc.vector.tensor_tensor(h2[:, :, :], bank[:, G_B:G_B + 2, 0:CHUNK], sig2[:, :, :],
                                        ALU.mult).then_inc(sg("h2_ready"), 1)
                v.wait_ge(sg("h2_ready"), i)
                nc.vector.tensor_tensor(h2x[:, :, :, :], h2[:, :, None, :].broadcast_to([P, GROUPS, B4, CHUNK]),
                                        quad_t[:, None, :, :].broadcast_to([P, GROUPS, B4, CHUNK]),
                                        ALU.mult).then_inc(sg("h2x_ready"), 1)

            def chain_b(i, p):
                v.wait_ge(sg("dh_done"), i + 1)
                nc.vector.tensor_tensor(de[:, 0, :], bank[:, PD_B, P:2 * P], dsilu[:, :], ALU.mult).then_inc(v_step, cv.one())
                v.wait_ge(v_step, cv.now)
                v.wait_ge(sg("e_ready"), i + 1)
                nc.vector.tensor_tensor(sq[:, :, :], de[:, :, :], de[:, :, :], ALU.mult).then_inc(v_step, cv.one())
                v.wait_ge(v_step, cv.now)
                nc.vector.tensor_reduce(sde[:, :, :], sq[:, :, :].rearrange("p k (b d) -> p k b d", b=B4), AX,
                                        ALU.add).then_inc(v_step, cv.one())
                v.wait_ge(v_step, cv.now)
                nc.vector.tensor_tensor(sde[:, :, :], sde[:, :, :], skh[:, :, :], ALU.mult).then_inc(v_step, cv.one())
                v.wait_ge(v_step, cv.now)
                nc.vector.tensor_tensor(cl[:, 0, :], sde[:, 0, :], sde[:, 1, :], ALU.add).then_inc(v_step, cv.one())
                v.wait_ge(v_step, cv.now)
                nc.vector.tensor_scalar(cl[:, 1, :], cl[:, 0, :], 25.0, None, ALU.max).then_inc(sg("norm_ready"), 1)

            def back_b(i):
                v.wait_ge(sg("s2_done"), i)
                nc.vector.tensor_tensor(p2[:, :, :], bank[:, SC_B, 0:256].rearrange("p (b t) -> p b t", b=B4),
                                        y5[:, :, i - 1, :], ALU.mult).then_inc(sg("p2_ready"), 1)

            def chain_c(i, p):
                v.wait_ge(sg("s1_done"), i + 1)
                nc.vector.tensor_tensor(p1[:, :, :], bank[:, SC_B, 0:256].rearrange("p (b t) -> p b t", b=B4),
                                        y5[:, :, i, :], ALU.mult).then_inc(sg("p1_ready"), 1)
                v.wait_ge(sg("clip_ready"), i + 1)
                nc.vector.tensor_tensor(
                    dec[:, p].rearrange("p k (b d) -> p k b d", b=B4),
                    de[:, :, :].rearrange("p k (b d) -> p k b d", b=B4),
                    cl[:, 2, :][:, None, :, None].broadcast_to([P, 2, B4, D]), ALU.mult).then_inc(sg("dec_ready"), 1)
                v.wait_ge(sg("dec_ready"), i + 1)
                nc.vector.tensor_tensor(
                    dexy[:, :, 1, :].rearrange("p k (b d) -> p k b d", b=B4),
                    dec[:, p].rearrange("p k (b d) -> p k b d", b=B4),
                    y5[:, :, i, CHUNK - 1:CHUNK][:, None, :, :].broadcast_to([P, 2, B4, D]),
                    ALU.mult).then_inc(sg("dy_ready"), 1)
                v.wait_ge(sg("g_done"), i + 1)
                last = lambda a, g: a[:, g, bass.ds(i * CHUNK + CHUNK - 1, 1)]
                fresh = lambda g, w: bank[:, G_B + g, 0:128].rearrange("p (k w d) -> p k w d", k=2, w=2)[:, :, w, :]
                for g in range(GROUPS):
                    nc.vector.scalar_tensor_tensor(sd[:, g], sc[:, g], last(b_st, g), fresh(g, 1),
                                                   ALU.mult, ALU.add).then_inc(v_step, cv.one())
                v.wait_ge(v_step, cv.now)
                for g in range(GROUPS):
                    nc.vector.scalar_tensor_tensor(wc[:, g], wc[:, g], last(w_st, g), sd[:, g],
                                                   ALU.mult, ALU.add).then_inc(v_step, cv.one())
                v.wait_ge(v_step, cv.now)
                expand(wx[:, 1 - p], wc).then_inc(sg("wx_ready"), 1)
                for g in range(GROUPS):
                    nc.vector.scalar_tensor_tensor(sc[:, g], sc[:, g], last(e_st, g), fresh(g, 0),
                                                   ALU.mult, ALU.add).then_inc(v_step, cv.one())
                v.wait_ge(v_step, cv.now)
                expand(sx[:, 1 - p], sc).then_inc(sg("sx_ready"), 1)

            def step(i, p, chain, back):
                if chain:
                    chain_a(i, p)
                if back:
                    back_a(i)
                if chain:
                    chain_b(i, p)
                if back:
                    back_b(i)
                if chain:
                    chain_c(i, p)

            step(0, 0, True, False)
            with cv.loop(v, (CHUNKS - 2) // 2, 2 * STEPS_V) as r:
                step(2 * r + 1, 1, True, True)
                step(2 * r + 2, 0, True, True)
            step(CHUNKS - 1, 1, True, True)
            step(CHUNKS, 0, False, True)

        def recur_tensor(pe):
            def flip_w2(p):
                for g in range(GROUPS):
                    i = nc.tensor.transpose(bank[:, W2_B, g * P:(g + 1) * P],
                                            wx[:, p, 2 * g + 1].rearrange("p b d -> p (b d)"), ident)
                i.then_inc(sg("w2_done"), 1)

            def w(p, g, k):
                return wx[:, p, 2 * g + k].rearrange("p b d -> p (b d)")

            def s(p, g, k):
                return sx[:, p, 2 * g + k].rearrange("p b d -> p (b d)")

            def back_sum(p, k, src, pair, a, b, col):
                for g in range(GROUPS):
                    o = bank[:, G_B + g, col:col + CHUNK]
                    nc.tensor.matmul(o, w(p, g, k), a[:, g, :], start=True, stop=False)
                    nc.tensor.matmul(o, s(p, g, k), b[:, g, :], start=False, stop=True)
                    for b4 in range(B4):
                        i = nc.tensor.matmul(bank[D * b4:D * b4 + D, G_B + g, col:col + CHUNK],
                                             grp(dec[:, p, pair, D * b4:D * b4 + D], g), grp(src[:, b4, :], g),
                                             start=False, stop=True, skip_group_check=True)
                return i

            pe.wait_ge(sg("wx_ready"), 1)
            flip_w2(0)

            def step(i, p, chain, back):
                if chain:
                    pe.wait_ge(sg("staged"), i + 1)
                    pe.wait_ge(sg("wx_ready"), i + 1)
                    for g in range(GROUPS):
                        j = nc.tensor.matmul(bank[64 * g:64 * g + 64, A_B, 0:P], ks[:, p, g, :], w(p, g, 0),
                                             start=True, stop=True)
                    j.then_inc(sg("a_done"), 1)
                    for k, src in enumerate((ks, vs)):
                        j = nc.tensor.transpose(bank[:, KV_B, k * P:(k + 1) * P],
                                                src[:, p].rearrange("p g t -> p (g t)"), ident)
                    j.then_inc(sg("kv_done"), 1)
                    if back:
                        flip_w2(p)
                if back:
                    pe.wait_ge(sg("p1_ready"), i)
                    pe.wait_ge(sg("sx_ready"), i)
                    back_sum(1 - p, 0, p1, 0, qa[:, 1 - p], qb[:, 1 - p], 0).then_inc(sg("r1_done"), 1)
                if chain:
                    pe.wait_ge(sg("h_ready"), i + 1)
                    nc.tensor.transpose(bank[:, TR_B, 0:P], kh[:, 1, :], ident).then_inc(sg("hT_done"), 1)
                    pe.wait_ge(sg("hT_ready"), i + 1)
                    for g in range(GROUPS):
                        j = nc.tensor.matmul(bank[64 * g:64 * g + 64, PD_B, 0:P], hT[:, p, g, :], w(p, g, 1),
                                             start=True, stop=True)
                    j.then_inc(sg("pred_done"), 1)
                    pe.wait_ge(sg("e_ready"), i + 1)
                    nc.tensor.transpose(bank[:, TR_B, P:2 * P], de[:, 1, :], ident).then_inc(sg("eT_done"), 1)
                if back:
                    pe.wait_ge(sg("h2x_ready"), i)
                    for g in range(GROUPS):
                        j = nc.tensor.matmul(bank[64 * g:64 * g + 64, SC_B, 0:256], hT[:, 1 - p, g, :],
                                             h2x[:, g].rearrange("p b t -> p (b t)"), start=True, stop=True)
                    j.then_inc(sg("s2_done"), 1)
                if chain:
                    pe.wait_ge(sg("eT_ready"), i + 1)
                    pe.wait_ge(sg("w2_ready"), i + 1)
                    for g in range(GROUPS):
                        j = nc.tensor.matmul(bank[64 * g:64 * g + 64, PD_B, P:2 * P], eT[:, g, :], w2x[:, p, g, :],
                                             start=True, stop=True)
                    j.then_inc(sg("dh_done"), 1)
                if back:
                    pe.wait_ge(sg("p2_ready"), i)
                    pe.wait_ge(sg("h2ab"), i)
                    back_sum(1 - p, 1, p2, 1, h2a, h2b, CHUNK).then_inc(sg("r3_done"), 1)
                if chain:
                    for g in range(GROUPS):
                        j = nc.tensor.matmul(bank[64 * g:64 * g + 64, SC_B, 0:256], ks[:, p, g, :],
                                             qx[:, p, g].rearrange("p b t -> p (b t)"), start=True, stop=True)
                    j.then_inc(sg("s1_done"), 1)
                    pe.wait_ge(sg("dx_ready"), i + 1)
                    pe.wait_ge(sg("dy_ready"), i + 1)
                    if back:
                        pe.wait_ge(sg("ret_ready"), i)
                    pe.sem_inc(sg("g_started"), 1)
                    for g in range(GROUPS):
                        for k in range(2):
                            for b4 in range(B4):
                                j = nc.tensor.matmul(
                                    bank[D * b4:D * b4 + D, G_B + g, 64 * k:64 * k + 64],
                                    grp(kh[:, k, D * b4:D * b4 + D], g), grp(dexy[:, k, :, D * b4:D * b4 + D], g),
                                    start=True, stop=True)
                    j.then_inc(sg("g_done"), 1)

            chunks_on(pe, step)

        def post_tensor(pe):
            pe.wait_ge(sg("ret_ready"), CHUNKS)
            for n in range(GROUPS * TPB):
                g, j = divmod(n, TPB)
                if n >= 2:
                    pe.wait_ge(sg("o_read"), n - 1)
                nc.tensor.matmul(bank[:, n % 2, :], ret[:, g, j * P:(j + 1) * P], par("wo"),
                                 start=True, stop=True).then_inc(sg("o_done"), 1)

        tiles = lambda a: a[:, :].rearrange("p (t c) -> p t c", t=TILES)
        o_all = tiles(big[2])
        carved[0] = 0
        o_sq = kvq[:, :, :, :].rearrange("p k g n -> p (k g) n")

        def post_scalar(act):
            o5 = o_all.rearrange("p (g b j) c -> p g b j c", g=GROUPS, b=B4)
            for n in range(GROUPS * TPB):
                g, j = divmod(n, TPB)
                act.wait_ge(sg("o_done"), n + 1)
                src = bank[:, n % 2, :].rearrange("p (b c) -> p b c", b=B4)
                nc.scalar.activation(o5[:, g, :, j, :], src, ACT.Identity)
                if n >= 2:
                    act.wait_ge(sg("sq_read"), n - 1)
                nc.scalar.activation(o_sq[:, n % 2, :], bank[:, n % 2, :], ACT.Square).then_inc(sg("o_read"), 1)

        def post_vector(v):
            s4 = st[:, :, 0].rearrange("p (g b j) -> p g b j", g=GROUPS, b=B4)
            for n in range(GROUPS * TPB):
                g, j = divmod(n, TPB)
                v.wait_ge(sg("o_read"), n + 1)
                nc.vector.tensor_reduce(s4[:, g, :, j], o_sq[:, n % 2, :].rearrange("p (b c) -> p b c", b=B4),
                                        AX, ALU.add).then_inc(sg("sq_read"), 1)
            v.wait_ge(sg("sq_read"), GROUPS * TPB)
            nc.vector.tensor_scalar(var[:, :], st[:, :, 0], 1.0 / H, 1e-6, ALU.mult, ALU.add).then_inc(sg("var_ready"), 1)
            v.wait_ge(sg("rstd_ready"), 3)
            with cv.loop(v, BATCH, 2) as b:
                for k in range(TPB):
                    t = b * TPB + k
                    i = nc.vector.scalar_tensor_tensor(o_all[:, t, :], o_all[:, t, :], rstd[:, bass.ds(t, 1)],
                                                       gate_t[:, t, :], ALU.mult, ALU.mult)
                i.then_inc(v_step, cv.one())
                v.wait_ge(v_step, cv.now)
                for k in range(TPB):
                    i = nc.vector.bn_stats(st[:, b * TPB + k, :], o_all[:, b * TPB + k, :])
                i.then_inc(v_step, cv.one())
            v.wait_ge(v_step, cv.now)
            moments(v, 0, TILES)
            residual(v, o_all, 4)
            v.wait_ge(v_step, cv.now)
            moments(v, 0, TILES)

        def post_gpsimd(pool):
            rsqrts(0, TILES)
            rsqrts(0, TILES)
            rsqrts(0, TILES)

        def residual(v, src, n_rstd):
            v.wait_ge(sg("rstd_ready"), n_rstd)
            with cv.loop(v, BATCH, 3) as b:
                for k in range(TPB):
                    t = b * TPB + k
                    i = nc.vector.tensor_scalar(src[:, t, :], src[:, t, :], mean[:, bass.ds(t, 1)],
                                                rstd[:, bass.ds(t, 1)], ALU.subtract, ALU.mult)
                i.then_inc(v_step, cv.one())
                v.wait_ge(v_step, cv.now)
                four = bass.ds(b * TPB, TPB)
                nc.vector.tensor_tensor(xres[:, four, :], xres[:, four, :], src[:, four, :], ALU.add).then_inc(v_step, cv.one())
                v.wait_ge(v_step, cv.now)
                for k in range(TPB):
                    i = nc.vector.bn_stats(st[:, b * TPB + k, :], xres[:, b * TPB + k, :])
                i.then_inc(v_step, cv.one())

        zeros = sb("zeros", [P, H])
        rows_d = [nc.dram_tensor(f"sorted{n}", (SLOTS * P, H), F32).ap() for n in range(2)]
        made_d = [nc.dram_tensor(f"made{n}", (SLOTS * P, H), F32).ap() for n in range(2)]
        xa = carve("xa", [P, 2, TPB, H])
        xb = carve("xb", [P, 2, SEQ])
        lg = carve("lg", [P, TILES, EXPERTS])
        pr = carve("pr", [P, TILES, EXPERTS])
        key = carve("key", [P, TILES, EXPERTS])
        hot = [carve(f"hot{k}", [P, TILES, EXPERTS]) for k in range(3)]
        t8 = carve("t8", [P, TILES, EXPERTS])
        t8b = carve("t8b", [P, TILES, EXPERTS])
        m32 = carve("m32", [P, 2, TILES])
        gain = carve("gain", [P, 2, TILES])
        csum = carve("csum", [P, EXPERTS, TILES])
        e8 = carve("e8", [P, 4, EXPERTS])
        slot8 = carve("slot8", [P, SLOTS, EXPERTS])
        slotf = carve("slotf", [P, SLOTS])
        rowf = carve("rowf", [P, 2, TILES])
        row_of = sb("row_of", [P, 2, TILES], I32)
        expert_of = sb("expert_of", [P, SLOTS], I32)
        sgs = carve("sgs", [P, 2, SEQ])
        hs = carve("hs", [P, 2, 2, SEQ])
        xr = carve("xr", [P, 2, 4, H])
        xT2 = carve("xT2", [P, 2, P])
        sgb = carve("sgb", [P, 2, MID])
        hb = carve("hb", [P, 2, MID])
        hTb = carve("hTb", [P, 2, MID])
        yb = carve("yb", [P, 2, 4, H])
        rows = tiles(big[0])
        xt_all = big[1][:, :]
        T0, L0B = 0, 2
        was = lambda n, per: n * per

        def route_vector(v, n, lead):
            def logits_out(b, p):
                v.wait_ge(sg("lg_done"), was(n, BATCH) + b + 3)
                nc.vector.tensor_copy(lg[:, bass.ds(b * TPB, TPB), :],
                                      bank[:, L0B + p, 0:TPB * EXPERTS].rearrange("p (j e) -> p j e", j=TPB)
                                      ).then_inc(sg("lg_out"), 1)

            with cv.loop(v, BATCH // 2, lead.steps * 2) as r:
                for p in range(2):
                    b = 2 * r + p
                    v.wait_ge(sg("xa_copied"), was(n, BATCH) + b + 1)
                    v.wait_ge(sg("xa_turned"), was(n, BATCH) + b + 1)
                    lead(b, p)
                for p in range(2):
                    logits_out(2 * r + p, p)
            v.wait_ge(sg("lg_out"), was(n, BATCH) + BATCH + 2)

        def route_gpsimd(pool, n):
            if n == 0:
                pool.sem_inc(sg("xa_copied"), 2)
                pool.sem_inc(sg("xb_copied"), 2)
            with pool.Fori(0, BATCH // 2) as r:
                for p in range(2):
                    b = 2 * r + p
                    pool.wait_ge(sg("xa_ready"), was(n, BATCH) + b + 1)
                    nc.gpsimd.tensor_copy(rows_of[n][:, bass.ds(b * TPB, TPB), :], xa[:, p]).then_inc(sg("xa_copied"), 1)
                    if n == 0:
                        pool.wait_ge(sg("xb_ready"), b + 1)
                        nc.gpsimd.tensor_copy(xt_all[:, bass.ds(b * SEQ, SEQ)], xb[:, p]).then_inc(sg("xb_copied"), 1)

        def route_scalar(act, n):
            with act.Fori(0, BATCH // 2) as r:
                for p in range(2):
                    b = 2 * r + p
                    act.wait_ge(sg("xa_turned"), was(n, BATCH) + b + 3)
                    act.wait_ge(sg("lg_done"), was(n, BATCH) + b + 1)
                    if n == 0:
                        act.wait_ge(sg("xb_copied"), b + 1)
                    nc.scalar.activation(xb[:, p], bank[:, T0 + p, :], ACT.Identity).then_inc(sg("xb_ready"), 1)

        def route_tensor(pe, n):
            if n == 0:
                pe.sem_inc(sg("xa_turned"), 2)
                pe.sem_inc(sg("lg_done"), 2)
                pe.wait_ge(sg("o_read"), GROUPS * TPB)
            with pe.Fori(0, BATCH // 2) as r:
                for p in range(2):
                    b = 2 * r + p
                    pe.wait_ge(sg("xa_ready"), was(n, BATCH) + b + 1)
                    for j in range(TPB):
                        i = nc.tensor.transpose(bank[:, T0 + p, j * P:(j + 1) * P], xa[:, p, j, :], ident)
                    i.then_inc(sg("xa_turned"), 1)
                    pe.wait_ge(sg("xb_ready"), was(n, BATCH) + b + 1)
                    pe.wait_ge(sg("lg_out"), was(n, BATCH) + b + 1)
                    for j in range(TPB):
                        i = nc.tensor.matmul(bank[:, L0B + p, j * EXPERTS:(j + 1) * EXPERTS], xb[:, p, j * P:(j + 1) * P],
                                             par(f"route{n}"), start=True, stop=True)
                    i.then_inc(sg("lg_done"), 1)
            pe.wait_ge(sg("hot_ready"), n + 1)
            for k, w in enumerate(("before", "ones")):
                i = nc.tensor.matmul(bank[:, 6 + k, 0:TILES * EXPERTS], par(w),
                                     hot[2][:, :, :].rearrange("p t e -> p (t e)"), start=True, stop=True)
            i.then_inc(sg("ranks"), 1)

        wide = lambda a: a[:, :, None].broadcast_to([P, TILES, EXPERTS])

        def vdo(v, i):
            i.then_inc(v_step, cv.one())
            v.wait_ge(v_step, cv.now)

        def choose(v, dst):
            vdo(v, nc.vector.tensor_reduce(m32[:, 0, :], key[:, :, :], AX, ALU.max))
            vdo(v, nc.vector.tensor_tensor(t8[:, :, :], key[:, :, :], wide(m32[:, 0, :]), ALU.is_equal))
            vdo(v, nc.vector.tensor_tensor(t8[:, :, :], t8[:, :, :],
                                           par("rank8")[:, None, :].broadcast_to([P, TILES, EXPERTS]), ALU.mult))
            vdo(v, nc.vector.tensor_reduce(m32[:, 0, :], t8[:, :, :], AX, ALU.max))
            vdo(v, nc.vector.tensor_tensor(dst[:, :, :], t8[:, :, :], wide(m32[:, 0, :]), ALU.is_equal))

        def place_vector(v, n):
            choose(v, hot[0])
            vdo(v, nc.vector.scalar_tensor_tensor(key[:, :, :], hot[0][:, :, :], -3.0e38, key[:, :, :],
                                                  ALU.mult, ALU.add))
            choose(v, hot[1])
            nc.vector.tensor_tensor(hot[2][:, :, :], hot[0][:, :, :], hot[1][:, :, :], ALU.add).then_inc(sg("hot_ready"), 1)
            for k in range(2):
                vdo(v, nc.vector.tensor_tensor(t8[:, :, :], hot[k][:, :, :], pr[:, :, :], ALU.mult))
                vdo(v, nc.vector.tensor_reduce(gain[:, k, :], t8[:, :, :], AX, ALU.add))
            v.wait_ge(sg("ranks"), n + 1)
            before = bank[:, 6, 0:TILES * EXPERTS].rearrange("p (t e) -> p t e", e=EXPERTS)
            total = bank[:, 7, 0:TILES * EXPERTS].rearrange("p (t e) -> p t e", e=EXPERTS)
            for e in range(EXPERTS):
                i = nc.vector.tensor_tensor_scan(csum[:, e, :], par("ones", 0, TILES), total[:, :, e], 0.0,
                                                 ALU.mult, ALU.add)
            vdo(v, i)
            c8 = t8[:, :, :].rearrange("p t e -> p (t e)").rearrange("p (e t) -> p e t", e=EXPERTS)
            vdo(v, nc.vector.tensor_tensor(c8, csum[:, :, TILES - 1:TILES].broadcast_to([P, EXPERTS, TILES]),
                                           par("edge")[:, None, :].broadcast_to([P, EXPERTS, TILES]), ALU.is_gt))
            vdo(v, nc.vector.tensor_reduce(e8[:, 0, :], c8, AX, ALU.add))
            vdo(v, nc.vector.tensor_tensor_scan(e8[:, 1, :], par("ones", 0, EXPERTS), e8[:, 0, :], 0.0,
                                                ALU.mult, ALU.add))
            vdo(v, nc.vector.tensor_tensor(e8[:, 2, :], e8[:, 1, :], e8[:, 0, :], ALU.subtract))
            vdo(v, nc.vector.tensor_scalar(e8[:, 3, :], e8[:, 2, :], float(P), None, ALU.mult))
            vdo(v, nc.vector.tensor_tensor(t8b[:, :, :], csum[:, :, :].rearrange("p e t -> p t e"), total, ALU.subtract))
            vdo(v, nc.vector.tensor_tensor(t8b[:, :, :], t8b[:, :, :], before, ALU.add))
            vdo(v, nc.vector.tensor_tensor(t8b[:, :, :], t8b[:, :, :],
                                           e8[:, 3, :][:, None, :].broadcast_to([P, TILES, EXPERTS]), ALU.add))
            for k in range(2):
                vdo(v, nc.vector.tensor_tensor(t8[:, :, :], hot[k][:, :, :], t8b[:, :, :], ALU.mult))
                vdo(v, nc.vector.tensor_reduce(rowf[:, k, :], t8[:, :, :], AX, ALU.add))
            nc.vector.tensor_copy(row_of[:, :, :], rowf[:, :, :]).then_inc(sg("rows_ready"), 1)
            vdo(v, nc.vector.tensor_tensor(slot8[:, :, :], par("slot")[:, :, None].broadcast_to([P, SLOTS, EXPERTS]),
                                           e8[:, 1, :][:, None, :].broadcast_to([P, SLOTS, EXPERTS]), ALU.is_ge))
            vdo(v, nc.vector.tensor_reduce(slotf[:, :], slot8[:, :, :], AX, ALU.add))
            vdo(v, nc.vector.tensor_scalar(slotf[:, :], slotf[:, :], float(EXPERTS - 1), None, ALU.min))
            nc.vector.tensor_copy(expert_of[:, :], slotf[:, :]).then_inc(sg("experts_ready"), 1)

        def scatter_gpsimd(pool, n, src):
            pool.wait_ge(sg("rows_ready"), n + 1)
            pool.wait_ge(sg("xa_copied"), 2 + BATCH * (n + 1))
            pool.wait_ge(sg("zeroed"), 32)
            for t in range(TILES):
                for k in range(2):
                    nc.gpsimd.indirect_dma_start(
                        rows_d[n][:, :], bass.IndirectOffsetOnAxis(ap=row_of[:, k, t:t + 1], axis=0),
                        src[k][:, t, :], None).then_inc(sg("sorted"), 16)

        def gather_gpsimd(pool, n, dst):
            for q in range(2):
                pool.wait_ge(sg(f"made{q}"), 16 * (SLOTS // 8) * (n + 1))
            for b in range(BATCH):
                for t in range(b * TPB, (b + 1) * TPB):
                    for k in range(2):
                        nc.gpsimd.indirect_dma_start(
                            dst[k][:, t, :], None, made_d[n][:, :],
                            bass.IndirectOffsetOnAxis(ap=row_of[:, k, t:t + 1], axis=0)
                        ).then_inc(sg(f"back{b}"), 16)

        def shared_tensor(pe):
            pe.wait_ge(sg("experts_in"), 32)
            pe.wait_ge(sg("xb_copied"), 2 + BATCH)

            def up(b):
                pe.wait_ge(sg("hs_ready"), b + 1)
                for c in range(4):
                    i = nc.tensor.matmul(bank[:, c, :], experts_up[:, EXPERTS, c * P:(c + 1) * P],
                                         xt_all[:, bass.ds(b * SEQ, SEQ)], start=True, stop=True)
                i.then_inc(sg("su_done"), 1)

            def down(b, p):
                pe.wait_ge(sg("hs_ready"), b + 2)
                pe.wait_ge(sg("acc_ready"), b + 1)
                for j in range(TPB):
                    for m in range(2):
                        i = nc.tensor.matmul(bank[:, 4 + p, j * P:(j + 1) * P], hs[:, p, m, j * P:(j + 1) * P],
                                             experts_down[:, EXPERTS, m, :], start=(m == 0), stop=(m == 1))
                i.then_inc(sg("sd_done"), 1)

            up(0)
            with pe.Fori(0, (BATCH - 2) // 2) as r:
                up(2 * r + 1)
                down(2 * r, 0)
                up(2 * r + 2)
                down(2 * r + 1, 1)
            up(BATCH - 1)
            down(BATCH - 2, 0)
            down(BATCH - 1, 1)

        def shared_scalar(act):
            act.sem_inc(sg("acc_ready"), 2)
            silu(act, 0)
            with act.Fori(0, (BATCH - 2) // 2) as r:
                silu(act, 2 * r + 1)
                out_shared(act, 2 * r, 0)
                silu(act, 2 * r + 2)
                out_shared(act, 2 * r + 1, 1)
            silu(act, BATCH - 1)
            out_shared(act, BATCH - 2, 0)
            out_shared(act, BATCH - 1, 1)

        def silu(act, b):
            act.wait_ge(sg("su_done"), b + 1)
            act.wait_ge(sg("hs_ready"), b + 1)
            nc.scalar.activation(sgs[:, :, :], bank[:, 0:2, :], ACT.Silu).then_inc(sg("sgs_ready"), 1)

        def out_shared(act, b, p):
            act.wait_ge(sg("sd_done"), b + 1)
            nc.scalar.activation(o_all[:, bass.ds(b * TPB, TPB), :],
                                 bank[:, 4 + p, :].rearrange("p (j c) -> p j c", j=TPB), ACT.Identity
                                 ).then_inc(sg("acc_ready"), 1)

        def shared_vector(v):
            v.sem_inc(sg("hs_ready"), 1)
            with v.Fori(0, BATCH // 2) as r:
                for p in range(2):
                    b = 2 * r + p
                    v.wait_ge(sg("sgs_ready"), b + 1)
                    v.wait_ge(sg("acc_ready"), b + 1)
                    nc.vector.tensor_tensor(hs[:, p], sgs[:, :, :], bank[:, 2:4, :], ALU.mult).then_inc(sg("hs_ready"), 1)

        LAG = 3
        XT, GU, HT, YB = 0, 2, 4, 6

        def tiles_on(eng, slot):
            for m in range(8):
                slot(m, m, 0)
            with eng.Fori(1, SLOTS // 8) as r:
                for m in range(8):
                    slot(r * 8 + m, m, r)
            for m in range(LAG):
                slot(SLOTS + m, m, SLOTS // 8)

        def has(s, lag):
            return not isinstance(s, int) or 0 <= s - lag < SLOTS

        def need(eng, name, value, base=0):
            if not isinstance(value, int) or value > 0:
                eng.wait_ge(sg(name), base + value)

        def experts_tensor(pe, n):
            at0 = n * SLOTS
            dma0 = n * 16 * (SLOTS // 8)
            pe.wait_ge(sg("experts_ready"), n + 1)
            pe.wait_ge(sg("experts_in"), 32 * (n + 1))

            def expert(tile):
                return pe.value_load(expert_of[0:1, bass.ds(tile, 1)], min_val=0, max_val=EXPERTS - 1)

            def slot(s, m, r):
                if has(s, 0):
                    if m % 4 == 0:
                        pe.wait_ge(sg(f"rows_in{m // 4}"), dma0 + (r + 1) * 16)
                    nc.tensor.transpose(bank[:, XT + m % 2, 0:P], xr[:, m // 4, m % 4, :], ident).then_inc(sg("x_turned"), 1)
                if has(s, 1):
                    o = (m - 1) % 2
                    e = expert(s - 1)
                    need(pe, "xT_in", s, at0)
                    nc.tensor.matmul(bank[:, GU + o, :], xT2[:, o, :], experts_up[:, e, :], start=True,
                                     stop=True).then_inc(sg("gu_done"), 1)
                if has(s, 2):
                    o = m % 2
                    need(pe, "hb_ready", s - 1, at0)
                    for c in range(2):
                        i = nc.tensor.transpose(bank[:, HT + o, c * P:(c + 1) * P], hb[:, o, c * P:(c + 1) * P], ident)
                    i.then_inc(sg("h_turned"), 1)
                if has(s, 3):
                    o = (m - 3) % 2
                    e = expert(s - 3)
                    need(pe, "hT_in", s - 2, at0)
                    need(pe, "y_out", s - 4, at0)
                    for c in range(2):
                        i = nc.tensor.matmul(bank[:, YB + o, 0:H], hTb[:, o, c * P:(c + 1) * P], experts_down[:, e, c, :],
                                             start=(c == 0), stop=(c == 1))
                    i.then_inc(sg("y_done"), 1)

            tiles_on(pe, slot)

        def experts_scalar(act, n):
            at0 = n * SLOTS
            dma0 = n * 16 * (SLOTS // 8)

            def slot(s, m, r):
                if has(s, 0):
                    need(act, "x_turned", s + 1, at0)
                    need(act, "gu_done", s - 1, at0)
                    nc.scalar.activation(xT2[:, m % 2, :], bank[:, XT + m % 2, 0:P], ACT.Identity).then_inc(sg("xT_in"), 1)
                if has(s, 1):
                    o = (m - 1) % 2
                    need(act, "gu_done", s, at0)
                    need(act, "hb_ready", s - 2, at0)
                    nc.scalar.activation(sgb[:, o, :], bank[:, GU + o, 0:MID], ACT.Silu).then_inc(sg("silu_ready"), 1)
                if has(s, 2):
                    o = m % 2
                    need(act, "h_turned", s - 1, at0)
                    need(act, "y_done", s - 3, at0)
                    nc.scalar.activation(hTb[:, o, :], bank[:, HT + o, 0:MID], ACT.Identity).then_inc(sg("hT_in"), 1)

            tiles_on(act, slot)

        def experts_vector(v, n):
            at0 = n * SLOTS
            dma0 = n * 16 * (SLOTS // 8)

            def slot(s, m, r):
                if has(s, 1):
                    o = (m - 1) % 2
                    need(v, "silu_ready", s, at0)
                    need(v, "h_turned", s - 2, at0)
                    nc.vector.tensor_tensor(hb[:, o, :], sgb[:, o, :], bank[:, GU + o, MID:2 * MID],
                                            ALU.mult).then_inc(sg("hb_ready"), 1)
                if has(s, 3):
                    o = (m - 3) % 2
                    m4 = (m - 3) % 8
                    need(v, "y_done", s - 2, at0)
                    if m4 % 4 == 0 and not (isinstance(r, int) and r == 0):
                        v.wait_ge(sg(f"made{m4 // 4}"), dma0 + r * 16)
                    nc.vector.tensor_copy(yb[:, m4 // 4, m4 % 4, :], bank[:, YB + o, 0:H]).then_inc(sg("y_out"), 1)

            tiles_on(v, slot)

        def experts_sync(sync, n):
            at0 = n * SLOTS
            dma0 = n * 16 * (SLOTS // 8)
            sync.wait_ge(sg("sorted"), 16 * 2 * TILES * (n + 1))
            four = lambda d, k: d.rearrange("(a j p) c -> a p j c", j=4, p=P)[k]
            four_d = lambda d, k: d.rearrange("(a j p) c -> p a j c", j=4, p=P)[:, k]

            def load(k, o):
                sync.dma_start(xr[:, o], four_d(rows_d[n], k)).then_inc(sg(f"rows_in{o}"), 16)

            def store(k, o):
                sync.wait_ge(sg("y_out"), at0 + 4 * k + 4)
                sync.dma_start(four_d(made_d[n], k), yb[:, o]).then_inc(sg(f"made{o}"), 16)

            load(0, 0)
            load(1, 1)
            with sync.Fori(0, SLOTS // 8 - 1) as r:
                for o in range(2):
                    k = 2 * r + o
                    sync.wait_ge(sg("x_turned"), at0 + 4 * k + 4)
                    load(k + 2, o)
                    store(k, o)
            for o in range(2):
                store(SLOTS // 4 - 2 + o, o)

        rows_of = [rows, tiles(big[2])]

        def lead0(b, p):
            for k in range(TPB):
                t = b * TPB + k
                i = nc.vector.tensor_scalar(xa[:, p, k, :], xres[:, t, :], mean[:, bass.ds(t, 1)],
                                            rstd[:, bass.ds(t, 1)], ALU.subtract, ALU.mult)
            i.then_inc(sg("xa_ready"), 1)

        lead0.steps = 0

        def moe0_vector(v):
            v.sem_inc(sg("lg_out"), 2)
            v.wait_ge(sg("rstd_ready"), 5)
            route_vector(v, 0, lead0)
            vdo(v, nc.vector.tensor_tensor(key[:, :, :], lg[:, :, :], par("beta0")[:, None, :].broadcast_to([P, TILES, EXPERTS]),
                                           ALU.add))
            v.wait_ge(sg("pr_ready"), 1)
            place_vector(v, 0)
            shared_vector(v)
            experts_vector(v, 0)
            v.wait_ge(sg("acc_ready"), 2 + BATCH)
            for b in range(BATCH):
                v.wait_ge(sg(f"back{b}"), 16 * 2 * TPB)
                for k in range(2):
                    for t in range(b * TPB, (b + 1) * TPB):
                        i = nc.vector.scalar_tensor_tensor(o_all[:, t, :], got[k][:, t, :], gain[:, k, t:t + 1],
                                                           o_all[:, t, :], ALU.mult, ALU.add)
                    vdo(v, i)
                for t in range(b * TPB, (b + 1) * TPB):
                    i = nc.vector.bn_stats(st[:, t, :], o_all[:, t, :])
            vdo(v, i)
            moments(v, 0, TILES)
            residual(v, o_all, 6)
            v.wait_ge(v_step, cv.now)

        got = [tiles(big[0]), tiles(big[1])]

        def moe0_scalar(act):
            route_scalar(act, 0)
            act.wait_ge(sg("lg_out"), BATCH + 2)
            nc.scalar.activation(pr[:, :, :], lg[:, :, :], ACT.Sigmoid).then_inc(sg("pr_ready"), 1)
            shared_scalar(act)
            experts_scalar(act, 0)

        def moe0_tensor(pe):
            route_tensor(pe, 0)
            shared_tensor(pe)
            experts_tensor(pe, 0)

        def moe0_gpsimd(pool):
            route_gpsimd(pool, 0)
            scatter_gpsimd(pool, 0, [rows, rows])
            gather_gpsimd(pool, 0, got)
            rsqrts(0, TILES)
            rsqrts(0, TILES, twice=True)


        dt, xc, sz = big[0], big[1], big[2]
        f_res = tiles(big[3])
        end_of_moe = carved[0]
        carved[0] = 0
        xf = carve("xf", [P, 2, TPB, H])
        xfT = carve("xfT", [P, 2, SEQ])
        xxp = carve("xxp", [P, 2, SEQ + 2])
        cvd = carve("cvd", [P, 2, SEQ])
        bcr = carve("bcr", [P, 2, SEQ])
        bch = carve("bch", [P, 2, SEQ], BF16)
        bcm = carve("bcm", [P, 2, SEQ], BF16)
        bc3 = carve("bc3", [P, TOKENS], BF16)
        pick = carve("pick", [P, 2 * STATE, P], BF16)
        neg_a = carve("neg_a", [P, 2, STATE])
        da = carve("da", [P, 2, SEQ])
        db = carve("db", [P, 4, SEQ])
        sta = carve("sta", [P, 2, SEQ])
        cs = carve("cs", [P, 2, SEQ])
        yc = carve("yc", [P, 4, SEQ])
        yf = carve("yf", [P, 2, SEQ])
        lnx = carve("lnx", [P, TPB, H])
        ROWS = 3 * 2 * STATE

        def at_b(a, b):
            return a[:, bass.ds(b * SEQ, SEQ)]

        def ssm_prep_vector(v):
            nc.vector.memset(xxp[:, :, 0:SEQ + 2], 0.0).then_inc(sg("xxp_zero"), 1)
            nc.vector.tensor_copy(pick[0:ROWS], par("pick")[0:ROWS, :, None].broadcast_to([ROWS, 2 * STATE, P])
                                  ).then_inc(sg("pick_ready"), 1)
            v.sem_inc(sg("cv_free"), 2)
            v.wait_ge(sg("rstd_ready"), 7)

            def norm(b, p):
                v.wait_ge(sg("f_turned"), b + 1)
                for k in range(TPB):
                    t = b * TPB + k
                    i = nc.vector.tensor_scalar(xf[:, p, k, :], xres[:, t, :], mean[:, bass.ds(t, 1)],
                                                rstd2[:, bass.ds(t, 1)], ALU.subtract, ALU.mult)
                i.then_inc(sg("f_rows"), 1)

            def conv(b, p):
                v.wait_ge(sg("xx_ready"), b + 1)
                v.wait_ge(sg("xc_ready"), b + 1)
                w = lambda k: par("sconv", k, k + 1)
                vdo(v, nc.vector.tensor_scalar(cvd[:, p], xxp[:, p, 0:SEQ], w(0), None, ALU.mult))
                vdo(v, nc.vector.scalar_tensor_tensor(cvd[:, p], xxp[:, p, 1:SEQ + 1], w(1), cvd[:, p], ALU.mult, ALU.add))
                nc.vector.scalar_tensor_tensor(cvd[:, p], xxp[:, p, 2:SEQ + 2], w(2), cvd[:, p],
                                               ALU.mult, ALU.add).then_inc(sg("cv_done"), 1)

            def split(b, p):
                v.wait_ge(sg("bc_first"), b + 1)
                nc.vector.tensor_tensor(bcr[0:ROWS, p], bank[0:ROWS, 7, :], bch[0:ROWS, p], ALU.subtract).then_inc(sg("bc_rest"), 1)
                v.wait_ge(sg("bc_second"), b + 1)
                nc.vector.tensor_tensor(at_b(bc3, b)[64:ROWS], bcr[64:ROWS, p], bcm[64:ROWS, p], ALU.subtract).then_inc(sg("bc_third"), 1)

            with cv.loop(v, BATCH // 2, 4) as r:
                for p in range(2):
                    norm(2 * r + p, p)
                for p in range(2):
                    conv(2 * r + p, p)
                for p in range(2):
                    split(2 * r + p, p)
            v.wait_ge(sg("dt_parts"), 2)
            nc.vector.scalar_tensor_tensor(dt[:, :], dt[:, :], 0.0, big[3][:, :], ALU.max, ALU.add).then_inc(sg("dt_ready"), 1)
            nc.vector.tensor_scalar(neg_a[:, 1, :], neg_a[:, 0, :], -1.0, None, ALU.mult).then_inc(sg("dt_ready"), 1)

        def ssm_prep_tensor(pe):
            pe.sem_inc(sg("f_turned"), 2)
            with pe.Fori(0, BATCH // 2) as r:
                def head(b, p):
                    pe.wait_ge(sg("f_rows"), b + 1)
                    for j in range(TPB):
                        i = nc.tensor.transpose(bank[:, p, j * P:(j + 1) * P], xf[:, p, j, :], ident)
                    i.then_inc(sg("f_turned"), 1)
                    pe.wait_ge(sg("fT_ready"), b + 1)
                    pe.wait_ge(sg("z_ready"), b + 1)
                    nc.tensor.matmul(bank[:, 2 + p, :], par("w_in", 0, H), xfT[:, p], start=True, stop=True)
                    nc.tensor.matmul(bank[:, 4 + p, :], par("w_in", H, 2 * H), xfT[:, p], start=True,
                                     stop=True).then_inc(sg("xz_done"), 1)

                def tail(b, p):
                    pe.wait_ge(sg("xc_ready"), b + 3)
                    pe.wait_ge(sg("bc_read"), b + 1)
                    nc.tensor.matmul(bank[:, 6, :], par("w_dt"), at_b(xc, b), start=True, stop=True)
                    nc.tensor.matmul(bank[0:ROWS, 7, :], par("w_bc"), at_b(xc, b), start=True,
                                     stop=True).then_inc(sg("dtbc_done"), 1)

                for p in range(2):
                    head(2 * r + p, p)
                for p in range(2):
                    tail(2 * r + p, p)

        def ssm_prep_scalar(act):
            act.sem_inc(sg("z_ready"), 2)
            act.sem_inc(sg("xz_free"), 2)
            act.sem_inc(sg("xc_ready"), 2)
            act.sem_inc(sg("bc_read"), 1)
            act.wait_ge(sg("xxp_zero"), 1)
            with act.Fori(0, BATCH // 2) as r:
                def head(b, p):
                    act.wait_ge(sg("f_turned"), b + 3)
                    act.wait_ge(sg("xz_free"), b + 1)
                    nc.scalar.activation(xfT[:, p], bank[:, p, :], ACT.Identity, bias=par("beta"),
                                         scale=par("gamma")).then_inc(sg("fT_ready"), 1)
                    act.wait_ge(sg("xz_done"), b + 1)
                    act.sem_inc(sg("xz_free"), 1)
                    act.wait_ge(sg("cv_free"), b + 1)
                    nc.scalar.activation(xxp[:, p, 1:SEQ + 1], bank[:, 2 + p, :], ACT.Identity).then_inc(sg("xx_ready"), 1)
                    nc.scalar.activation(at_b(sz, b), bank[:, 4 + p, :], ACT.Silu).then_inc(sg("z_ready"), 1)

                def mid(b, p):
                    act.wait_ge(sg("cv_done"), b + 1)
                    act.sem_inc(sg("cv_free"), 1)
                    nc.scalar.activation(at_b(xc, b), cvd[:, p], ACT.Silu).then_inc(sg("xc_ready"), 1)

                def tail(b, p):
                    act.wait_ge(sg("dtbc_done"), b + 1)
                    act.sem_inc(sg("act_go"), 1)
                    nc.scalar.activation(at_b(big[3], b), bank[:, 6, :], ACT.Abs, bias=par("b_dt"))
                    nc.scalar.activation(at_b(dt, b), bank[:, 6, :], ACT.Identity, bias=par("b_dt"))
                    nc.scalar.activation(at_b(bc3, b)[0:32], bank[0:32, 7, :], ACT.Identity)
                    nc.scalar.activation(bch[0:ROWS, p], bank[0:ROWS, 7, :], ACT.Identity).then_inc(sg("bc_first"), 1)
                    act.wait_ge(sg("bc_rest"), b + 1)
                    act.sem_inc(sg("bc_read"), 1)
                    nc.scalar.activation(at_b(bc3, b)[32:64], bcr[32:64, p], ACT.Identity)
                    nc.scalar.activation(bcm[64:ROWS, p], bcr[64:ROWS, p], ACT.Identity).then_inc(sg("bc_second"), 1)

                for p in range(2):
                    head(2 * r + p, p)
                for p in range(2):
                    mid(2 * r + p, p)
                for p in range(2):
                    tail(2 * r + p, p)
            act.wait_ge(sg("bc_second"), BATCH)
            nc.scalar.activation(big[3][:, :], big[3][:, :], ACT.Exp, scale=-1.0).then_inc(a_step, ca.one())
            nc.scalar.activation(neg_a[:, 0, :], par("a_log"), ACT.Exp).then_inc(sg("dt_parts"), 1)
            act.wait_ge(a_step, ca.now)
            nc.scalar.activation(big[3][:, :], big[3][:, :], ACT.Ln, bias=1.0).then_inc(sg("dt_parts"), 1)

        BB, CB, Y_B, O_B = 0, 2, 4, 5

        def batches_on(eng, batch):
            batch(0, False)
            with eng.Fori(1, BATCH) as b:
                batch(b, True)

        def scan_vector(v):
            v.wait_ge(sg("dt_ready"), 2)

            def scan(u, s):
                p = s % 2
                v.wait_ge(sg("da_ready"), u + 1)
                v.wait_ge(sg("db_ready"), u + 1)
                need(v, "yc_ready", u - 1)
                nc.vector.tensor_tensor_scan(sta[:, p], da[:, p], db[:, s % 4], 0.0, ALU.mult, ALU.add).then_inc(sg("state_ready"), 1)

            def final(b):
                v.wait_ge(sg("y_summed"), 16 * b + 16)
                nc.vector.scalar_tensor_tensor(yf[:, 0], at_b(xc, b), par("skip_d"), bank[:, Y_B, :],
                                               ALU.mult, ALU.add).then_inc(sg("y_read"), 1)
                v.wait_ge(sg("y_read"), b + 1)
                nc.vector.tensor_tensor(yf[:, 1], yf[:, 0], at_b(sz, b), ALU.mult).then_inc(sg("yf_ready"), 1)

            def result(b):
                for k in range(TPB):
                    t = b * TPB + k
                    i = nc.vector.tensor_scalar(lnx[:, k, :], xres[:, t, :], mean[:, bass.ds(t, 1)],
                                                rstd[:, bass.ds(t, 1)], ALU.subtract, ALU.mult)
                i.then_inc(sg("lnx"), 1)
                v.wait_ge(sg("lnx"), b + 1)
                v.wait_ge(sg("out_done_f"), b + 1)
                nc.vector.tensor_tensor(f_res[:, bass.ds(b * TPB, TPB), :], lnx[:, :, :],
                                        bank[:, O_B, :].rearrange("p (k c) -> p k c", k=TPB), ALU.add).then_inc(sg("res_ready"), 1)
                v.wait_ge(sg("res_ready"), b + 1)
                for k in range(TPB):
                    i = nc.vector.bn_stats(st[:, b * TPB + k, :], f_res[:, b * TPB + k, :])
                i.then_inc(sg("f_stats"), 1)

            def batch(b, back):
                for s in range(STATE):
                    u = b * STATE + s
                    if back and s == 2:
                        final(b - 1)
                    if back and s == 5:
                        result(b - 1)
                    v.wait_ge(sg("b_done"), u + 1)
                    need(v, "state_ready", u - 3)
                    nc.vector.tensor_tensor(db[:, s % 4], at_b(dt, b), bank[:, BB + s % 2, :], ALU.mult).then_inc(sg("db_ready"), 1)
                    if s > 0 or back:
                        scan(u - 1, (s - 1) % STATE)

            batches_on(v, batch)
            scan(BATCH * STATE - 1, STATE - 1)
            final(BATCH - 1)
            result(BATCH - 1)
            v.wait_ge(sg("f_stats"), BATCH)
            moments(v, 0, TILES)
            residual(v, f_res, 8)
            v.wait_ge(v_step, cv.now)
            moments(v, 0, TILES, twice=True)

        def scan_scalar(act):
            act.wait_ge(sg("dt_ready"), 2)

            def batch(b, back):
                for s in range(STATE):
                    u = b * STATE + s
                    need(act, "state_ready", u - 1)
                    act.sem_inc(sg("act_go"), 1)
                    nc.scalar.activation(da[:, s % 2], at_b(dt, b), ACT.Exp, scale=neg_a[:, 1, s:s + 1]).then_inc(sg("da_ready"), 1)
                    act.wait_ge(sg("c_done"), u + 1)
                    need(act, "yc_ready", u - 1)
                    nc.scalar.activation(cs[:, s % 2], bank[:, CB + s % 2, :], ACT.Identity).then_inc(sg("cs_ready"), 1)

            batches_on(act, batch)

        def scan_gpsimd(pool):
            def batch(b, back):
                for s in range(STATE):
                    u = b * STATE + s
                    pool.wait_ge(sg("state_ready"), u + 1)
                    pool.wait_ge(sg("cs_ready"), u + 1)
                    need(pool, "y_summed", u - 3)
                    nc.gpsimd.tensor_tensor(yc[:, s % 4], sta[:, s % 2], cs[:, s % 2], ALU.mult).then_inc(sg("yc_ready"), 1)

            batches_on(pool, batch)
            rsqrts(0, TILES)
            rsqrts(0, TILES, twice=True)

        def scan_tensor(pe):
            pe.wait_ge(sg("pick_ready"), 1)
            pe.wait_ge(sg("bc_third"), BATCH)
            pe.wait_ge(sg("dt_ready"), 1)

            def summed(b, s):
                u = b * STATE + s
                if s == 0:
                    need(pe, "y_read", b)
                pe.wait_ge(sg("yc_ready"), u + 1)
                nc.tensor.matmul(bank[:, Y_B, :], ident, yc[:, s % 4], start=(s == 0), stop=(s == STATE - 1)
                                 ).then_inc(sg("y_summed"), 1)

            def output(b):
                pe.wait_ge(sg("yf_ready"), b + 1)
                need(pe, "res_ready", b)
                for k in range(TPB):
                    i = nc.tensor.matmul(bank[:, O_B, k * H:(k + 1) * H], yf[:, 1, k * P:(k + 1) * P], par("w_out"),
                                         start=True, stop=True)
                i.then_inc(sg("out_done_f"), 1)

            def batch(b, back):
                for s in range(STATE):
                    u = b * STATE + s
                    need(pe, "db_ready", u - 1)
                    nc.tensor.matmul(bank[:, BB + s % 2, :], pick[0:ROWS, s, :], at_b(bc3, b)[0:ROWS],
                                     start=True, stop=True).then_inc(sg("b_done"), 1)
                    need(pe, "cs_ready", u - 1)
                    nc.tensor.matmul(bank[:, CB + s % 2, :], pick[0:ROWS, STATE + s, :], at_b(bc3, b)[0:ROWS],
                                     start=True, stop=True).then_inc(sg("c_done"), 1)
                    if s >= 2:
                        summed(b, s - 2)
                    elif back:
                        summed(b - 1, STATE - 2 + s)
                    if back and s == 4:
                        output(b - 1)

            batches_on(pe, batch)
            summed(BATCH - 1, STATE - 2)
            summed(BATCH - 1, STATE - 1)
            output(BATCH - 1)

        carved[0] = end_of_moe
        xe = [tiles(big[0]), tiles(big[1])]
        rows1 = tiles(big[2])
        m1 = lambda k: m32[:, k, :]

        def lead1(b, p):
            for k in range(TPB):
                t = b * TPB + k
                i = nc.vector.tensor_scalar(xa[:, p, k, :], xres[:, t, :], mean[:, bass.ds(t, 1)],
                                            rstd2[:, bass.ds(t, 1)], ALU.subtract, ALU.mult)
            vdo(nc.vector, i)
            vdo(nc.vector, nc.vector.tensor_tensor(xa[:, p], xa[:, p], par("ln_g")[:, None, :].broadcast_to([P, TPB, H]), ALU.mult))
            nc.vector.tensor_tensor(xa[:, p], xa[:, p], par("ln_b")[:, None, :].broadcast_to([P, TPB, H]),
                                    ALU.add).then_inc(sg("xa_ready"), 1)

        lead1.steps = 2

        def moe1_vector(v):
            v.wait_ge(sg("rstd_ready"), 9)
            route_vector(v, 1, lead1)
            vdo(v, nc.vector.tensor_scalar(lg[:, :, :], lg[:, :, :], -10000.0, 10000.0, ALU.max, ALU.min))
            vdo(v, nc.vector.tensor_reduce(m1(0), lg[:, :, :], AX, ALU.max))
            nc.vector.tensor_tensor(key[:, :, :], lg[:, :, :], wide(m1(0)), ALU.subtract).then_inc(sg("key_ready"), 1)
            v.wait_ge(sg("pr_ready"), 2)
            vdo(v, nc.vector.tensor_reduce(m1(0), pr[:, :, :], AX, ALU.add))
            vdo(v, nc.vector.tensor_scalar(m1(0), m1(0), 1e-8, None, ALU.add))
            vdo(v, nc.vector.reciprocal(m1(1), m1(0)))
            vdo(v, nc.vector.tensor_tensor(pr[:, :, :], pr[:, :, :], wide(m1(1)), ALU.mult))
            vdo(v, nc.vector.tensor_scalar(pr[:, :, :], pr[:, :, :], 1e-8, 1.0, ALU.max, ALU.min))
            vdo(v, nc.vector.tensor_copy(key[:, :, :], pr[:, :, :]))
            place_vector(v, 1)
            v.wait_ge(sg("xa_copied"), 2 + 2 * BATCH)
            with v.Fori(0, BATCH) as b:
                for k in range(2):
                    for j in range(TPB):
                        t = b * TPB + j
                        i = nc.vector.tensor_scalar(xe[k][:, t, :], rows1[:, t, :], gain[:, k, bass.ds(t, 1)], None, ALU.mult)
                i.then_inc(sg("xe_ready"), 1)
            experts_vector(v, 1)
            for b in range(BATCH):
                four = slice(b * TPB, (b + 1) * TPB)
                for t in range(b * TPB, (b + 1) * TPB):
                    i = nc.vector.tensor_scalar(f_res[:, t, :], xres[:, t, :], mean[:, t:t + 1], rstd[:, t:t + 1],
                                                ALU.subtract, ALU.mult)
                vdo(v, i)
                v.wait_ge(sg(f"back{b}"), 2 * 16 * 2 * TPB)
                for k in range(2):
                    vdo(v, nc.vector.tensor_tensor(f_res[:, four, :], f_res[:, four, :], xe[k][:, four, :], ALU.add))
                for t in range(b * TPB, (b + 1) * TPB):
                    i = nc.vector.bn_stats(st[:, t, :], f_res[:, t, :])
            vdo(v, i)
            moments(v, 0, TILES)
            v.wait_ge(sg("rstd_ready"), 10)
            for b in range(BATCH):
                four = slice(b * TPB, (b + 1) * TPB)
                for t in range(b * TPB, (b + 1) * TPB):
                    i = nc.vector.tensor_scalar(f_res[:, t, :], f_res[:, t, :], mean[:, t:t + 1], rstd[:, t:t + 1],
                                                ALU.subtract, ALU.mult)
                vdo(v, i)
                nc.vector.tensor_tensor(xres[:, four, :], xres[:, four, :], f_res[:, four, :], ALU.add).then_inc(sg("x_out"), 1)

        def moe1_scalar(act):
            route_scalar(act, 1)
            act.wait_ge(sg("key_ready"), 1)
            nc.scalar.activation(pr[:, :, :], key[:, :, :], ACT.Exp).then_inc(sg("pr_ready"), 1)
            experts_scalar(act, 1)

        def moe1_tensor(pe):
            route_tensor(pe, 1)
            experts_tensor(pe, 1)

        def moe1_gpsimd(pool):
            route_gpsimd(pool, 1)
            pool.wait_ge(sg("xe_ready"), BATCH)
            scatter_gpsimd(pool, 1, xe)
            gather_gpsimd(pool, 1, xe)
            rsqrts(0, TILES)

        def moe1_sync(sync):
            sync.wait_ge(sg("y_out"), SLOTS)
            sync.dma_start(experts_up[:, 0:EXPERTS, :], up1_d).then_inc(sg("experts_in"), 16)
            sync.dma_start(experts_down[:, 0:EXPERTS, :, :], down1_d).then_inc(sg("experts_in"), 16)
            experts_sync(sync, 1)
            for b in range(BATCH):
                sync.wait_ge(sg("x_out"), b + 1)
                sync.dma_start(out_d.rearrange("(t p) c -> p t c", p=P)[:, b * TPB:(b + 1) * TPB, :],
                               xres[:, b * TPB:(b + 1) * TPB, :]).then_inc(sg("stored"), 16)
            sync.wait_ge(sg("stored"), 16 * BATCH)

        block = ctx.enter_context(nc.Block())

        @block.sync
        def _(sync):
            prep_sync(sync)
            experts_sync(sync, 0)
            moe1_sync(sync)

        @block.gpsimd
        def _(pool):
            prep_gpsimd(pool)
            recur_gpsimd(pool)
            post_gpsimd(pool)
            moe0_gpsimd(pool)
            scan_gpsimd(pool)
            moe1_gpsimd(pool)

        @block.vector
        def _(v):
            prep_vector(v)
            recur_vector(v)
            post_vector(v)
            moe0_vector(v)
            moments(v, 0, TILES, twice=True)
            ssm_prep_vector(v)
            scan_vector(v)
            moe1_vector(v)

        @block.tensor
        def _(pe):
            prep_tensor(pe)
            recur_tensor(pe)
            post_tensor(pe)
            moe0_tensor(pe)
            ssm_prep_tensor(pe)
            scan_tensor(pe)
            moe1_tensor(pe)

        @block.scalar
        def _(act):
            prep_scalar(act)
            recur_scalar(act)
            post_scalar(act)
            moe0_scalar(act)
            ssm_prep_scalar(act)
            scan_scalar(act)
            moe1_scalar(act)


def _packed(x):
    def rows(v):
        return np.broadcast_to(v[None, :], (P, v.shape[0]))

    def bd(v):
        return np.tile(v, (B4, 1))

    part = {}
    part["proj"] = np.concatenate([x["L0_attn_W" + n].T for n in "kvq"] +
                                  [x["L0_attn_" + n + "W"].T for n in "aet"], axis=1)
    part["gate"] = x["L0_attn_gW"].T
    part["gate_b"] = rows(x["L0_attn_gb"])
    part["norm_g"] = rows(x["L0_attn_norm_g"])
    wo = np.zeros((B4, D, B4, H), np.float32)
    for b in range(B4):
        wo[b, :, b, :] = x["L0_attn_Wo"].T
    part["wo"] = wo.reshape(P, B4 * H)
    part["conv_w"] = np.concatenate([bd(x[f"L0_attn_c{n}w"]) for n in "kvq"], axis=1)
    part["conv_b"] = np.concatenate([bd(x[f"L0_attn_c{n}b"][:, None]) for n in "kvq"], axis=1)
    part["bias3"] = np.concatenate([bd(x[f"L0_attn_{n}b"][:, None]) for n in "aet"], axis=1)
    part["mem"] = np.concatenate([bd(x["L0_attn_mW1"].T), bd(x["L0_attn_mW2"].T)], axis=1)
    part["route0"] = x["L0_ffn_gate_w"].T
    part["beta0"] = rows(x["L0_ffn_beta"])
    part["route1"] = x["L1_ffn_router_w"].T
    part["ln_g"] = rows(x["L1_ffn_ln_gamma"])
    part["ln_b"] = rows(x["L1_ffn_ln_beta"])
    part["w_in"] = x["L1_attn_W_in"].T
    part["w_bc"] = np.tile(x["L1_attn_W_x"].T, (1, 3))
    part["w_dt"] = x["L1_attn_W_dt"].T
    part["w_out"] = x["L1_attn_W_out"].T
    part["sconv"] = x["L1_attn_conv_w"][:, 0, :]
    part["b_dt"] = x["L1_attn_b_dt"][:, None]
    part["a_log"] = x["L1_attn_A_log"]
    part["skip_d"] = x["L1_attn_D_param"][:, None]
    part["gamma"] = x["L1_attn_gamma"][:, None]
    part["beta"] = x["L1_attn_beta"][:, None]
    p = np.arange(P)
    part["ident"] = np.eye(P)
    part["quad"] = (p[:, None] // D == p[None, :] // D)
    part["neg_i"] = -(p[:, None] % CHUNK == np.arange(CHUNK)[None, :]).astype(np.float32)
    part["mean_bd"] = (p[:, None] // D == p[None, :] // D) / D
    part["mean_sel"] = (p[:, None] // D == np.arange(B4 * 64)[None, :] // 64) / D
    part["before"] = (p[:, None] < p[None, :])
    part["ones"] = np.ones((P, P))
    part["rank8"] = rows(np.arange(EXPERTS, 0, -1))
    part["edge"] = rows(np.arange(TILES) * P)
    part["slot"] = rows(np.arange(SLOTS))
    part["pick"] = (p[:, None] % (2 * STATE) == np.arange(2 * STATE)[None, :])
    packed = np.zeros((P, PACKED), np.float32)
    for name, (at, width) in AT.items():
        assert part[name].shape == (P, width), (name, part[name].shape)
        packed[:, at:at + width] = part[name]
    return packed


def _experts(up, down):
    n = up.shape[0]
    return (np.ascontiguousarray(up.transpose(1, 0, 2)),
            np.ascontiguousarray(down.reshape(n, 2, P, H).transpose(2, 0, 1, 3)))


def kernel(**inputs):
    import concourse.bacc as _bacc
    from concourse.bass_utils import run_bass_kernel_spmd as _run

    x = {k: np.asarray(v) for k, v in inputs.items()}
    up0 = np.concatenate([np.concatenate([x["L0_ffn_gate_proj_w"], x["L0_ffn_shared_gate_w"]]),
                          np.concatenate([x["L0_ffn_up_proj_w"], x["L0_ffn_shared_up_w"]])], axis=2)
    down0 = np.concatenate([x["L0_ffn_down_proj_w"], x["L0_ffn_shared_down_w"]])
    up0, down0 = _experts(up0, down0)
    up1, down1 = _experts(x["L1_ffn_gate_up_w"].transpose(0, 2, 1), x["L1_ffn_down_w"].transpose(0, 2, 1))
    arrays = {"x": np.ascontiguousarray(x["L0_attn_hidden"]).reshape(TOKENS, H), "packed": _packed(x),
              "up0": up0, "down0": down0, "up1": up1, "down1": down1}
    nc = _bacc.Bacc("TRN2", target_bir_lowering=False, num_devices=1)
    args = [nc.dram_tensor(n, a.shape, F32, kind="ExternalInput").ap() for n, a in arrays.items()]
    out = nc.dram_tensor("out", (TOKENS, H), F32, kind="ExternalOutput").ap()
    build(nc, *args, out)
    r = _run(nc, [arrays], core_ids=[0])
    return r.results[0]["out"].reshape(BATCH, SEQ, H)
```

```python
from contextlib import ExitStack, contextmanager

import numpy as np

import concourse.bass as bass
from concourse import mybir

F32 = mybir.dt.float32
BF16 = mybir.dt.bfloat16
I32 = mybir.dt.int32
ALU = mybir.AluOpType
ACT = mybir.ActivationFunctionType
AX = mybir.AxisListType.X

P = 128
BATCH, SEQ, H = 8, 512, 128
TOKENS = BATCH * SEQ
TILES = TOKENS // P
TPB = SEQ // P
GROUPS, B4 = 2, 4
D = 32
CHUNK = 64
CHUNKS = SEQ // CHUNK
EXPERTS, MID = 8, 256
HALVES = 2
HALF = TILES // HALVES
HALF_SLOTS = 2 * HALF + EXPERTS
SLOTS = HALVES * HALF_SLOTS
STATE = 16
EPS = 1e-5

PARTS = [
    ("proj", 6 * D), ("gate", H), ("gate_b", H), ("norm_g", H), ("wo", B4 * H),
    ("conv_w", 12), ("conv_b", 3), ("bias3", 3), ("mem", 2 * D),
    ("route0", EXPERTS), ("beta0", EXPERTS), ("route1", EXPERTS), ("ln_g", H), ("ln_b", H),
    ("w_in", 2 * H), ("w_bc", 3 * 2 * STATE), ("w_dt", H), ("w_out", H),
    ("sconv", 3), ("b_dt", 1), ("a_log", STATE), ("skip_d", 1), ("gamma", 1), ("beta", 1),
    ("ident", P), ("quad", P), ("neg_i", CHUNK), ("mean_bd", P), ("mean_sel", B4 * 64),
    ("before", P), ("ones", P), ("rank8", EXPERTS), ("edge", TILES), ("slot", HALF_SLOTS),
    ("pick", 2 * STATE),
]
AT = {}
_at = 0
for _name, _width in PARTS:
    AT[_name] = (_at, _width)
    _at += _width
PACKED = _at


class Count:

    def __init__(self):
        self.base, self.k = 0, 0

    def one(self):
        self.k += 1
        return 1

    @property
    def now(self):
        return self.base + self.k

    @contextmanager
    def loop(self, eng, n, per):
        start = self.now
        with eng.Fori(0, n) as i:
            self.base, self.k = start + i * per, 0
            yield i
            assert self.k == per, f"{self.k} increments in a round, {per} said"
        self.base, self.k = start + n * per, 0

STEPS_V = 15
SCRATCH = 20500


def build(nc, x_d, packed_d, up0_d, down0_d, up1_d, down1_d, out_d):
    ctx = ExitStack()
    with ctx:
        def sb(name, shape, dt=F32):
            return ctx.enter_context(nc.sbuf_tensor(name, shape, dt))

        def sem(name):
            return ctx.enter_context(nc.semaphore(name))

        xres = sb("xres", [P, TILES, H])
        pk = sb("pk", [P, PACKED])

        def par(name, a=0, b=None):
            at, width = AT[name]
            return pk[:, at + a:at + (width if b is None else b)]

        big = [sb(f"big{n}", [P, TOKENS]) for n in range(4)]
        experts_up = sb("experts_up", [P, EXPERTS + 1, 2 * MID])
        experts_down = sb("experts_down", [P, EXPERTS + 1, 2, H])
        scratch = sb("scratch", [P, SCRATCH])
        carved = [0]

        def carve(name, shape, dt=F32):
            n = int(np.prod(shape[1:])) // (2 if dt == BF16 else 1)
            a = scratch[:, carved[0]:carved[0] + n]
            carved[0] += n
            assert carved[0] <= SCRATCH, (name, carved[0])
            if dt != F32:
                a = a.bitcast(dt)
            axes = " ".join(f"a{k}" for k in range(1, len(shape)))
            if len(shape) == 2:
                return a
            return a.rearrange(f"p ({axes}) -> p {axes}", **{f"a{k}": shape[k] for k in range(1, len(shape))})

        ident, quad = par("ident"), par("quad")
        quad4 = quad.rearrange("p (b c) -> p b c", b=B4)
        pow_c = sb("pow_c", [P, TILES])
        st = sb("st", [P, TILES, 6])
        mean = sb("mean", [P, TILES])
        var = sb("var", [P, TILES])
        var2 = sb("var2", [P, TILES])
        rstd = sb("rstd", [P, TILES])
        rstd2 = sb("rstd2", [P, TILES])
        lnts = sb("lnts", [P, 2, 3, TILES])

        bank = ctx.enter_context(nc.psum_tensor("bank", [P, 8, 512], F32))

        S = {}

        def sg(name):
            if name not in S:
                S[name] = sem(name)
            return S[name]

        v_step, p_step, a_step = sg("v_step"), sg("p_step"), sg("a_step")
        cv, cp, ca = Count(), Count(), Count()

        def moments(v, lo, hi, twice=False):
            n = hi - lo
            lnt = lnts[:, n_asked[0] % 2]
            s = st[:, lo:hi, :]
            nc.vector.tensor_tensor(lnt[:, 0, 0:n], s[:, :, 1], s[:, :, 4], ALU.add).then_inc(v_step, cv.one())
            nc.vector.tensor_tensor(lnt[:, 1, 0:n], s[:, :, 1], s[:, :, 4], ALU.subtract).then_inc(v_step, cv.one())
            nc.vector.tensor_tensor(lnt[:, 2, 0:n], s[:, :, 2], s[:, :, 5], ALU.add).then_inc(v_step, cv.one())
            v.wait_ge(v_step, cv.now)
            nc.vector.tensor_scalar(mean[:, lo:hi], lnt[:, 0, 0:n], 0.5, None, ALU.mult).then_inc(v_step, cv.one())
            nc.vector.tensor_scalar(lnt[:, 2, 0:n], lnt[:, 2, 0:n], 1.0 / H, EPS, ALU.mult, ALU.add).then_inc(v_step, cv.one())
            nc.vector.scalar_tensor_tensor(lnt[:, 1, 0:n], lnt[:, 1, 0:n], 0.25, lnt[:, 1, 0:n],
                                           ALU.mult, ALU.mult).then_inc(v_step, cv.one())
            v.wait_ge(v_step, cv.now)
            if twice:
                nc.vector.tensor_tensor(var[:, lo:hi], lnt[:, 1, 0:n], lnt[:, 2, 0:n], ALU.add).then_inc(v_step, cv.one())
                v.wait_ge(v_step, cv.now)
                nc.vector.tensor_scalar(var2[:, lo:hi], var[:, lo:hi], 1.0 + EPS, -EPS,
                                        ALU.mult, ALU.add).then_inc(sg("var_ready"), 1)
            else:
                nc.vector.tensor_tensor(var[:, lo:hi], lnt[:, 1, 0:n], lnt[:, 2, 0:n],
                                        ALU.add).then_inc(sg("var_ready"), 1)
            n_asked[0] += 1
            return n_asked[0]

        n_asked = [0]
        n_var = [0]

        def rsqrts(lo, hi, twice=False):
            n_var[0] += 1
            nc.gpsimd.wait_ge(sg("var_ready"), n_var[0])
            i = nc.gpsimd.tensor_tensor(rstd[:, lo:hi], var[:, lo:hi], pow_c[:, lo:hi], ALU.pow)
            if twice:
                i = nc.gpsimd.tensor_tensor(rstd2[:, lo:hi], var2[:, lo:hi], pow_c[:, lo:hi], ALU.pow)
            i.then_inc(sg("rstd_ready"), 1)

        if True:
            xn = carve("xn", [P, 2, TPB, H])
            xT = carve("xT", [P, 2, SEQ])
            pre = carve("pre", [P, 3, 4 + SEQ])
            kvq = carve("kvq", [P, 3, GROUPS, SEQ])
            w_st = carve("w_st", [P, GROUPS, SEQ])
            b_st = carve("b_st", [P, GROUPS, SEQ])
            e_st = carve("e_st", [P, GROUPS, SEQ])
            gw_n = carve("gw_n", [P, H])
            gb_n = carve("gb_n", [P, H])
            gate_t = big[0][:, :].rearrange("p (t c) -> p t c", t=TILES)
            sga = big[1][:, 0:1024].rearrange("p (g n) -> p g n", g=GROUPS)
            sge = big[1][:, 1024:2048].rearrange("p (g n) -> p g n", g=GROUPS)
            tabs = big[1][:, 2048:3072].rearrange("p (g n) -> p g n", g=GROUPS)
            tlin = big[1][:, 3072:4096].rearrange("p (g n) -> p g n", g=GROUPS)
            eta_c, keep_c = big[2][:, 0:2048], big[2][:, 2048:4096]
            xco, yco = big[3][:, 0:2048], big[3][:, 2048:4096]

        TB, GB = 0, 1

        def prep_sync(sync):
            sync.dma_start(pk[:, :], packed_d).then_inc(sg("packed_in"), 16)
            for g in range(GROUPS):
                sync.dma_start(xres[:, g * 16:g * 16 + 16, :],
                               x_d.rearrange("(t p) c -> p t c", p=P)[:, g * 16:g * 16 + 16, :]
                               ).then_inc(sg(f"x_in{g}"), 16)

        def prep_gpsimd(pool):
            nc.gpsimd.memset(zeros[:, :], 0.0).then_inc(sg("zeros_ready"), 1)
            nc.gpsimd.memset(pow_c[:, :], -0.5).then_inc(p_step, cp.one())
            pool.wait_ge(p_step, cp.now)
            rsqrts(0, 16)
            rsqrts(16, 32)

        def prep_vector(v):
            v.sem_inc(sg("gt_free"), 1)
            v.sem_inc(sg("pre_free"), 1)
            nc.vector.memset(pre[:, :, :], 0.0).then_inc(sg("pre_zero"), 1)
            v.wait_ge(sg("packed_in"), 16)
            nc.vector.tensor_tensor(gw_n[:, :], par("gate"), par("norm_g"), ALU.mult).then_inc(sg("gw_ready"), 1)
            nc.vector.tensor_tensor(gb_n[:, :], par("gate_b"), par("norm_g"), ALU.mult).then_inc(v_step, cv.one())
            for g in range(GROUPS):
                v.wait_ge(sg(f"x_in{g}"), 16)
                with cv.loop(v, 16, 1) as t:
                    nc.vector.bn_stats(st[:, g * 16 + t, :], xres[:, g * 16 + t, :]).then_inc(v_step, cv.one())
                v.wait_ge(v_step, cv.now)
                moments(v, g * 16, g * 16 + 16)

            v.wait_ge(sg("rstd_ready"), 2)
            with cv.loop(v, GROUPS, 9) as g:
                def gate_add(b4):
                    v.wait_ge(sg("gt_done"), g * B4 + b4 + 1)
                    nc.vector.tensor_tensor(
                        gate_t[:, bass.ds(g * 16 + b4 * TPB, TPB), :],
                        bank[:, GB, :].rearrange("p (j c) -> p j c", j=TPB),
                        gb_n[:, None, :].broadcast_to([P, TPB, H]), ALU.add).then_inc(sg("gt_free"), 1)

                for b4 in range(B4):
                    v.wait_ge(sg("xn_free"), g * B4 + b4 + 1)
                    for j in range(TPB):
                        t = g * 16 + b4 * TPB + j
                        i = nc.vector.tensor_scalar(xn[:, b4 % 2, j, :], xres[:, t, :], mean[:, bass.ds(t, 1)],
                                                    rstd[:, bass.ds(t, 1)], ALU.subtract, ALU.mult)
                    i.then_inc(sg("xn_ready"), 1)
                    if b4 >= 1:
                        gate_add(b4 - 1)
                gate_add(B4 - 1)
                v.wait_ge(sg("pre_ready"), g + 1)
                for tap in range(4):
                    for kind in range(3):
                        src = pre[:, kind, tap:tap + SEQ]
                        dst = kvq[:, kind, g, :]
                        w = par("conv_w", kind * 4 + tap, kind * 4 + tap + 1)
                        if tap == 0:
                            i = nc.vector.tensor_scalar(dst, src, w, par("conv_b", kind, kind + 1), ALU.mult, ALU.add)
                        else:
                            i = nc.vector.scalar_tensor_tensor(dst, src, w, dst, ALU.mult, ALU.add)
                        if tap < 3:
                            i.then_inc(v_step, cv.one())
                    if tap < 3:
                        v.wait_ge(v_step, cv.now)
                i.then_inc(sg("pre_free"), 1)

            v.wait_ge(sg("theta_parts"), 1)
            theta = tlin
            nc.vector.scalar_tensor_tensor(theta[:, :, :], tlin[:, :, :], 0.0, tabs[:, :, :],
                                           ALU.max, ALU.add).then_inc(sg("theta_ready"), 1)
            starts = lambda a: a.rearrange("p (c t) -> p c t", t=CHUNK)[:, :, 0:1]
            flat = lambda a: a[:, :, :].rearrange("p g n -> p (g n)")
            tmp = lambda k: big[2][:, k * 1024:(k + 1) * 1024]
            v.wait_ge(sg("means"), 1)
            nc.vector.tensor_scalar(tmp(0).rearrange("p (g n) -> p g n", g=2), bank[:, 0:2, :], 0.9, 0.05, ALU.mult, ALU.add).then_inc(sg("bd_read"), 1)
            nc.vector.tensor_scalar(tmp(1).rearrange("p (g n) -> p g n", g=2), bank[:, 2:4, :], -0.1, 1.0, ALU.mult, ALU.add).then_inc(sg("bd_read"), 1)
            v.wait_ge(sg("bd_read"), 2)
            nc.vector.memset(tmp(2), 0.0).then_inc(v_step, cv.one())
            nc.vector.memset(tmp(3), 0.0).then_inc(v_step, cv.one())
            v.wait_ge(v_step, cv.now)
            nc.vector.tensor_copy(starts(tmp(2)), starts(tmp(0))).then_inc(v_step, cv.one())
            nc.vector.tensor_copy(starts(tmp(3)), starts(tmp(1))).then_inc(v_step, cv.one())
            v.wait_ge(v_step, cv.now)
            nc.vector.memset(starts(tmp(0)), 0.0).then_inc(v_step, cv.one())
            nc.vector.memset(starts(tmp(1)), 0.0).then_inc(v_step, cv.one())
            v.wait_ge(v_step, cv.now)
            nc.vector.tensor_tensor_scan(flat(e_st), tmp(0), tmp(2), 0.0, ALU.mult, ALU.add).then_inc(v_step, cv.one())
            nc.vector.tensor_tensor_scan(flat(w_st), tmp(1), tmp(3), 0.0, ALU.mult, ALU.add).then_inc(v_step, cv.one())
            v.wait_ge(v_step, cv.now)
            nc.vector.tensor_tensor_scan(flat(b_st), tmp(1), flat(e_st), 0.0, ALU.mult, ALU.add).then_inc(v_step, cv.one())
            v.wait_ge(v_step, cv.now)
            v.wait_ge(sg("means"), 2)
            nc.vector.tensor_scalar(eta_c.rearrange("p (b n) -> p b n", b=4), bank[:, 4:8, :], 0.9, 0.05, ALU.mult, ALU.add).then_inc(v_step, cv.one())
            v.wait_ge(sg("means"), 3)
            nc.vector.tensor_scalar(keep_c.rearrange("p (b n) -> p b n", b=4), bank[:, 0:4, :], -0.1, 1.0, ALU.mult, ALU.add).then_inc(v_step, cv.one())
            v.wait_ge(v_step, cv.now)
            v.sem_inc(sg("bank_free"), 1)
            nc.vector.memset(starts(eta_c), 0.0).then_inc(v_step, cv.one())
            nc.vector.memset(starts(keep_c), 0.0).then_inc(v_step, cv.one())
            v.wait_ge(sg("means"), 4)
            nc.vector.scalar_tensor_tensor(
                yco.rearrange("p (c t) -> p c t", t=CHUNK),
                bank[:, 4:8, :].rearrange("p b n -> p (b n)").rearrange("p (c t) -> p c t", t=CHUNK), 0.1,
                par("neg_i")[:, None, :].broadcast_to([P, 4 * CHUNKS, CHUNK]),
                ALU.mult, ALU.mult).then_inc(v_step, cv.one())
            v.wait_ge(v_step, cv.now)
            nc.vector.tensor_tensor_scan(xco, eta_c, yco, 0.0, ALU.mult, ALU.add).then_inc(v_step, cv.one())
            v.wait_ge(v_step, cv.now)
            nc.vector.tensor_tensor_scan(yco, keep_c, xco, 0.0, ALU.mult, ALU.add).then_inc(sg("coef_ready"), 1)

        def prep_tensor(pe):
            pe.sem_inc(sg("xn_free"), 2)
            pe.sem_inc(sg("xT_free"), 2)
            pe.wait_ge(sg("packed_in"), 16)
            pe.wait_ge(sg("gw_ready"), 1)
            with pe.Fori(0, GROUPS) as g:
                for b4 in range(B4):
                    u = g * B4 + b4
                    pe.wait_ge(sg("xn_ready"), u + 1)
                    for j in range(TPB):
                        i = nc.tensor.transpose(bank[:, TB, j * P:(j + 1) * P], xn[:, b4 % 2, j, :], ident)
                    i.then_inc(sg("xn_free"), 1)
                    pe.wait_ge(sg("xT_ready"), u + 1)
                    pe.wait_ge(sg("gt_free"), u + 1)
                    for j in range(TPB):
                        i = nc.tensor.matmul(bank[:, GB, j * H:(j + 1) * H], xT[:, b4 % 2, j * P:(j + 1) * P],
                                             gw_n[:, :], start=True, stop=True)
                    i.then_inc(sg("gt_done"), 1)
                    if b4 == 0:
                        pe.wait_ge(sg("kinds_free"), g + 1)
                    for kind in range(6):
                        i = nc.tensor.matmul(bank[D * b4:D * b4 + D, 2 + kind, :], par("proj", kind * D, kind * D + D),
                                             xT[:, b4 % 2, :], start=True, stop=True)
                    i.then_inc(sg("xT_free"), 1)
            pe.wait_ge(sg("kinds_free"), 1 + GROUPS)
            pe.wait_ge(sg("gt_free"), 1 + BATCH)
            for k, s in enumerate((sge, sga)):
                for g in range(GROUPS):
                    i = nc.tensor.matmul(bank[:, 2 * k + g, :], par("mean_bd"), s[:, g, :], start=True, stop=True)
            i.then_inc(sg("means"), 1)

            def spread(s, at):
                for b4 in range(B4):
                    for g in range(GROUPS):
                        i = nc.tensor.matmul(bank[64 * g:64 * g + 64, at + b4, :], par("mean_sel", b4 * 64, b4 * 64 + 64),
                                             s[:, g, :], start=True, stop=True)
                i.then_inc(sg("means"), 1)

            spread(sge, 4)
            pe.wait_ge(sg("bd_read"), 2)
            spread(sga, 0)
            pe.wait_ge(sg("theta_ready"), 1)
            pe.wait_ge(sg("bank_free"), 1)
            spread(tlin, 4)

        def prep_scalar(act):
            act.sem_inc(sg("kinds_free"), 1)
            act.dma_start(experts_up[:, :, :], up0_d).then_inc(sg("experts_in"), 16)
            act.dma_start(experts_down[:, :, :, :], down0_d).then_inc(sg("experts_in"), 16)
            act.wait_ge(sg("zeros_ready"), 1)
            for n in range(2):
                for h in range(HALVES):
                    act.dma_start(rows_d[n][h].rearrange("(s p) c -> p s c", p=P),
                                  zeros[:, None, :].broadcast_to([P, HALF_SLOTS, H])).then_inc(sg("zeroed"), 16)
            act.wait_ge(sg("packed_in"), 16)
            act.wait_ge(sg("pre_zero"), 1)
            with act.Fori(0, GROUPS) as g:
                for b4 in range(B4):
                    u = g * B4 + b4
                    act.wait_ge(sg("xn_free"), u + 3)
                    act.wait_ge(sg("xT_free"), u + 1)
                    nc.scalar.activation(xT[:, b4 % 2, :], bank[:, TB, :], ACT.Identity).then_inc(sg("xT_ready"), 1)
                act.wait_ge(sg("xT_free"), g * B4 + B4 + 2)
                act.wait_ge(sg("pre_free"), g + 1)
                for kind in range(3):
                    i = nc.scalar.activation(pre[:, kind, 3:3 + SEQ], bank[:, 2 + kind, :], ACT.Identity)
                i.then_inc(sg("pre_ready"), 1)
                nc.scalar.activation(sga[:, g, :], bank[:, 5, :], ACT.Sigmoid, bias=par("bias3", 0, 1))
                nc.scalar.activation(sge[:, g, :], bank[:, 6, :], ACT.Sigmoid, bias=par("bias3", 1, 2))
                nc.scalar.activation(tabs[:, g, :], bank[:, 7, :], ACT.Abs, bias=par("bias3", 2, 3))
                nc.scalar.activation(tlin[:, g, :], bank[:, 7, :], ACT.Identity,
                                     bias=par("bias3", 2, 3)).then_inc(sg("kinds_free"), 1)
            act.wait_ge(sg("kinds_free"), 1 + GROUPS)
            nc.scalar.activation(tabs[:, :, :], tabs[:, :, :], ACT.Exp, scale=-1.0).then_inc(a_step, ca.one())
            act.wait_ge(a_step, ca.now)
            nc.scalar.activation(tabs[:, :, :], tabs[:, :, :], ACT.Ln, bias=1.0).then_inc(sg("theta_parts"), 1)

        ks = carve("ks", [P, 2, GROUPS, CHUNK])
        vs = carve("vs", [P, 2, GROUPS, CHUNK])
        qx = carve("qx", [P, 2, GROUPS, B4, CHUNK])
        qa = carve("qa", [P, 2, GROUPS, CHUNK])
        qb = carve("qb", [P, 2, GROUPS, CHUNK])
        kh = carve("kh", [P, 2, P])
        vt = carve("vt", [P, P])
        de = carve("de", [P, 2, P])
        dec = carve("dec", [P, 2, 2, P])
        dexy = carve("dexy", [P, 2, 2, P])
        sq = carve("sq", [P, 2, P])
        skh = carve("skh", [P, 2, B4])
        sde = carve("sde", [P, 2, B4])
        cl = carve("cl", [P, 3, B4])
        sig = carve("sig", [P, P])
        dsilu = carve("dsilu", [P, P])
        hT = carve("hT", [P, 2, GROUPS, CHUNK])
        eT = carve("eT", [P, GROUPS, CHUNK])
        p1 = carve("p1", [P, B4, CHUNK])
        p2 = carve("p2", [P, B4, CHUNK])
        sig2 = carve("sig2", [P, GROUPS, CHUNK])
        h2 = carve("h2", [P, GROUPS, CHUNK])
        h2x = carve("h2x", [P, GROUPS, B4, CHUNK])
        h2a = carve("h2a", [P, GROUPS, CHUNK])
        h2b = carve("h2b", [P, GROUPS, CHUNK])
        wc = carve("wc", [P, GROUPS, 2, D])
        sc = carve("sc", [P, GROUPS, 2, D])
        sd = carve("sd", [P, GROUPS, 2, D])
        wx = carve("wx", [P, 2, GROUPS * 2, B4, D])
        sx = carve("sx", [P, 2, GROUPS * 2, B4, D])
        w2x = carve("w2x", [P, 2, GROUPS, P])
        ret = carve("ret", [P, GROUPS, SEQ])
        A_B, KV_B, SC_B, TR_B, PD_B, G_B, W2_B = 0, 1, 2, 3, 4, 5, 7
        y5 = yco.rearrange("p (b c t) -> p b c t", b=B4, c=CHUNKS)
        x5 = xco.rearrange("p (b c t) -> p b c t", b=B4, c=CHUNKS)
        quad_t = quad4[:, :, 0:1]

        def grp(a, g):
            return a[64 * g:64 * g + 64]

        def at(i):
            return bass.ds(i * CHUNK, CHUNK)

        def expand(dst, src):
            return nc.vector.tensor_tensor(
                dst, src[:, :, :, :].rearrange("p g k d -> p (g k) d")[:, :, None, :].broadcast_to([P, 4, B4, D]),
                quad4[:, None, :, :].broadcast_to([P, 4, B4, D]), ALU.mult)

        def chunks_on(eng, step):
            step(0, 0, True, False)
            with eng.Fori(0, (CHUNKS - 2) // 2) as r:
                step(2 * r + 1, 1, True, True)
                step(2 * r + 2, 0, True, True)
            step(CHUNKS - 1, 1, True, True)
            step(CHUNKS, 0, False, True)

        def recur_gpsimd(pool):
            pool.wait_ge(sg("coef_ready"), 1)

            def stage(i, p):
                nc.gpsimd.tensor_copy(ks[:, p], kvq[:, 0, :, at(i)])
                nc.gpsimd.tensor_copy(vs[:, p], kvq[:, 1, :, at(i)])
                for g in range(GROUPS):
                    nc.gpsimd.tensor_tensor(qx[:, p, g], kvq[:, 2, g, at(i)][:, None, :].broadcast_to([P, B4, CHUNK]),
                                            quad_t.broadcast_to([P, B4, CHUNK]), ALU.mult)
                nc.gpsimd.tensor_tensor(qa[:, p], kvq[:, 2, :, at(i)], w_st[:, :, at(i)], ALU.mult)
                nc.gpsimd.tensor_tensor(qb[:, p], kvq[:, 2, :, at(i)], b_st[:, :, at(i)],
                                        ALU.mult).then_inc(sg("staged"), 1)

            def step(i, p, chain, back):
                if back:
                    pool.wait_ge(sg("h2_ready"), i)
                    nc.gpsimd.tensor_tensor(h2a[:, :, :], h2[:, :, :], w_st[:, :, at(i - 1)], ALU.mult)
                    nc.gpsimd.tensor_tensor(h2b[:, :, :], h2[:, :, :], b_st[:, :, at(i - 1)],
                                            ALU.mult).then_inc(sg("h2ab"), 1)
                if chain:
                    pool.wait_ge(sg("norm_ready"), i + 1)
                    nc.gpsimd.tensor_tensor(cl[:, 2, :], cl[:, 1, :], pow_c[:, 0:B4], ALU.pow).then_inc(sg("clip_ready"), 1)
                    pool.wait_ge(sg("dec_ready"), i + 1)
                    nc.gpsimd.tensor_tensor(
                        dexy[:, :, 0, :].rearrange("p k (b d) -> p k b d", b=B4),
                        dec[:, p].rearrange("p k (b d) -> p k b d", b=B4),
                        x5[:, :, i, CHUNK - 1:CHUNK][:, None, :, :].broadcast_to([P, 2, B4, D]),
                        ALU.mult).then_inc(sg("dx_ready"), 1)

            stage(0, 0)

            def both(i, p, chain, back):
                if chain and not (isinstance(i, int) and i == CHUNKS - 1):
                    if back:
                        pool.wait_ge(sg("r1_done"), i)
                    stage(i + 1, 1 - p)
                step(i, p, chain, back)

            chunks_on(pool, both)

        def recur_scalar(act):
            act.wait_ge(sg("coef_ready"), 1)

            def step(i, p, chain, back):
                if chain:
                    act.wait_ge(sg("a_done"), i + 1)
                    nc.scalar.activation(sig[:, :], bank[:, A_B, 0:P], ACT.Sigmoid).then_inc(sg("sig_ready"), 1)
                    act.wait_ge(sg("kv_done"), i + 1)
                    nc.scalar.activation(kh[:, 0, :], bank[:, KV_B, 0:P], ACT.Identity)
                    nc.scalar.activation(vt[:, :], bank[:, KV_B, P:2 * P], ACT.Identity).then_inc(sg("kv_ready"), 1)
                    act.wait_ge(sg("hT_done"), i + 1)
                    nc.scalar.activation(hT[:, p], bank[:, TR_B, 0:P].rearrange("p (g t) -> p g t", g=2),
                                         ACT.Identity).then_inc(sg("hT_ready"), 1)
                if chain and back:
                    act.wait_ge(sg("w2_done"), i + 1)
                    nc.scalar.activation(w2x[:, p], bank[:, W2_B, 0:2 * P].rearrange("p (g n) -> p g n", g=2),
                                         ACT.Identity).then_inc(sg("w2_ready"), 1)
                if back:
                    act.wait_ge(sg("r1_done"), i)
                    nc.scalar.activation(sig2[:, :, :], bank[:, G_B:G_B + 2, 0:CHUNK], ACT.Sigmoid).then_inc(sg("sig2_ready"), 1)
                if chain:
                    act.wait_ge(sg("eT_done"), i + 1)
                    nc.scalar.activation(eT[:, :, :], bank[:, TR_B, P:2 * P].rearrange("p (g t) -> p g t", g=2),
                                         ACT.Identity).then_inc(sg("eT_ready"), 1)
                if back:
                    act.wait_ge(sg("r3_done"), i)
                    nc.scalar.activation(ret[:, :, at(i - 1)], bank[:, G_B:G_B + 2, CHUNK:2 * CHUNK],
                                         ACT.Identity).then_inc(sg("ret_ready"), 1)
            act.wait_ge(sg("w2_done"), 1)
            nc.scalar.activation(w2x[:, 0], bank[:, W2_B, 0:2 * P].rearrange("p (g n) -> p g n", g=2),
                                 ACT.Identity).then_inc(sg("w2_ready"), 1)
            chunks_on(act, step)

        def recur_vector(v):
            for g in range(GROUPS):
                nc.vector.tensor_copy(wc[:, g], par("mem").rearrange("p (k d) -> p k d", k=2)).then_inc(v_step, cv.one())
            nc.vector.memset(sc[:, :, :, :], 0.0).then_inc(v_step, cv.one())
            v.wait_ge(v_step, cv.now)
            v.wait_ge(sg("coef_ready"), 1)
            expand(sx[:, 0], sc)
            expand(wx[:, 0], wc).then_inc(sg("wx_ready"), 1)

            def chain_a(i, p):
                v.wait_ge(sg("sig_ready"), i + 1)
                a = bank[:, A_B, 0:P]
                v.wait_ge(sg("hT_done"), i) if not (isinstance(i, int) and i == 0) else None
                nc.vector.tensor_tensor(kh[:, 1, :], a, sig[:, :], ALU.mult).then_inc(sg("h_ready"), 1)
                v.wait_ge(sg("h_ready"), i + 1)
                nc.vector.scalar_tensor_tensor(dsilu[:, :], a, 1.0, kh[:, 1, :], ALU.add, ALU.subtract).then_inc(v_step, cv.one())
                v.wait_ge(v_step, cv.now)
                nc.vector.tensor_tensor(dsilu[:, :], dsilu[:, :], sig[:, :], ALU.mult).then_inc(v_step, cv.one())
                v.wait_ge(sg("kv_ready"), i + 1)
                nc.vector.tensor_tensor(sq[:, :, :], kh[:, :, :], kh[:, :, :], ALU.mult).then_inc(v_step, cv.one())
                v.wait_ge(v_step, cv.now)
                nc.vector.tensor_reduce(skh[:, :, :], sq[:, :, :].rearrange("p k (b d) -> p k b d", b=B4), AX,
                                        ALU.add).then_inc(v_step, cv.one())
                v.wait_ge(sg("pred_done"), i + 1)
                nc.vector.tensor_tensor(de[:, 1, :], bank[:, PD_B, 0:P], vt[:, :], ALU.subtract).then_inc(sg("e_ready"), 1)

            def back_a(i):
                v.wait_ge(sg("sig2_ready"), i)
                nc.vector.tensor_tensor(h2[:, :, :], bank[:, G_B:G_B + 2, 0:CHUNK], sig2[:, :, :],
                                        ALU.mult).then_inc(sg("h2_ready"), 1)
                v.wait_ge(sg("h2_ready"), i)
                nc.vector.tensor_tensor(h2x[:, :, :, :], h2[:, :, None, :].broadcast_to([P, GROUPS, B4, CHUNK]),
                                        quad_t[:, None, :, :].broadcast_to([P, GROUPS, B4, CHUNK]),
                                        ALU.mult).then_inc(sg("h2x_ready"), 1)

            def chain_b(i, p):
                v.wait_ge(sg("dh_done"), i + 1)
                nc.vector.tensor_tensor(de[:, 0, :], bank[:, PD_B, P:2 * P], dsilu[:, :], ALU.mult).then_inc(v_step, cv.one())
                v.wait_ge(v_step, cv.now)
                v.wait_ge(sg("e_ready"), i + 1)
                nc.vector.tensor_tensor(sq[:, :, :], de[:, :, :], de[:, :, :], ALU.mult).then_inc(v_step, cv.one())
                v.wait_ge(v_step, cv.now)
                nc.vector.tensor_reduce(sde[:, :, :], sq[:, :, :].rearrange("p k (b d) -> p k b d", b=B4), AX,
                                        ALU.add).then_inc(v_step, cv.one())
                v.wait_ge(v_step, cv.now)
                nc.vector.tensor_tensor(sde[:, :, :], sde[:, :, :], skh[:, :, :], ALU.mult).then_inc(v_step, cv.one())
                v.wait_ge(v_step, cv.now)
                nc.vector.tensor_tensor(cl[:, 0, :], sde[:, 0, :], sde[:, 1, :], ALU.add).then_inc(v_step, cv.one())
                v.wait_ge(v_step, cv.now)
                nc.vector.tensor_scalar(cl[:, 1, :], cl[:, 0, :], 25.0, None, ALU.max).then_inc(sg("norm_ready"), 1)

            def back_b(i):
                v.wait_ge(sg("s2_done"), i)
                nc.vector.tensor_tensor(p2[:, :, :], bank[:, SC_B, 0:256].rearrange("p (b t) -> p b t", b=B4),
                                        y5[:, :, i - 1, :], ALU.mult).then_inc(sg("p2_ready"), 1)

            def chain_c(i, p):
                v.wait_ge(sg("s1_done"), i + 1)
                nc.vector.tensor_tensor(p1[:, :, :], bank[:, SC_B, 0:256].rearrange("p (b t) -> p b t", b=B4),
                                        y5[:, :, i, :], ALU.mult).then_inc(sg("p1_ready"), 1)
                v.wait_ge(sg("clip_ready"), i + 1)
                nc.vector.tensor_tensor(
                    dec[:, p].rearrange("p k (b d) -> p k b d", b=B4),
                    de[:, :, :].rearrange("p k (b d) -> p k b d", b=B4),
                    cl[:, 2, :][:, None, :, None].broadcast_to([P, 2, B4, D]), ALU.mult).then_inc(sg("dec_ready"), 1)
                v.wait_ge(sg("dec_ready"), i + 1)
                nc.vector.tensor_tensor(
                    dexy[:, :, 1, :].rearrange("p k (b d) -> p k b d", b=B4),
                    dec[:, p].rearrange("p k (b d) -> p k b d", b=B4),
                    y5[:, :, i, CHUNK - 1:CHUNK][:, None, :, :].broadcast_to([P, 2, B4, D]),
                    ALU.mult).then_inc(sg("dy_ready"), 1)
                v.wait_ge(sg("g_done"), i + 1)
                last = lambda a, g: a[:, g, bass.ds(i * CHUNK + CHUNK - 1, 1)]
                fresh = lambda g, w: bank[:, G_B + g, 0:128].rearrange("p (k w d) -> p k w d", k=2, w=2)[:, :, w, :]
                for g in range(GROUPS):
                    nc.vector.scalar_tensor_tensor(sd[:, g], sc[:, g], last(b_st, g), fresh(g, 1),
                                                   ALU.mult, ALU.add).then_inc(v_step, cv.one())
                v.wait_ge(v_step, cv.now)
                for g in range(GROUPS):
                    nc.vector.scalar_tensor_tensor(wc[:, g], wc[:, g], last(w_st, g), sd[:, g],
                                                   ALU.mult, ALU.add).then_inc(v_step, cv.one())
                v.wait_ge(v_step, cv.now)
                expand(wx[:, 1 - p], wc).then_inc(sg("wx_ready"), 1)
                for g in range(GROUPS):
                    nc.vector.scalar_tensor_tensor(sc[:, g], sc[:, g], last(e_st, g), fresh(g, 0),
                                                   ALU.mult, ALU.add).then_inc(v_step, cv.one())
                v.wait_ge(v_step, cv.now)
                expand(sx[:, 1 - p], sc).then_inc(sg("sx_ready"), 1)

            def step(i, p, chain, back):
                if chain:
                    chain_a(i, p)
                if back:
                    back_a(i)
                if chain:
                    chain_b(i, p)
                if back:
                    back_b(i)
                if chain:
                    chain_c(i, p)

            step(0, 0, True, False)
            with cv.loop(v, (CHUNKS - 2) // 2, 2 * STEPS_V) as r:
                step(2 * r + 1, 1, True, True)
                step(2 * r + 2, 0, True, True)
            step(CHUNKS - 1, 1, True, True)
            step(CHUNKS, 0, False, True)

        def recur_tensor(pe):
            def flip_w2(p):
                for g in range(GROUPS):
                    i = nc.tensor.transpose(bank[:, W2_B, g * P:(g + 1) * P],
                                            wx[:, p, 2 * g + 1].rearrange("p b d -> p (b d)"), ident)
                i.then_inc(sg("w2_done"), 1)

            def w(p, g, k):
                return wx[:, p, 2 * g + k].rearrange("p b d -> p (b d)")

            def s(p, g, k):
                return sx[:, p, 2 * g + k].rearrange("p b d -> p (b d)")

            def back_sum(p, k, src, pair, a, b, col):
                for g in range(GROUPS):
                    o = bank[:, G_B + g, col:col + CHUNK]
                    nc.tensor.matmul(o, w(p, g, k), a[:, g, :], start=True, stop=False)
                    nc.tensor.matmul(o, s(p, g, k), b[:, g, :], start=False, stop=True)
                    for b4 in range(B4):
                        i = nc.tensor.matmul(bank[D * b4:D * b4 + D, G_B + g, col:col + CHUNK],
                                             grp(dec[:, p, pair, D * b4:D * b4 + D], g), grp(src[:, b4, :], g),
                                             start=False, stop=True, skip_group_check=True)
                return i

            pe.wait_ge(sg("wx_ready"), 1)
            flip_w2(0)

            def step(i, p, chain, back):
                if chain:
                    pe.wait_ge(sg("staged"), i + 1)
                    pe.wait_ge(sg("wx_ready"), i + 1)
                    for g in range(GROUPS):
                        j = nc.tensor.matmul(bank[64 * g:64 * g + 64, A_B, 0:P], ks[:, p, g, :], w(p, g, 0),
                                             start=True, stop=True)
                    j.then_inc(sg("a_done"), 1)
                    for k, src in enumerate((ks, vs)):
                        j = nc.tensor.transpose(bank[:, KV_B, k * P:(k + 1) * P],
                                                src[:, p].rearrange("p g t -> p (g t)"), ident)
                    j.then_inc(sg("kv_done"), 1)
                    if back:
                        flip_w2(p)
                if back:
                    pe.wait_ge(sg("p1_ready"), i)
                    pe.wait_ge(sg("sx_ready"), i)
                    back_sum(1 - p, 0, p1, 0, qa[:, 1 - p], qb[:, 1 - p], 0).then_inc(sg("r1_done"), 1)
                if chain:
                    pe.wait_ge(sg("h_ready"), i + 1)
                    nc.tensor.transpose(bank[:, TR_B, 0:P], kh[:, 1, :], ident).then_inc(sg("hT_done"), 1)
                    pe.wait_ge(sg("hT_ready"), i + 1)
                    for g in range(GROUPS):
                        j = nc.tensor.matmul(bank[64 * g:64 * g + 64, PD_B, 0:P], hT[:, p, g, :], w(p, g, 1),
                                             start=True, stop=True)
                    j.then_inc(sg("pred_done"), 1)
                    pe.wait_ge(sg("e_ready"), i + 1)
                    nc.tensor.transpose(bank[:, TR_B, P:2 * P], de[:, 1, :], ident).then_inc(sg("eT_done"), 1)
                if back:
                    pe.wait_ge(sg("h2x_ready"), i)
                    for g in range(GROUPS):
                        j = nc.tensor.matmul(bank[64 * g:64 * g + 64, SC_B, 0:256], hT[:, 1 - p, g, :],
                                             h2x[:, g].rearrange("p b t -> p (b t)"), start=True, stop=True)
                    j.then_inc(sg("s2_done"), 1)
                if chain:
                    pe.wait_ge(sg("eT_ready"), i + 1)
                    pe.wait_ge(sg("w2_ready"), i + 1)
                    for g in range(GROUPS):
                        j = nc.tensor.matmul(bank[64 * g:64 * g + 64, PD_B, P:2 * P], eT[:, g, :], w2x[:, p, g, :],
                                             start=True, stop=True)
                    j.then_inc(sg("dh_done"), 1)
                if back:
                    pe.wait_ge(sg("p2_ready"), i)
                    pe.wait_ge(sg("h2ab"), i)
                    back_sum(1 - p, 1, p2, 1, h2a, h2b, CHUNK).then_inc(sg("r3_done"), 1)
                if chain:
                    for g in range(GROUPS):
                        j = nc.tensor.matmul(bank[64 * g:64 * g + 64, SC_B, 0:256], ks[:, p, g, :],
                                             qx[:, p, g].rearrange("p b t -> p (b t)"), start=True, stop=True)
                    j.then_inc(sg("s1_done"), 1)
                    pe.wait_ge(sg("dx_ready"), i + 1)
                    pe.wait_ge(sg("dy_ready"), i + 1)
                    if back:
                        pe.wait_ge(sg("ret_ready"), i)
                    pe.sem_inc(sg("g_started"), 1)
                    for g in range(GROUPS):
                        for k in range(2):
                            for b4 in range(B4):
                                j = nc.tensor.matmul(
                                    bank[D * b4:D * b4 + D, G_B + g, 64 * k:64 * k + 64],
                                    grp(kh[:, k, D * b4:D * b4 + D], g), grp(dexy[:, k, :, D * b4:D * b4 + D], g),
                                    start=True, stop=True)
                    j.then_inc(sg("g_done"), 1)

            chunks_on(pe, step)

        def post_tensor(pe):
            pe.wait_ge(sg("ret_ready"), CHUNKS)
            for n in range(GROUPS * TPB):
                g, j = divmod(n, TPB)
                if n >= 2:
                    pe.wait_ge(sg("o_read"), n - 1)
                nc.tensor.matmul(bank[:, n % 2, :], ret[:, g, j * P:(j + 1) * P], par("wo"),
                                 start=True, stop=True).then_inc(sg("o_done"), 1)

        tiles = lambda a: a[:, :].rearrange("p (t c) -> p t c", t=TILES)
        o_all = tiles(big[2])
        carved[0] = 0
        o_sq = kvq[:, :, :, :].rearrange("p k g n -> p (k g) n")

        def post_scalar(act):
            o5 = o_all.rearrange("p (g b j) c -> p g b j c", g=GROUPS, b=B4)
            for n in range(GROUPS * TPB):
                g, j = divmod(n, TPB)
                act.wait_ge(sg("o_done"), n + 1)
                src = bank[:, n % 2, :].rearrange("p (b c) -> p b c", b=B4)
                nc.scalar.activation(o5[:, g, :, j, :], src, ACT.Identity)
                if n >= 2:
                    act.wait_ge(sg("sq_read"), n - 1)
                nc.scalar.activation(o_sq[:, n % 2, :], bank[:, n % 2, :], ACT.Square).then_inc(sg("o_read"), 1)

        def post_vector(v):
            s4 = st[:, :, 0].rearrange("p (g b j) -> p g b j", g=GROUPS, b=B4)
            for n in range(GROUPS * TPB):
                g, j = divmod(n, TPB)
                v.wait_ge(sg("o_read"), n + 1)
                nc.vector.tensor_reduce(s4[:, g, :, j], o_sq[:, n % 2, :].rearrange("p (b c) -> p b c", b=B4),
                                        AX, ALU.add).then_inc(sg("sq_read"), 1)
            v.wait_ge(sg("sq_read"), GROUPS * TPB)
            nc.vector.tensor_scalar(var[:, :], st[:, :, 0], 1.0 / H, 1e-6, ALU.mult, ALU.add).then_inc(sg("var_ready"), 1)
            n_asked[0] += 1
            v.wait_ge(sg("rstd_ready"), n_asked[0])

            def gated(b):
                for t in range(b * TPB, (b + 1) * TPB):
                    i = nc.vector.scalar_tensor_tensor(o_all[:, t, :], o_all[:, t, :], rstd[:, t:t + 1],
                                                       gate_t[:, t, :], ALU.mult, ALU.mult)
                vdo(v, i)
                stats(v, o_all, b)

            flow_vector(v, o_all, gated, False, lambda s, asked: route_slot_vector(v, 0, lead0, place0, s, asked), ROUTE_LAG)

        def vdo(v, i):
            i.then_inc(v_step, cv.one())
            v.wait_ge(v_step, cv.now)

        def stats(v, src, b):
            for t in range(b * TPB, (b + 1) * TPB):
                i = nc.vector.bn_stats(st[:, t, :], src[:, t, :])
            vdo(v, i)

        def flow_vector(v, src, finish, twice, follow, lag):
            branch, fresh = {}, {}
            for s in range(BATCH + 2 + lag):
                if s < BATCH:
                    finish(s)
                    branch[s] = moments(v, s * TPB, (s + 1) * TPB)
                if 0 <= s - 1 < BATCH:
                    b = s - 1
                    four = slice(b * TPB, (b + 1) * TPB)
                    v.wait_ge(sg("rstd_ready"), branch[b])
                    for t in range(b * TPB, (b + 1) * TPB):
                        i = nc.vector.tensor_scalar(src[:, t, :], src[:, t, :], mean[:, t:t + 1], rstd[:, t:t + 1],
                                                    ALU.subtract, ALU.mult)
                    vdo(v, i)
                    vdo(v, nc.vector.tensor_tensor(xres[:, four, :], xres[:, four, :], src[:, four, :], ALU.add))
                    stats(v, xres, b)
                    fresh[b] = moments(v, b * TPB, (b + 1) * TPB, twice)
                if s >= 2:
                    follow(s - 2, fresh.get(s - 2))

        def flow_gpsimd(s, twice):
            for lag, both in ((0, False), (1, twice)):
                if 0 <= s - lag < BATCH:
                    rsqrts((s - lag) * TPB, (s - lag + 1) * TPB, both)

        def post_gpsimd(pool):
            rsqrts(0, TILES)
            for s in range(BATCH + 1):
                flow_gpsimd(s, False)

        zeros = sb("zeros", [P, H])
        in_dram = lambda name: [[nc.dram_tensor(f"{name}{n}{h}", (HALF_SLOTS * P, H), F32).ap()
                                 for h in range(HALVES)] for n in range(2)]
        rows_d, made_d = in_dram("sorted_rows"), in_dram("made_rows")
        xb = carve("xb", [P, 2, SEQ])
        lg = carve("lg", [P, TILES, EXPERTS])
        pr = carve("pr", [P, TILES, EXPERTS])
        key = carve("key", [P, TILES, EXPERTS])
        hot = [carve(f"hot{k}", [P, TILES, EXPERTS]) for k in range(3)]
        t8 = carve("t8", [P, TILES, EXPERTS])
        t8b = carve("t8b", [P, TILES, EXPERTS])
        m32 = carve("m32", [P, 2, TILES])
        gain = sb("gain", [P, 2, TILES])
        csum = carve("csum", [P, EXPERTS, HALF])
        e8 = carve("e8", [P, 4, EXPERTS])
        slot8 = carve("slot8", [P, HALF_SLOTS, EXPERTS])
        slotf = carve("slotf", [P, HALF_SLOTS])
        rowf = carve("rowf", [P, 2, TILES])
        row_of = sb("row_of", [P, 2, TILES], I32)
        expert_of = sb("expert_of", [P, SLOTS], I32)
        sgs = carve("sgs", [P, 2, SEQ])
        hs = carve("hs", [P, 2, 2, SEQ])
        xr = carve("xr", [P, 2, 4, H])
        xT2 = carve("xT2", [P, 2, P])
        sgb = carve("sgb", [P, 2, MID])
        hb = carve("hb", [P, 2, MID])
        hTb = carve("hTb", [P, 2, MID])
        yb = carve("yb", [P, 2, 4, H])
        rows = tiles(big[0])
        xt_all = big[1][:, :]
        T0, L0B = 0, 2
        ROUTE_LAG = 2
        RANK_AT = BATCH // HALVES - 1 + ROUTE_LAG
        rows_of = [rows, tiles(big[2])]

        def turned(n, b):
            return xt_all[:, b * SEQ:(b + 1) * SEQ] if n == 0 else xb[:, b % 2]

        def route_slot_vector(v, n, lead, place, s, asked):
            if s < BATCH:
                v.wait_ge(sg("rstd_ready"), asked)
                lead(s)
            if s >= ROUTE_LAG:
                b = s - ROUTE_LAG
                v.wait_ge(sg("lg_done"), n * BATCH + b + 1)
                nc.vector.tensor_copy(lg[:, b * TPB:(b + 1) * TPB, :],
                                      bank[:, L0B + b % 2, 0:TPB * EXPERTS].rearrange("p (j e) -> p j e", j=TPB)
                                      ).then_inc(sg("lg_out"), 1)
                if (b + 1) % (BATCH // HALVES) == 0:
                    v.wait_ge(sg("lg_out"), n * BATCH + b + 1)
                    place(v, b * HALVES // BATCH)

        def route_scalar(act, n, half):
            for b in range(BATCH):
                act.wait_ge(sg("xa_turned"), n * BATCH + b + 1)
                if n == 1 and b >= 2:
                    act.wait_ge(sg("lg_done"), n * BATCH + b - 1)
                nc.scalar.activation(turned(n, b), bank[:, T0 + b % 2, :], ACT.Identity).then_inc(sg("xb_ready"), 1)
                if b == RANK_AT:
                    half(0)
            half(1)

        def route_tensor(pe, n):
            pe.wait_ge(sg("o_read"), GROUPS * TPB)

            def rank(h):
                pe.wait_ge(sg("hot_ready"), n * HALVES + h + 1)
                for k, w in enumerate(("before", "ones")):
                    i = nc.tensor.matmul(bank[:, 6 + k, h * HALF * EXPERTS:(h + 1) * HALF * EXPERTS], par(w),
                                         hot[2][:, h * HALF:(h + 1) * HALF, :].rearrange("p t e -> p (t e)"),
                                         start=True, stop=True)
                i.then_inc(sg("ranks"), 1)

            for s in range(BATCH + 1):
                if s < BATCH:
                    pe.wait_ge(sg("xa_ready"), n * BATCH + s + 1)
                    if s >= 2:
                        pe.wait_ge(sg("xb_ready"), n * BATCH + s - 1)
                    for j in range(TPB):
                        i = nc.tensor.transpose(bank[:, T0 + s % 2, j * P:(j + 1) * P], rows_of[n][:, s * TPB + j, :], ident)
                    i.then_inc(sg("xa_turned"), 1)
                if s >= 1:
                    b = s - 1
                    pe.wait_ge(sg("xb_ready"), n * BATCH + b + 1)
                    if b >= 2:
                        pe.wait_ge(sg("lg_out"), n * BATCH + b - 1)
                    for j in range(TPB):
                        i = nc.tensor.matmul(bank[:, L0B + b % 2, j * EXPERTS:(j + 1) * EXPERTS],
                                             turned(n, b)[:, j * P:(j + 1) * P], par(f"route{n}"), start=True, stop=True)
                    i.then_inc(sg("lg_done"), 1)
                if s == RANK_AT:
                    rank(0)
            rank(1)

        def half_of(h):
            tl = slice(h * HALF, (h + 1) * HALF)
            return tl, (lambda a: a[:, tl, :]), (lambda a: a[:, tl, None].broadcast_to([P, HALF, EXPERTS]))

        def choose(v, dst, h):
            tl, of, wide = half_of(h)
            vdo(v, nc.vector.tensor_reduce(m32[:, 0, tl], of(key), AX, ALU.max))
            vdo(v, nc.vector.tensor_tensor(of(t8), of(key), wide(m32[:, 0]), ALU.is_equal))
            vdo(v, nc.vector.tensor_tensor(of(t8), of(t8), par("rank8")[:, None, :].broadcast_to([P, HALF, EXPERTS]),
                                           ALU.mult))
            vdo(v, nc.vector.tensor_reduce(m32[:, 0, tl], of(t8), AX, ALU.max))
            vdo(v, nc.vector.tensor_tensor(of(dst), of(t8), wide(m32[:, 0]), ALU.is_equal))

        def place_vector(v, n, h):
            tl, of, wide = half_of(h)
            choose(v, hot[0], h)
            vdo(v, nc.vector.scalar_tensor_tensor(of(key), of(hot[0]), -3.0e38, of(key), ALU.mult, ALU.add))
            choose(v, hot[1], h)
            nc.vector.tensor_tensor(of(hot[2]), of(hot[0]), of(hot[1]), ALU.add).then_inc(sg("hot_ready"), 1)
            for k in range(2):
                vdo(v, nc.vector.tensor_tensor(of(t8), of(hot[k]), of(pr), ALU.mult))
                vdo(v, nc.vector.tensor_reduce(gain[:, k, tl], of(t8), AX, ALU.add))
            v.wait_ge(sg("ranks"), n * HALVES + h + 1)
            cols = slice(h * HALF * EXPERTS, (h + 1) * HALF * EXPERTS)
            before = bank[:, 6, cols].rearrange("p (t e) -> p t e", e=EXPERTS)
            total = bank[:, 7, cols].rearrange("p (t e) -> p t e", e=EXPERTS)
            for e in range(EXPERTS):
                i = nc.vector.tensor_tensor_scan(csum[:, e, :], par("ones", 0, HALF), total[:, :, e], 0.0,
                                                 ALU.mult, ALU.add)
            vdo(v, i)
            c8 = of(t8).rearrange("p t e -> p (t e)").rearrange("p (e t) -> p e t", e=EXPERTS)
            vdo(v, nc.vector.tensor_tensor(c8, csum[:, :, HALF - 1:HALF].broadcast_to([P, EXPERTS, HALF]),
                                           par("edge", 0, HALF)[:, None, :].broadcast_to([P, EXPERTS, HALF]), ALU.is_gt))
            vdo(v, nc.vector.tensor_reduce(e8[:, 0, :], c8, AX, ALU.add))
            vdo(v, nc.vector.tensor_tensor_scan(e8[:, 1, :], par("ones", 0, EXPERTS), e8[:, 0, :], 0.0,
                                                ALU.mult, ALU.add))
            vdo(v, nc.vector.tensor_tensor(e8[:, 2, :], e8[:, 1, :], e8[:, 0, :], ALU.subtract))
            vdo(v, nc.vector.tensor_scalar(e8[:, 3, :], e8[:, 2, :], float(P), None, ALU.mult))
            vdo(v, nc.vector.tensor_tensor(of(t8b), csum[:, :, :].rearrange("p e t -> p t e"), total, ALU.subtract))
            vdo(v, nc.vector.tensor_tensor(of(t8b), of(t8b), before, ALU.add))
            vdo(v, nc.vector.tensor_tensor(of(t8b), of(t8b), e8[:, 3, :][:, None, :].broadcast_to([P, HALF, EXPERTS]),
                                           ALU.add))
            for k in range(2):
                vdo(v, nc.vector.tensor_tensor(of(t8), of(hot[k]), of(t8b), ALU.mult))
                vdo(v, nc.vector.tensor_reduce(rowf[:, k, tl], of(t8), AX, ALU.add))
            nc.vector.tensor_copy(row_of[:, :, tl], rowf[:, :, tl]).then_inc(sg("rows_ready"), 1)
            vdo(v, nc.vector.tensor_tensor(slot8[:, :, :], par("slot")[:, :, None].broadcast_to([P, HALF_SLOTS, EXPERTS]),
                                           e8[:, 1, :][:, None, :].broadcast_to([P, HALF_SLOTS, EXPERTS]), ALU.is_ge))
            vdo(v, nc.vector.tensor_reduce(slotf[:, :], slot8[:, :, :], AX, ALU.add))
            vdo(v, nc.vector.tensor_scalar(slotf[:, :], slotf[:, :], float(EXPERTS - 1), None, ALU.min))
            nc.vector.tensor_copy(expert_of[:, h * HALF_SLOTS:(h + 1) * HALF_SLOTS], slotf[:, :]
                                  ).then_inc(sg("experts_ready"), 1)

        def scatter_gpsimd(pool, n, src):
            pool.wait_ge(sg("zeroed"), 16 * 2 * HALVES)
            for h in range(HALVES):
                pool.wait_ge(sg("rows_ready"), n * HALVES + h + 1)
                for t in range(h * HALF, (h + 1) * HALF):
                    if n == 1 and t % TPB == 0:
                        for k in range(2):
                            pool.wait_ge(sg(f"xe{k}_ready"), t // TPB + 1)
                    for k in range(2):
                        nc.gpsimd.indirect_dma_start(
                            rows_d[n][h][:, :], bass.IndirectOffsetOnAxis(ap=row_of[:, k, t:t + 1], axis=0),
                            src[k][:, t, :], None).then_inc(sg(f"sorted{h}"), 16)

        def gather_gpsimd(pool, n, dst, flow):
            def gather(h, t):
                for k in range(2):
                    nc.gpsimd.indirect_dma_start(
                        dst[k][:, t, :], None, made_d[n][h][:, :],
                        bass.IndirectOffsetOnAxis(ap=row_of[:, k, t:t + 1], axis=0)
                    ).then_inc(sg(f"back{t // TPB}"), 16)

            for h in range(HALVES):
                for q in range(2):
                    pool.wait_ge(sg(f"made{q}"), 16 * (HALF_SLOTS // 8) * (n * HALVES + h + 1))
                for t in range(h * HALF, (h + 1) * HALF):
                    gather(h, t)
                    if h == 1 and t % 2 == 1:
                        flow((t - HALF) // 2)
            flow(BATCH)

        def shared_tensor(pe):
            pe.wait_ge(sg("experts_in"), 32)

            def up(b):
                pe.wait_ge(sg("hs_ready"), b + 1)
                for c in range(4):
                    i = nc.tensor.matmul(bank[:, c, :], experts_up[:, EXPERTS, c * P:(c + 1) * P],
                                         xt_all[:, bass.ds(b * SEQ, SEQ)], start=True, stop=True)
                i.then_inc(sg("su_done"), 1)

            def down(b, p):
                pe.wait_ge(sg("hs_ready"), b + 2)
                pe.wait_ge(sg("acc_ready"), b + 1)
                for j in range(TPB):
                    for m in range(2):
                        i = nc.tensor.matmul(bank[:, 4 + p, j * P:(j + 1) * P], hs[:, p, m, j * P:(j + 1) * P],
                                             experts_down[:, EXPERTS, m, :], start=(m == 0), stop=(m == 1))
                i.then_inc(sg("sd_done"), 1)

            up(0)
            with pe.Fori(0, (BATCH - 2) // 2) as r:
                up(2 * r + 1)
                down(2 * r, 0)
                up(2 * r + 2)
                down(2 * r + 1, 1)
            up(BATCH - 1)
            down(BATCH - 2, 0)
            down(BATCH - 1, 1)

        def shared_scalar(act):
            act.sem_inc(sg("acc_ready"), 2)
            silu(act, 0)
            with act.Fori(0, (BATCH - 2) // 2) as r:
                silu(act, 2 * r + 1)
                out_shared(act, 2 * r, 0)
                silu(act, 2 * r + 2)
                out_shared(act, 2 * r + 1, 1)
            silu(act, BATCH - 1)
            out_shared(act, BATCH - 2, 0)
            out_shared(act, BATCH - 1, 1)

        def silu(act, b):
            act.wait_ge(sg("su_done"), b + 1)
            act.wait_ge(sg("hs_ready"), b + 1)
            nc.scalar.activation(sgs[:, :, :], bank[:, 0:2, :], ACT.Silu).then_inc(sg("sgs_ready"), 1)

        def out_shared(act, b, p):
            act.wait_ge(sg("sd_done"), b + 1)
            nc.scalar.activation(o_all[:, bass.ds(b * TPB, TPB), :],
                                 bank[:, 4 + p, :].rearrange("p (j c) -> p j c", j=TPB), ACT.Identity
                                 ).then_inc(sg("acc_ready"), 1)

        def shared_vector(v):
            v.sem_inc(sg("hs_ready"), 1)
            with v.Fori(0, BATCH // 2) as r:
                for p in range(2):
                    b = 2 * r + p
                    v.wait_ge(sg("sgs_ready"), b + 1)
                    v.wait_ge(sg("acc_ready"), b + 1)
                    nc.vector.tensor_tensor(hs[:, p], sgs[:, :, :], bank[:, 2:4, :], ALU.mult).then_inc(sg("hs_ready"), 1)

        LAG = 3
        XT, GU, HT, YB = 0, 2, 4, 6

        def tiles_on(eng, slot):
            for m in range(8):
                slot(m, m, 0)
            with eng.Fori(1, SLOTS // 8) as r:
                for m in range(8):
                    slot(r * 8 + m, m, r)
            for m in range(LAG):
                slot(SLOTS + m, m, SLOTS // 8)

        def has(s, lag):
            return not isinstance(s, int) or 0 <= s - lag < SLOTS

        def need(eng, name, value, base=0):
            if not isinstance(value, int) or value > 0:
                eng.wait_ge(sg(name), base + value)

        def experts_tensor(pe, n):
            at0 = n * SLOTS
            dma0 = n * 16 * (SLOTS // 8)
            pe.wait_ge(sg("experts_ready"), HALVES * (n + 1))
            pe.wait_ge(sg("experts_in"), 32 * (n + 1))

            def expert(tile):
                return pe.value_load(expert_of[0:1, bass.ds(tile, 1)], min_val=0, max_val=EXPERTS - 1)

            loaded = {}

            def slot(s, m, r):
                if m == 0:
                    loaded.clear()
                    if has(s, 1) and has(s, 3):
                        loaded[-1] = expert(s - 1)
                if has(s, 0):
                    if m % 4 == 0:
                        pe.wait_ge(sg(f"rows_in{m // 4}"), dma0 + (r + 1) * 16)
                    nc.tensor.transpose(bank[:, XT + m % 2, 0:P], xr[:, m // 4, m % 4, :], ident).then_inc(sg("x_turned"), 1)
                if has(s, 1):
                    o = (m - 1) % 2
                    e = loaded[m - 1]
                    need(pe, "xT_in", s, at0)
                    nc.tensor.matmul(bank[:, GU + o, :], xT2[:, o, :], experts_up[:, e, :], start=True,
                                     stop=True).then_inc(sg("gu_done"), 1)
                if has(s, 0) and m < 7:
                    loaded[m] = expert(s)
                if has(s, 3) and m - 3 not in loaded:
                    loaded[m - 3] = expert(s - 3)
                if has(s, 2):
                    o = m % 2
                    need(pe, "hb_ready", s - 1, at0)
                    for c in range(2):
                        i = nc.tensor.transpose(bank[:, HT + o, c * P:(c + 1) * P], hb[:, o, c * P:(c + 1) * P], ident)
                    i.then_inc(sg("h_turned"), 1)
                if has(s, 3):
                    o = (m - 3) % 2
                    e = loaded[m - 3]
                    need(pe, "hT_in", s - 2, at0)
                    need(pe, "y_out", s - 4, at0)
                    for c in range(2):
                        i = nc.tensor.matmul(bank[:, YB + o, 0:H], hTb[:, o, c * P:(c + 1) * P], experts_down[:, e, c, :],
                                             start=(c == 0), stop=(c == 1))
                    i.then_inc(sg("y_done"), 1)

            tiles_on(pe, slot)

        def experts_scalar(act, n):
            at0 = n * SLOTS
            dma0 = n * 16 * (SLOTS // 8)

            def slot(s, m, r):
                if has(s, 0):
                    need(act, "x_turned", s + 1, at0)
                    need(act, "gu_done", s - 1, at0)
                    nc.scalar.activation(xT2[:, m % 2, :], bank[:, XT + m % 2, 0:P], ACT.Identity).then_inc(sg("xT_in"), 1)
                if has(s, 1):
                    o = (m - 1) % 2
                    need(act, "gu_done", s, at0)
                    need(act, "hb_ready", s - 2, at0)
                    nc.scalar.activation(sgb[:, o, :], bank[:, GU + o, 0:MID], ACT.Silu).then_inc(sg("silu_ready"), 1)
                if has(s, 2):
                    o = m % 2
                    need(act, "h_turned", s - 1, at0)
                    need(act, "y_done", s - 3, at0)
                    nc.scalar.activation(hTb[:, o, :], bank[:, HT + o, 0:MID], ACT.Identity).then_inc(sg("hT_in"), 1)

            tiles_on(act, slot)

        def experts_vector(v, n):
            at0 = n * SLOTS
            dma0 = n * 16 * (SLOTS // 8)

            def slot(s, m, r):
                if has(s, 1):
                    o = (m - 1) % 2
                    need(v, "silu_ready", s, at0)
                    need(v, "h_turned", s - 2, at0)
                    nc.vector.tensor_tensor(hb[:, o, :], sgb[:, o, :], bank[:, GU + o, MID:2 * MID],
                                            ALU.mult).then_inc(sg("hb_ready"), 1)
                if has(s, 3):
                    o = (m - 3) % 2
                    m4 = (m - 3) % 8
                    need(v, "y_done", s - 2, at0)
                    if m4 % 4 == 0 and not (isinstance(r, int) and r == 0):
                        v.wait_ge(sg(f"made{m4 // 4}"), dma0 + r * 16)
                    nc.vector.tensor_copy(yb[:, m4 // 4, m4 % 4, :], bank[:, YB + o, 0:H]).then_inc(sg("y_out"), 1)

            tiles_on(v, slot)

        def experts_sync(sync, n):
            at0 = n * SLOTS
            four = lambda d, k: d.rearrange("(a j p) c -> p a j c", j=4, p=P)[:, k]
            FOURS = HALF_SLOTS // 4

            def load(h, k, o):
                sync.dma_start(xr[:, o], four(rows_d[n][h], k)).then_inc(sg(f"rows_in{o}"), 16)

            def store(h, k, o):
                sync.wait_ge(sg("y_out"), at0 + h * HALF_SLOTS + 4 * k + 4)
                sync.dma_start(four(made_d[n][h], k), yb[:, o]).then_inc(sg(f"made{o}"), 16)

            def sorted_rows(h):
                sync.wait_ge(sg(f"sorted{h}"), 16 * 2 * HALF * (n + 1))

            sorted_rows(0)
            load(0, 0, 0)
            load(0, 1, 1)
            for h in range(HALVES):
                with sync.Fori(0, FOURS // 2 - 1) as r:
                    for o in range(2):
                        k = 2 * r + o
                        sync.wait_ge(sg("x_turned"), at0 + h * HALF_SLOTS + 4 * k + 4)
                        load(h, k + 2, o)
                        store(h, k, o)
                if h == 0:
                    sorted_rows(1)
                for o in range(2):
                    k = FOURS - 2 + o
                    if h == 0:
                        sync.wait_ge(sg("x_turned"), at0 + 4 * k + 4)
                        load(1, o, o)
                    store(h, k, o)

        def lead0(b):
            for t in range(b * TPB, (b + 1) * TPB):
                i = nc.vector.tensor_scalar(rows[:, t, :], xres[:, t, :], mean[:, t:t + 1], rstd[:, t:t + 1],
                                            ALU.subtract, ALU.mult)
            i.then_inc(sg("xa_ready"), 1)

        def place0(v, h):
            tl, of, _ = half_of(h)
            vdo(v, nc.vector.tensor_tensor(of(key), of(lg), par("beta0")[:, None, :].broadcast_to([P, HALF, EXPERTS]),
                                           ALU.add))
            v.wait_ge(sg("pr_ready"), h + 1)
            place_vector(v, 0, h)

        def moe0_vector(v):
            shared_vector(v)
            experts_vector(v, 0)
            v.wait_ge(sg("acc_ready"), 2 + BATCH)

            def combine(b):
                v.wait_ge(sg(f"back{b}"), 16 * 2 * TPB)
                for k in range(2):
                    for t in range(b * TPB, (b + 1) * TPB):
                        i = nc.vector.scalar_tensor_tensor(o_all[:, t, :], got[k][:, t, :], gain[:, k, t:t + 1],
                                                           o_all[:, t, :], ALU.mult, ALU.add)
                    vdo(v, i)
                stats(v, o_all, b)

            flow_vector(v, o_all, combine, True, lambda s, asked: ssm_slot_vector(v, s, asked), SSM_LAG)

        got = [tiles(big[0]), tiles(big[1])]

        def moe0_scalar(act):
            def half(h):
                tl, of, _ = half_of(h)
                act.wait_ge(sg("lg_out"), (h + 1) * BATCH // HALVES)
                nc.scalar.activation(of(pr), of(lg), ACT.Sigmoid).then_inc(sg("pr_ready"), 1)

            route_scalar(act, 0, half)
            shared_scalar(act)
            experts_scalar(act, 0)

        def moe0_tensor(pe):
            route_tensor(pe, 0)
            shared_tensor(pe)
            experts_tensor(pe, 0)

        def moe0_gpsimd(pool):
            scatter_gpsimd(pool, 0, [rows, rows])

            gather_gpsimd(pool, 0, got, lambda s: flow_gpsimd(s, True))

        dt, xc, sz = big[0], big[1], big[2]
        f_res = tiles(big[3])
        end_of_moe = carved[0]
        carved[0] = 0
        xf = carve("xf", [P, 2, TPB, H])
        xfT = carve("xfT", [P, 2, SEQ])
        xxp = carve("xxp", [P, 2, SEQ + 2])
        cvd = carve("cvd", [P, 2, SEQ])
        bcr = carve("bcr", [P, 2, SEQ])
        bch = carve("bch", [P, 2, SEQ], BF16)
        bcm = carve("bcm", [P, 2, SEQ], BF16)
        bc3 = carve("bc3", [P, TOKENS], BF16)
        pick = carve("pick", [P, 2 * STATE, P], BF16)
        neg_a = carve("neg_a", [P, 2, STATE])
        da = carve("da", [P, 2, SEQ])
        db = carve("db", [P, 4, SEQ])
        sta = carve("sta", [P, 2, SEQ])
        cs = carve("cs", [P, 2, SEQ])
        yc = carve("yc", [P, 4, SEQ])
        yf = carve("yf", [P, 2, SEQ])
        lnx = carve("lnx", [P, TPB, H])
        ROWS = 3 * 2 * STATE

        def at_b(a, b):
            return a[:, bass.ds(b * SEQ, SEQ)]

        SSM_LAG = 2

        def ssm_slots(eng, slot):
            slot(0, 0)
            slot(1, 1)
            with eng.Fori(1, BATCH // 2) as r:
                slot(2 * r, 0)
                slot(2 * r + 1, 1)
            for s in range(SSM_LAG):
                slot(BATCH + s, s % 2)

        def in_batch(s, lag):
            return not isinstance(s, int) or 0 <= s - lag < BATCH

        def ssm_start(v):
            nc.vector.memset(xxp[:, :, 0:SEQ + 2], 0.0).then_inc(sg("xxp_zero"), 1)
            nc.vector.tensor_copy(pick[0:ROWS], par("pick")[0:ROWS, :, None].broadcast_to([ROWS, 2 * STATE, P])
                                  ).then_inc(sg("pick_ready"), 1)
            v.sem_inc(sg("cv_free"), 2)

        def ssm_slot_vector(v, s, asked):
            if s == 0:
                ssm_start(v)
            if in_batch(s, 0):
                v.wait_ge(sg("rstd_ready"), asked)
                v.wait_ge(sg("f_turned"), s + 1)
                for k in range(TPB):
                    t = s * TPB + k
                    i = nc.vector.tensor_scalar(xf[:, s % 2, k, :], xres[:, t, :], mean[:, t:t + 1],
                                                rstd2[:, t:t + 1], ALU.subtract, ALU.mult)
                i.then_inc(sg("f_rows"), 1)
            if in_batch(s, 2):
                b, p = s - 2, s % 2
                v.wait_ge(sg("bc_first"), b + 1)
                nc.vector.tensor_tensor(bcr[0:ROWS, p], bank[0:ROWS, 7, :], bch[0:ROWS, p], ALU.subtract).then_inc(sg("bc_rest"), 1)
            if in_batch(s, 1):
                b, p = s - 1, (s - 1) % 2
                v.wait_ge(sg("xx_ready"), b + 1)
                v.wait_ge(sg("xc_ready"), b + 1)
                w = lambda k: par("sconv", k, k + 1)
                vdo(v, nc.vector.tensor_scalar(cvd[:, p], xxp[:, p, 0:SEQ], w(0), None, ALU.mult))
                vdo(v, nc.vector.scalar_tensor_tensor(cvd[:, p], xxp[:, p, 1:SEQ + 1], w(1), cvd[:, p], ALU.mult, ALU.add))
                nc.vector.scalar_tensor_tensor(cvd[:, p], xxp[:, p, 2:SEQ + 2], w(2), cvd[:, p],
                                               ALU.mult, ALU.add).then_inc(sg("cv_done"), 1)
            if in_batch(s, 2):
                b, p = s - 2, s % 2
                v.wait_ge(sg("bc_second"), b + 1)
                nc.vector.tensor_tensor(at_b(bc3, b)[64:ROWS], bcr[64:ROWS, p], bcm[64:ROWS, p], ALU.subtract).then_inc(sg("bc_third"), 1)

        def ssm_prep_vector(v):
            v.wait_ge(sg("dt_parts"), 2)
            nc.vector.scalar_tensor_tensor(dt[:, :], dt[:, :], 0.0, big[3][:, :], ALU.max, ALU.add).then_inc(sg("dt_ready"), 1)
            nc.vector.tensor_scalar(neg_a[:, 1, :], neg_a[:, 0, :], -1.0, None, ALU.mult).then_inc(sg("dt_ready"), 1)

        def ssm_prep_tensor(pe):
            pe.sem_inc(sg("f_turned"), 2)

            def head(b, p):
                pe.wait_ge(sg("f_rows"), b + 1)
                for j in range(TPB):
                    i = nc.tensor.transpose(bank[:, p, j * P:(j + 1) * P], xf[:, p, j, :], ident)
                i.then_inc(sg("f_turned"), 1)
                pe.wait_ge(sg("fT_ready"), b + 1)
                pe.wait_ge(sg("z_ready"), b + 1)
                nc.tensor.matmul(bank[:, 2 + p, :], par("w_in", 0, H), xfT[:, p], start=True, stop=True)
                nc.tensor.matmul(bank[:, 4 + p, :], par("w_in", H, 2 * H), xfT[:, p], start=True,
                                 stop=True).then_inc(sg("xz_done"), 1)

            def tail(b, p):
                pe.wait_ge(sg("xc_ready"), b + 3)
                pe.wait_ge(sg("bc_read"), b + 1)
                nc.tensor.matmul(bank[:, 6, :], par("w_dt"), at_b(xc, b), start=True, stop=True)
                nc.tensor.matmul(bank[0:ROWS, 7, :], par("w_bc"), at_b(xc, b), start=True,
                                 stop=True).then_inc(sg("dtbc_done"), 1)

            def slot(s, p):
                if in_batch(s, 0):
                    head(s, p)
                if in_batch(s, 1):
                    tail(s - 1, 1 - p)

            ssm_slots(pe, slot)

        def ssm_prep_scalar(act):
            act.sem_inc(sg("z_ready"), 2)
            act.sem_inc(sg("xz_free"), 2)
            act.sem_inc(sg("xc_ready"), 2)
            act.sem_inc(sg("bc_read"), 1)
            act.wait_ge(sg("xxp_zero"), 1)

            def slot(s, p):
                if in_batch(s, 2):
                    b = s - 2
                    act.wait_ge(sg("dtbc_done"), b + 1)
                    act.sem_inc(sg("act_go"), 1)
                    nc.scalar.activation(at_b(bc3, b)[0:32], bank[0:32, 7, :], ACT.Identity)
                    nc.scalar.activation(bch[0:ROWS, p], bank[0:ROWS, 7, :], ACT.Identity).then_inc(sg("bc_first"), 1)
                if in_batch(s, 0):
                    act.wait_ge(sg("f_turned"), s + 3)
                    act.wait_ge(sg("xz_free"), s + 1)
                    nc.scalar.activation(xfT[:, p], bank[:, p, :], ACT.Identity, bias=par("beta"),
                                         scale=par("gamma")).then_inc(sg("fT_ready"), 1)
                if in_batch(s, 2):
                    b = s - 2
                    nc.scalar.activation(at_b(big[3], b), bank[:, 6, :], ACT.Abs, bias=par("b_dt"))
                    nc.scalar.activation(at_b(dt, b), bank[:, 6, :], ACT.Identity, bias=par("b_dt"))
                    act.wait_ge(sg("bc_rest"), b + 1)
                    act.sem_inc(sg("bc_read"), 1)
                    nc.scalar.activation(at_b(bc3, b)[32:64], bcr[32:64, p], ACT.Identity)
                    nc.scalar.activation(bcm[64:ROWS, p], bcr[64:ROWS, p], ACT.Identity).then_inc(sg("bc_second"), 1)
                if in_batch(s, 1):
                    b = s - 1
                    act.wait_ge(sg("cv_done"), b + 1)
                    act.sem_inc(sg("cv_free"), 1)
                    nc.scalar.activation(at_b(xc, b), cvd[:, 1 - p], ACT.Silu).then_inc(sg("xc_ready"), 1)
                if in_batch(s, 0):
                    act.wait_ge(sg("xz_done"), s + 1)
                    act.sem_inc(sg("xz_free"), 1)
                    act.wait_ge(sg("cv_free"), s + 1)
                    nc.scalar.activation(xxp[:, p, 1:SEQ + 1], bank[:, 2 + p, :], ACT.Identity).then_inc(sg("xx_ready"), 1)
                    nc.scalar.activation(at_b(sz, s), bank[:, 4 + p, :], ACT.Silu).then_inc(sg("z_ready"), 1)

            ssm_slots(act, slot)
            act.wait_ge(sg("bc_second"), BATCH)
            nc.scalar.activation(big[3][:, :], big[3][:, :], ACT.Exp, scale=-1.0).then_inc(a_step, ca.one())
            nc.scalar.activation(neg_a[:, 0, :], par("a_log"), ACT.Exp).then_inc(sg("dt_parts"), 1)
            act.wait_ge(a_step, ca.now)
            nc.scalar.activation(big[3][:, :], big[3][:, :], ACT.Ln, bias=1.0).then_inc(sg("dt_parts"), 1)

        BB, CB, Y_B, O_B = 0, 2, 4, 5

        Y_LAG = 3

        def batches_on(eng, batch):
            batch(0, False)
            with eng.Fori(1, BATCH) as b:
                batch(b, True)

        def scan_vector(v):
            v.wait_ge(sg("dt_ready"), 2)

            def scan(u, s):
                p = s % 2
                v.wait_ge(sg("da_ready"), u + 1)
                v.wait_ge(sg("db_ready"), u + 1)
                need(v, "yc_ready", u - 1)
                nc.vector.tensor_tensor_scan(sta[:, p], da[:, p], db[:, s % 4], 0.0, ALU.mult, ALU.add).then_inc(sg("state_ready"), 1)

            def final(b):
                v.wait_ge(sg("y_summed"), 16 * b + 16)
                nc.vector.scalar_tensor_tensor(yf[:, 0], at_b(xc, b), par("skip_d"), bank[:, Y_B, :],
                                               ALU.mult, ALU.add).then_inc(sg("y_read"), 1)
                v.wait_ge(sg("y_read"), b + 1)
                nc.vector.tensor_tensor(yf[:, 1], yf[:, 0], at_b(sz, b), ALU.mult).then_inc(sg("yf_ready"), 1)

            def result(b):
                for k in range(TPB):
                    t = b * TPB + k
                    i = nc.vector.tensor_scalar(lnx[:, k, :], xres[:, t, :], mean[:, bass.ds(t, 1)],
                                                rstd[:, bass.ds(t, 1)], ALU.subtract, ALU.mult)
                i.then_inc(sg("lnx"), 1)
                v.wait_ge(sg("lnx"), b + 1)
                v.wait_ge(sg("out_done_f"), b + 1)
                nc.vector.tensor_tensor(f_res[:, bass.ds(b * TPB, TPB), :], lnx[:, :, :],
                                        bank[:, O_B, :].rearrange("p (k c) -> p k c", k=TPB), ALU.add).then_inc(sg("res_ready"), 1)
                v.wait_ge(sg("res_ready"), b + 1)
                for k in range(TPB):
                    i = nc.vector.bn_stats(st[:, b * TPB + k, :], f_res[:, b * TPB + k, :])
                i.then_inc(sg("f_stats"), 1)

            def batch(b, back):
                for s in range(STATE):
                    u = b * STATE + s
                    if back and s == Y_LAG:
                        final(b - 1)
                    if back and s == 6:
                        result(b - 1)
                    v.wait_ge(sg("b_done"), u + 1)
                    need(v, "state_ready", u - 3)
                    nc.vector.tensor_tensor(db[:, s % 4], at_b(dt, b), bank[:, BB + s % 2, :], ALU.mult).then_inc(sg("db_ready"), 1)
                    if s > 0 or back:
                        scan(u - 1, (s - 1) % STATE)

            batches_on(v, batch)
            scan(BATCH * STATE - 1, STATE - 1)
            final(BATCH - 1)
            result(BATCH - 1)
            v.wait_ge(sg("f_stats"), BATCH)
            flow_vector(v, f_res, lambda b: None, True,
                        lambda s, asked: route_slot_vector(v, 1, lead1, place1, s, asked), ROUTE_LAG)

        def scan_scalar(act):
            act.wait_ge(sg("dt_ready"), 2)

            def batch(b, back):
                for s in range(STATE):
                    u = b * STATE + s
                    need(act, "state_ready", u - 1)
                    act.sem_inc(sg("act_go"), 1)
                    nc.scalar.activation(da[:, s % 2], at_b(dt, b), ACT.Exp, scale=neg_a[:, 1, s:s + 1]).then_inc(sg("da_ready"), 1)
                    act.wait_ge(sg("c_done"), u + 1)
                    need(act, "yc_ready", u - 1)
                    nc.scalar.activation(cs[:, s % 2], bank[:, CB + s % 2, :], ACT.Identity).then_inc(sg("cs_ready"), 1)

            batches_on(act, batch)

        def scan_gpsimd(pool):
            def batch(b, back):
                for s in range(STATE):
                    u = b * STATE + s
                    pool.wait_ge(sg("state_ready"), u + 1)
                    pool.wait_ge(sg("cs_ready"), u + 1)
                    need(pool, "y_summed", u - 3)
                    nc.gpsimd.tensor_tensor(yc[:, s % 4], sta[:, s % 2], cs[:, s % 2], ALU.mult).then_inc(sg("yc_ready"), 1)

            batches_on(pool, batch)
            for s in range(BATCH + 1):
                flow_gpsimd(s, True)

        def scan_tensor(pe):
            pe.wait_ge(sg("pick_ready"), 1)
            pe.wait_ge(sg("bc_third"), BATCH)
            pe.wait_ge(sg("dt_ready"), 1)

            def summed(b, s):
                u = b * STATE + s
                if s == 0:
                    need(pe, "y_read", b)
                pe.wait_ge(sg("yc_ready"), u + 1)
                nc.tensor.matmul(bank[:, Y_B, :], ident, yc[:, s % 4], start=(s == 0), stop=(s == STATE - 1)
                                 ).then_inc(sg("y_summed"), 1)

            def output(b):
                pe.wait_ge(sg("yf_ready"), b + 1)
                need(pe, "res_ready", b)
                for k in range(TPB):
                    i = nc.tensor.matmul(bank[:, O_B, k * H:(k + 1) * H], yf[:, 1, k * P:(k + 1) * P], par("w_out"),
                                         start=True, stop=True)
                i.then_inc(sg("out_done_f"), 1)

            def batch(b, back):
                for s in range(STATE):
                    u = b * STATE + s
                    need(pe, "db_ready", u - 1)
                    nc.tensor.matmul(bank[:, BB + s % 2, :], pick[0:ROWS, s, :], at_b(bc3, b)[0:ROWS],
                                     start=True, stop=True).then_inc(sg("b_done"), 1)
                    need(pe, "cs_ready", u - 1)
                    nc.tensor.matmul(bank[:, CB + s % 2, :], pick[0:ROWS, STATE + s, :], at_b(bc3, b)[0:ROWS],
                                     start=True, stop=True).then_inc(sg("c_done"), 1)
                    if s >= Y_LAG:
                        summed(b, s - Y_LAG)
                    elif back:
                        summed(b - 1, STATE - Y_LAG + s)
                    if back and s == 4:
                        output(b - 1)

            batches_on(pe, batch)
            for s in range(STATE - Y_LAG, STATE):
                summed(BATCH - 1, s)
            output(BATCH - 1)

        carved[0] = end_of_moe
        xe = [tiles(big[0]), tiles(big[1])]
        rows1 = tiles(big[2])

        def lead1(b):
            four = slice(b * TPB, (b + 1) * TPB)
            for t in range(b * TPB, (b + 1) * TPB):
                i = nc.vector.tensor_scalar(rows1[:, t, :], xres[:, t, :], mean[:, t:t + 1], rstd2[:, t:t + 1],
                                            ALU.subtract, ALU.mult)
            vdo(nc.vector, i)
            over = lambda a: a[:, None, :].broadcast_to([P, TPB, H])
            vdo(nc.vector, nc.vector.tensor_tensor(rows1[:, four, :], rows1[:, four, :], over(par("ln_g")), ALU.mult))
            nc.vector.tensor_tensor(rows1[:, four, :], rows1[:, four, :], over(par("ln_b")),
                                    ALU.add).then_inc(sg("xa_ready"), 1)

        def place1(v, h):
            tl, of, wide = half_of(h)
            m1 = lambda k: m32[:, k, tl]
            vdo(v, nc.vector.tensor_scalar(of(lg), of(lg), -10000.0, 10000.0, ALU.max, ALU.min))
            vdo(v, nc.vector.tensor_reduce(m1(0), of(lg), AX, ALU.max))
            nc.vector.tensor_tensor(of(key), of(lg), wide(m32[:, 0]), ALU.subtract).then_inc(sg("key_ready"), 1)
            v.wait_ge(sg("pr_ready"), HALVES + h + 1)
            vdo(v, nc.vector.tensor_reduce(m1(0), of(pr), AX, ALU.add))
            vdo(v, nc.vector.tensor_scalar(m1(0), m1(0), 1e-8, None, ALU.add))
            vdo(v, nc.vector.reciprocal(m1(1), m1(0)))
            vdo(v, nc.vector.tensor_tensor(of(pr), of(pr), wide(m32[:, 1]), ALU.mult))
            vdo(v, nc.vector.tensor_scalar(of(pr), of(pr), 1e-8, 1.0, ALU.max, ALU.min))
            vdo(v, nc.vector.tensor_copy(of(key), of(pr)))
            place_vector(v, 1, h)
            for b in half_batches(h):
                for t in range(b * TPB, (b + 1) * TPB):
                    i = nc.vector.tensor_scalar(xe[0][:, t, :], rows1[:, t, :], gain[:, 0, t:t + 1], None, ALU.mult)
                i.then_inc(sg("xe0_ready"), 1)

        def half_batches(h):
            return range(h * BATCH // HALVES, (h + 1) * BATCH // HALVES)

        def moe1_vector(v):
            with cv.loop(v, BATCH, 1) as b:
                for j in range(TPB):
                    t = b * TPB + j
                    i = nc.vector.tensor_scalar(f_res[:, t, :], xres[:, t, :], mean[:, bass.ds(t, 1)],
                                                rstd[:, bass.ds(t, 1)], ALU.subtract, ALU.mult)
                i.then_inc(v_step, cv.one())
            experts_vector(v, 1)
            stats_of = {}
            for s in range(BATCH + 1):
                if s < BATCH:
                    four = slice(s * TPB, (s + 1) * TPB)
                    v.wait_ge(sg(f"back{s}"), 2 * 16 * 2 * TPB)
                    for k in range(2):
                        vdo(v, nc.vector.tensor_tensor(f_res[:, four, :], f_res[:, four, :], xe[k][:, four, :], ALU.add))
                    for t in range(s * TPB, (s + 1) * TPB):
                        i = nc.vector.bn_stats(st[:, t, :], f_res[:, t, :])
                    vdo(v, i)
                    stats_of[s] = moments(v, s * TPB, (s + 1) * TPB)
                if s >= 1:
                    four = slice((s - 1) * TPB, s * TPB)
                    v.wait_ge(sg("rstd_ready"), stats_of[s - 1])
                    for t in range((s - 1) * TPB, s * TPB):
                        i = nc.vector.tensor_scalar(f_res[:, t, :], f_res[:, t, :], mean[:, t:t + 1], rstd[:, t:t + 1],
                                                    ALU.subtract, ALU.mult)
                    vdo(v, i)
                    nc.vector.tensor_tensor(xres[:, four, :], xres[:, four, :], f_res[:, four, :], ALU.add).then_inc(sg("x_out"), 1)

        def moe1_scalar(act):
            def half(h):
                tl, of, _ = half_of(h)
                act.wait_ge(sg("key_ready"), h + 1)
                nc.scalar.activation(of(pr), of(key), ACT.Exp).then_inc(sg("pr_ready"), 1)
                act.wait_ge(sg("rows_ready"), HALVES + h + 1)
                for b in half_batches(h):
                    for t in range(b * TPB, (b + 1) * TPB):
                        i = nc.scalar.activation(xe[1][:, t, :], rows1[:, t, :], ACT.Identity, scale=gain[:, 1, t:t + 1])
                    i.then_inc(sg("xe1_ready"), 1)

            route_scalar(act, 1, half)
            experts_scalar(act, 1)

        def moe1_tensor(pe):
            route_tensor(pe, 1)
            experts_tensor(pe, 1)

        def moe1_gpsimd(pool):
            scatter_gpsimd(pool, 1, xe)
            gather_gpsimd(pool, 1, xe,
                          lambda s: rsqrts(s * TPB, (s + 1) * TPB) if s < BATCH else None)

        def moe1_sync(sync):
            sync.wait_ge(sg("y_out"), SLOTS)
            sync.dma_start(experts_up[:, 0:EXPERTS, :], up1_d).then_inc(sg("experts_in"), 16)
            sync.dma_start(experts_down[:, 0:EXPERTS, :, :], down1_d).then_inc(sg("experts_in"), 16)
            experts_sync(sync, 1)
            for b in range(BATCH):
                sync.wait_ge(sg("x_out"), b + 1)
                sync.dma_start(out_d.rearrange("(t p) c -> p t c", p=P)[:, b * TPB:(b + 1) * TPB, :],
                               xres[:, b * TPB:(b + 1) * TPB, :]).then_inc(sg("stored"), 16)
            sync.wait_ge(sg("stored"), 16 * BATCH)

        block = ctx.enter_context(nc.Block())

        @block.sync
        def _(sync):
            prep_sync(sync)
            experts_sync(sync, 0)
            moe1_sync(sync)

        @block.gpsimd
        def _(pool):
            prep_gpsimd(pool)
            recur_gpsimd(pool)
            post_gpsimd(pool)
            moe0_gpsimd(pool)
            scan_gpsimd(pool)
            moe1_gpsimd(pool)

        @block.vector
        def _(v):
            prep_vector(v)
            recur_vector(v)
            post_vector(v)
            moe0_vector(v)
            ssm_prep_vector(v)
            scan_vector(v)
            moe1_vector(v)

        @block.tensor
        def _(pe):
            prep_tensor(pe)
            recur_tensor(pe)
            post_tensor(pe)
            moe0_tensor(pe)
            ssm_prep_tensor(pe)
            scan_tensor(pe)
            moe1_tensor(pe)

        @block.scalar
        def _(act):
            prep_scalar(act)
            recur_scalar(act)
            post_scalar(act)
            moe0_scalar(act)
            ssm_prep_scalar(act)
            scan_scalar(act)
            moe1_scalar(act)


def _packed(x):
    def rows(v):
        return np.broadcast_to(v[None, :], (P, v.shape[0]))

    def bd(v):
        return np.tile(v, (B4, 1))

    part = {}
    part["proj"] = np.concatenate([x["L0_attn_W" + n].T for n in "kvq"] +
                                  [x["L0_attn_" + n + "W"].T for n in "aet"], axis=1)
    part["gate"] = x["L0_attn_gW"].T
    part["gate_b"] = rows(x["L0_attn_gb"])
    part["norm_g"] = rows(x["L0_attn_norm_g"])
    wo = np.zeros((B4, D, B4, H), np.float32)
    for b in range(B4):
        wo[b, :, b, :] = x["L0_attn_Wo"].T
    part["wo"] = wo.reshape(P, B4 * H)
    part["conv_w"] = np.concatenate([bd(x[f"L0_attn_c{n}w"]) for n in "kvq"], axis=1)
    part["conv_b"] = np.concatenate([bd(x[f"L0_attn_c{n}b"][:, None]) for n in "kvq"], axis=1)
    part["bias3"] = np.concatenate([bd(x[f"L0_attn_{n}b"][:, None]) for n in "aet"], axis=1)
    part["mem"] = np.concatenate([bd(x["L0_attn_mW1"].T), bd(x["L0_attn_mW2"].T)], axis=1)
    part["route0"] = x["L0_ffn_gate_w"].T
    part["beta0"] = rows(x["L0_ffn_beta"])
    part["route1"] = x["L1_ffn_router_w"].T
    part["ln_g"] = rows(x["L1_ffn_ln_gamma"])
    part["ln_b"] = rows(x["L1_ffn_ln_beta"])
    part["w_in"] = x["L1_attn_W_in"].T
    part["w_bc"] = np.tile(x["L1_attn_W_x"].T, (1, 3))
    part["w_dt"] = x["L1_attn_W_dt"].T
    part["w_out"] = x["L1_attn_W_out"].T
    part["sconv"] = x["L1_attn_conv_w"][:, 0, :]
    part["b_dt"] = x["L1_attn_b_dt"][:, None]
    part["a_log"] = x["L1_attn_A_log"]
    part["skip_d"] = x["L1_attn_D_param"][:, None]
    part["gamma"] = x["L1_attn_gamma"][:, None]
    part["beta"] = x["L1_attn_beta"][:, None]
    p = np.arange(P)
    part["ident"] = np.eye(P)
    part["quad"] = (p[:, None] // D == p[None, :] // D)
    part["neg_i"] = -(p[:, None] % CHUNK == np.arange(CHUNK)[None, :]).astype(np.float32)
    part["mean_bd"] = (p[:, None] // D == p[None, :] // D) / D
    part["mean_sel"] = (p[:, None] // D == np.arange(B4 * 64)[None, :] // 64) / D
    part["before"] = (p[:, None] < p[None, :])
    part["ones"] = np.ones((P, P))
    part["rank8"] = rows(np.arange(EXPERTS, 0, -1))
    part["edge"] = rows(np.arange(TILES) * P)
    part["slot"] = rows(np.arange(HALF_SLOTS))
    part["pick"] = (p[:, None] % (2 * STATE) == np.arange(2 * STATE)[None, :])
    packed = np.zeros((P, PACKED), np.float32)
    for name, (at, width) in AT.items():
        assert part[name].shape == (P, width), (name, part[name].shape)
        packed[:, at:at + width] = part[name]
    return packed


def _experts(up, down):
    n = up.shape[0]
    return (np.ascontiguousarray(up.transpose(1, 0, 2)),
            np.ascontiguousarray(down.reshape(n, 2, P, H).transpose(2, 0, 1, 3)))


def kernel(**inputs):
    import concourse.bacc as _bacc
    from concourse.bass_utils import run_bass_kernel_spmd as _run

    x = {k: np.asarray(v) for k, v in inputs.items()}
    up0 = np.concatenate([np.concatenate([x["L0_ffn_gate_proj_w"], x["L0_ffn_shared_gate_w"]]),
                          np.concatenate([x["L0_ffn_up_proj_w"], x["L0_ffn_shared_up_w"]])], axis=2)
    down0 = np.concatenate([x["L0_ffn_down_proj_w"], x["L0_ffn_shared_down_w"]])
    up0, down0 = _experts(up0, down0)
    up1, down1 = _experts(x["L1_ffn_gate_up_w"].transpose(0, 2, 1), x["L1_ffn_down_w"].transpose(0, 2, 1))
    arrays = {"x": np.ascontiguousarray(x["L0_attn_hidden"]).reshape(TOKENS, H), "packed": _packed(x),
              "up0": up0, "down0": down0, "up1": up1, "down1": down1}
    nc = _bacc.Bacc("TRN2", target_bir_lowering=False, num_devices=1)
    args = [nc.dram_tensor(n, a.shape, F32, kind="ExternalInput").ap() for n, a in arrays.items()]
    out = nc.dram_tensor("out", (TOKENS, H), F32, kind="ExternalOutput").ap()
    build(nc, *args, out)
    r = _run(nc, [arrays], core_ids=[0])
    return r.results[0]["out"].reshape(BATCH, SEQ, H)
```

```python
from contextlib import ExitStack, contextmanager

import numpy as np

import concourse.bass as bass
from concourse import mybir

F32 = mybir.dt.float32
BF16 = mybir.dt.bfloat16
I32 = mybir.dt.int32
ALU = mybir.AluOpType
ACT = mybir.ActivationFunctionType
AX = mybir.AxisListType.X

P = 128
BATCH, SEQ, H = 8, 512, 128
TOKENS = BATCH * SEQ
TILES = TOKENS // P
TPB = SEQ // P
GROUPS, B4 = 2, 4
D = 32
CHUNK = 64
CHUNKS = SEQ // CHUNK
EXPERTS, MID = 8, 256
SHARES = (4, 4)
SHARE_B = (0, 4, 8)
SHARE_T = tuple(b * TPB for b in SHARE_B)
SHARE_SLOTS = tuple(2 * n * TPB + EXPERTS for n in SHARES)
SLOTS = sum(SHARE_SLOTS)
SLOT_AT = (0, SHARE_SLOTS[0])
STATE = 16
EPS = 1e-5

PARTS = [
    ("proj", 6 * D), ("gate", H), ("gate_b", H), ("norm_g", H), ("wo", B4 * H),
    ("conv_w", 12), ("conv_b", 3), ("bias3", 3), ("mem", 2 * D),
    ("route0", EXPERTS), ("beta0", EXPERTS), ("route1", EXPERTS), ("ln_g", H), ("ln_b", H),
    ("w_in", 2 * H), ("w_bc", 3 * 2 * STATE), ("w_dt", H), ("w_out", H),
    ("sconv", 3), ("b_dt", 1), ("a_log", STATE), ("skip_d", 1), ("gamma", 1), ("beta", 1),
    ("ident", P), ("quad", P), ("neg_i", CHUNK), ("mean_bd", P), ("mean_sel", B4 * 64),
    ("before", P), ("ones", P), ("rank8", EXPERTS), ("edge", TILES), ("slot", max(SHARE_SLOTS)),
    ("pick", 2 * STATE), ("affine", 2),
]
AT = {}
_at = 0
for _name, _width in PARTS:
    AT[_name] = (_at, _width)
    _at += _width
PACKED = _at


class Count:

    def __init__(self):
        self.base, self.k = 0, 0

    def one(self):
        self.k += 1
        return 1

    @property
    def now(self):
        return self.base + self.k

    @contextmanager
    def loop(self, eng, n, per):
        start = self.now
        with eng.Fori(0, n) as i:
            self.base, self.k = start + i * per, 0
            yield i
            assert self.k == per, f"{self.k} increments in a round, {per} said"
        self.base, self.k = start + n * per, 0

STEPS_V = 21
SCRATCH = 20500


def build(nc, x_d, packed_d, up0_d, down0_d, up1_d, down1_d, out_d):
    ctx = ExitStack()
    with ctx:
        def sb(name, shape, dt=F32):
            return ctx.enter_context(nc.sbuf_tensor(name, shape, dt))

        def sem(name):
            return ctx.enter_context(nc.semaphore(name))

        xres = sb("xres", [P, TILES, H])
        pk = sb("pk", [P, PACKED])

        def par(name, a=0, b=None):
            at, width = AT[name]
            return pk[:, at + a:at + (width if b is None else b)]

        big = [sb(f"big{n}", [P, TOKENS]) for n in range(4)]
        experts_up = sb("experts_up", [P, EXPERTS + 1, 2 * MID])
        experts_down = sb("experts_down", [P, EXPERTS + 1, 2, H])
        scratch = sb("scratch", [P, SCRATCH])
        carved = [0]

        def carve(name, shape, dt=F32):
            n = int(np.prod(shape[1:])) // (2 if dt == BF16 else 1)
            a = scratch[:, carved[0]:carved[0] + n]
            carved[0] += n
            assert carved[0] <= SCRATCH, (name, carved[0])
            if dt != F32:
                a = a.bitcast(dt)
            axes = " ".join(f"a{k}" for k in range(1, len(shape)))
            if len(shape) == 2:
                return a
            return a.rearrange(f"p ({axes}) -> p {axes}", **{f"a{k}": shape[k] for k in range(1, len(shape))})

        ident, quad = par("ident"), par("quad")
        quad4 = quad.rearrange("p (b c) -> p b c", b=B4)
        pow_c = sb("pow_c", [P, TILES])
        st = sb("st", [P, TILES, 6])
        mv = sb("mv", [P, TILES, 2])
        neg_mean = sb("neg_mean", [P, TILES])
        var = sb("var", [P, TILES])
        var2 = sb("var2", [P, TILES])
        rstd = sb("rstd", [P, TILES])
        rstd2 = sb("rstd2", [P, TILES])
        shift = sb("shift", [P, TILES])
        shift2 = sb("shift2", [P, TILES])

        bank = ctx.enter_context(nc.psum_tensor("bank", [P, 8, 512], F32))

        S = {}

        def sg(name):
            if name not in S:
                S[name] = sem(name)
            return S[name]

        v_step, p_step, a_step = sg("v_step"), sg("p_step"), sg("a_step")
        cv, cp, ca = Count(), Count(), Count()

        def vdo(v, i):
            i.then_inc(v_step, cv.one())
            v.wait_ge(v_step, cv.now)

        def stats(v, src, b):
            for t in range(b * TPB, (b + 1) * TPB):
                i = nc.vector.bn_stats(st[:, t, :], src[:, t, :])
            vdo(v, i)

        def moments(v, lo, hi, twice=False):
            for t in range(lo, hi):
                i = nc.vector.bn_aggr(mv[:, t, :], st[:, t, :])
            vdo(v, i)
            nc.vector.tensor_scalar(neg_mean[:, lo:hi], mv[:, lo:hi, 0], -1.0, None, ALU.mult)
            i = nc.vector.tensor_scalar(var[:, lo:hi], mv[:, lo:hi, 1], EPS, None, ALU.add)
            if twice:
                i = nc.vector.tensor_scalar(var2[:, lo:hi], mv[:, lo:hi, 1], 1.0 + EPS, EPS * EPS, ALU.mult, ALU.add)
            i.then_inc(sg("var_ready"), 1)
            n_asked[0] += 1
            return n_asked[0]

        n_asked = [0]
        n_var = [0]

        def rsqrts(lo, hi, twice=False, shifts=True):
            n_var[0] += 1
            nc.gpsimd.wait_ge(sg("var_ready"), n_var[0])
            def out(var, rstd, shift):
                nc.gpsimd.tensor_tensor(rstd[:, lo:hi], var[:, lo:hi], pow_c[:, lo:hi], ALU.pow).then_inc(p_step, cp.one())
                if not shifts:
                    return
                nc.gpsimd.wait_ge(p_step, cp.now)
                nc.gpsimd.tensor_tensor(shift[:, lo:hi], neg_mean[:, lo:hi], rstd[:, lo:hi], ALU.mult).then_inc(p_step, cp.one())

            out(var, rstd, shift)
            if twice:
                out(var2, rstd2, shift2)
            nc.gpsimd.wait_ge(p_step, cp.now)
            nc.gpsimd.sem_inc(sg("rstd_ready"), 1)

        xn = carve("xn", [P, 2, TPB, H])
        xT = carve("xT", [P, 2, SEQ])
        pre = carve("pre", [P, 3, 4 + SEQ])
        kvq = carve("kvq", [P, 3, GROUPS, SEQ])
        w_st = carve("w_st", [P, GROUPS, SEQ])
        b_st = carve("b_st", [P, GROUPS, SEQ])
        e_st = carve("e_st", [P, GROUPS, SEQ])
        gw_n = carve("gw_n", [P, H])
        gb_n = carve("gb_n", [P, H])
        gate_t = big[0][:, :].rearrange("p (t c) -> p t c", t=TILES)
        sga = big[1][:, 0:1024].rearrange("p (g n) -> p g n", g=GROUPS)
        sge = big[1][:, 1024:2048].rearrange("p (g n) -> p g n", g=GROUPS)
        tabs = big[1][:, 2048:3072].rearrange("p (g n) -> p g n", g=GROUPS)
        tlin = big[1][:, 3072:4096].rearrange("p (g n) -> p g n", g=GROUPS)
        eta_c, keep_c = big[2][:, 0:2048], big[2][:, 2048:4096]
        xco, yco = big[3][:, 0:2048], big[3][:, 2048:4096]
        tmp = lambda k: big[3][:, k * 1024:(k + 1) * 1024]

        TB, GB = 0, 1

        def prep_sync(sync):
            for q in range(BATCH // 2):
                at = slice(q * 2 * TPB, (q + 1) * 2 * TPB)
                sync.dma_start(xres[:, at, :], x_d.rearrange("(t p) c -> p t c", p=P)[:, at, :]
                               ).then_inc(sg(f"x_in{q}"), 16)
                if q == 0:
                    sync.dma_start(pk[:, :], packed_d).then_inc(sg("packed_in"), 16)

        def prep_gpsimd(pool):
            nc.gpsimd.memset(zeros[:, :], 0.0).then_inc(sg("zeros_ready"), 1)
            nc.gpsimd.memset(pow_c[:, :], -0.5).then_inc(p_step, cp.one())
            nc.gpsimd.memset(big[3][:, 2048:4096], 0.0).then_inc(sg("tmp_zero"), 1)
            pool.wait_ge(p_step, cp.now)
            for b in range(BATCH):
                rsqrts(b * TPB, (b + 1) * TPB)

        def prep_vector(v):
            v.sem_inc(sg("gt_free"), 1)
            v.sem_inc(sg("pre_free"), 1)
            nc.vector.memset(pre[:, :, :], 0.0).then_inc(sg("pre_zero"), 1)

            def gate_add(b):
                v.wait_ge(sg("gt_done"), b + 1)
                nc.vector.tensor_tensor(
                    gate_t[:, b * TPB:(b + 1) * TPB, :], bank[:, GB, :].rearrange("p (j c) -> p j c", j=TPB),
                    gb_n[:, None, :].broadcast_to([P, TPB, H]), ALU.add).then_inc(sg("gt_free"), 1)

            def conv(g):
                v.wait_ge(sg("pre_ready"), g + 1)
                for tap in range(4):
                    for kind in range(3):
                        src = pre[:, kind, tap:tap + SEQ]
                        dst = kvq[:, kind, g, :]
                        w = par("conv_w", kind * 4 + tap, kind * 4 + tap + 1)
                        if tap == 0:
                            i = nc.vector.tensor_scalar(dst, src, w, par("conv_b", kind, kind + 1), ALU.mult, ALU.add)
                        else:
                            i = nc.vector.scalar_tensor_tensor(dst, src, w, dst, ALU.mult, ALU.add)
                        if tap < 3:
                            i.then_inc(v_step, cv.one())
                    if tap < 3:
                        v.wait_ge(v_step, cv.now)
                i.then_inc(sg("pre_free"), 1)

            asked = {}
            for s in range(BATCH + 2):
                if s < BATCH:
                    v.wait_ge(sg(f"x_in{s // 2}"), 16)
                    stats(v, xres, s)
                    asked[s] = moments(v, s * TPB, (s + 1) * TPB)
                if s == 0:
                    v.wait_ge(sg("packed_in"), 16)
                    nc.vector.tensor_tensor(gw_n[:, :], par("gate"), par("norm_g"), ALU.mult).then_inc(sg("gw_ready"), 1)
                    nc.vector.tensor_tensor(gb_n[:, :], par("gate_b"), par("norm_g"), ALU.mult).then_inc(v_step, cv.one())
                if 0 <= s - 1 < BATCH:
                    b = s - 1
                    v.wait_ge(sg("xn_free"), b + 1)
                    v.wait_ge(sg("rstd_ready"), asked[b])
                    for j in range(TPB):
                        t = b * TPB + j
                        i = nc.vector.tensor_scalar(xn[:, b % 2, j, :], xres[:, t, :], neg_mean[:, t:t + 1],
                                                    rstd[:, t:t + 1], ALU.add, ALU.mult)
                    i.then_inc(sg("xn_ready"), 1)
                if s >= 2:
                    gate_add(s - 2)
                if s == B4 + 3:
                    conv(0)
            conv(1)

            v.wait_ge(sg("theta_parts"), 1)
            theta = tlin
            nc.vector.scalar_tensor_tensor(theta[:, :, :], tlin[:, :, :], 0.0, tabs[:, :, :],
                                           ALU.max, ALU.add).then_inc(sg("theta_ready"), 1)
            starts = lambda a: a.rearrange("p (c t) -> p c t", t=CHUNK)[:, :, 0:1]
            flat = lambda a: a[:, :, :].rearrange("p g n -> p (g n)")
            v.wait_ge(sg("bd_read"), 1)
            v.wait_ge(sg("tmp_zero"), 1)
            nc.vector.tensor_copy(starts(tmp(2)), starts(tmp(0))).then_inc(v_step, cv.one())
            nc.vector.tensor_copy(starts(tmp(3)), starts(tmp(1))).then_inc(v_step, cv.one())
            v.wait_ge(v_step, cv.now)
            nc.vector.memset(starts(tmp(0)), 0.0).then_inc(v_step, cv.one())
            nc.vector.memset(starts(tmp(1)), 0.0).then_inc(v_step, cv.one())
            v.wait_ge(v_step, cv.now)
            nc.vector.tensor_tensor_scan(flat(e_st), tmp(0), tmp(2), 0.0, ALU.mult, ALU.add).then_inc(v_step, cv.one())
            nc.vector.tensor_tensor_scan(flat(w_st), tmp(1), tmp(3), 0.0, ALU.mult, ALU.add).then_inc(v_step, cv.one())
            v.wait_ge(v_step, cv.now)
            nc.vector.tensor_tensor_scan(flat(b_st), tmp(1), flat(e_st), 0.0, ALU.mult, ALU.add).then_inc(v_step, cv.one())
            v.wait_ge(v_step, cv.now)
            v.wait_ge(sg("bank_free"), 1)
            nc.vector.memset(starts(eta_c), 0.0).then_inc(v_step, cv.one())
            nc.vector.memset(starts(keep_c), 0.0).then_inc(v_step, cv.one())
            v.wait_ge(sg("means"), 4)
            nc.vector.scalar_tensor_tensor(
                yco.rearrange("p (c t) -> p c t", t=CHUNK),
                bank[:, 4:8, :].rearrange("p b n -> p (b n)").rearrange("p (c t) -> p c t", t=CHUNK), 0.1,
                par("neg_i")[:, None, :].broadcast_to([P, 4 * CHUNKS, CHUNK]),
                ALU.mult, ALU.mult).then_inc(v_step, cv.one())
            v.wait_ge(v_step, cv.now)
            nc.vector.tensor_tensor_scan(xco, eta_c, yco, 0.0, ALU.mult, ALU.add).then_inc(v_step, cv.one())
            v.wait_ge(v_step, cv.now)
            nc.vector.tensor_tensor_scan(yco, keep_c, xco, 0.0, ALU.mult, ALU.add).then_inc(sg("coef_ready"), 1)

        def prep_tensor(pe):
            pe.sem_inc(sg("xn_free"), 2)
            pe.sem_inc(sg("xT_free"), 2)
            pe.wait_ge(sg("packed_in"), 16)
            pe.wait_ge(sg("gw_ready"), 1)
            with pe.Fori(0, GROUPS) as g:
                for b4 in range(B4):
                    u = g * B4 + b4
                    pe.wait_ge(sg("xn_ready"), u + 1)
                    for j in range(TPB):
                        i = nc.tensor.transpose(bank[:, TB, j * P:(j + 1) * P], xn[:, b4 % 2, j, :], ident)
                    i.then_inc(sg("xn_free"), 1)
                    pe.wait_ge(sg("xT_ready"), u + 1)
                    pe.wait_ge(sg("gt_free"), u + 1)
                    for j in range(TPB):
                        i = nc.tensor.matmul(bank[:, GB, j * H:(j + 1) * H], xT[:, b4 % 2, j * P:(j + 1) * P],
                                             gw_n[:, :], start=True, stop=True)
                    i.then_inc(sg("gt_done"), 1)
                    if b4 == 0:
                        pe.wait_ge(sg("kinds_free"), g + 1)
                    for kind in range(6):
                        i = nc.tensor.matmul(bank[D * b4:D * b4 + D, 2 + kind, :], par("proj", kind * D, kind * D + D),
                                             xT[:, b4 % 2, :], start=True, stop=True)
                    i.then_inc(sg("xT_free"), 1)
            pe.wait_ge(sg("kinds_free"), 1 + GROUPS)
            pe.wait_ge(sg("gt_free"), 1 + BATCH)
            for k, s in enumerate((sge, sga)):
                for g in range(GROUPS):
                    i = nc.tensor.matmul(bank[:, 2 * k + g, :], par("mean_bd"), s[:, g, :], start=True, stop=True)
            i.then_inc(sg("means"), 1)

            def spread(s, at):
                for b4 in range(B4):
                    for g in range(GROUPS):
                        i = nc.tensor.matmul(bank[64 * g:64 * g + 64, at + b4, :], par("mean_sel", b4 * 64, b4 * 64 + 64),
                                             s[:, g, :], start=True, stop=True)
                i.then_inc(sg("means"), 1)

            spread(sge, 4)
            pe.wait_ge(sg("bd_read"), 1)
            spread(sga, 0)
            pe.wait_ge(sg("theta_ready"), 1)
            pe.wait_ge(sg("bank_free"), 1)
            spread(tlin, 4)

        def prep_scalar(act):
            act.sem_inc(sg("kinds_free"), 1)
            act.wait_ge(sg(f"x_in{BATCH // 2 - 1}"), 16)
            act.dma_start(experts_up[:, :, :], up0_d).then_inc(sg("experts_in"), 16)
            act.dma_start(experts_down[:, :, :, :], down0_d).then_inc(sg("experts_in"), 16)
            act.wait_ge(sg("zeros_ready"), 1)
            for n in range(2):
                for h in range(2):
                    act.dma_start(rows_d[n][h].rearrange("(s p) c -> p s c", p=P),
                                  zeros[:, None, :].broadcast_to([P, SHARE_SLOTS[h], H])).then_inc(sg("zeroed"), 16)
            act.wait_ge(sg("packed_in"), 16)
            act.wait_ge(sg("pre_zero"), 1)
            with act.Fori(0, GROUPS) as g:
                for b4 in range(B4):
                    u = g * B4 + b4
                    act.wait_ge(sg("xn_free"), u + 3)
                    act.wait_ge(sg("xT_free"), u + 1)
                    nc.scalar.activation(xT[:, b4 % 2, :], bank[:, TB, :], ACT.Identity).then_inc(sg("xT_ready"), 1)
                act.wait_ge(sg("xT_free"), g * B4 + B4 + 2)
                act.wait_ge(sg("pre_free"), g + 1)
                for kind in range(3):
                    i = nc.scalar.activation(pre[:, kind, 3:3 + SEQ], bank[:, 2 + kind, :], ACT.Identity)
                i.then_inc(sg("pre_ready"), 1)
                nc.scalar.activation(sga[:, g, :], bank[:, 5, :], ACT.Sigmoid, bias=par("bias3", 0, 1))
                nc.scalar.activation(sge[:, g, :], bank[:, 6, :], ACT.Sigmoid, bias=par("bias3", 1, 2))
                nc.scalar.activation(tabs[:, g, :], bank[:, 7, :], ACT.Abs, bias=par("bias3", 2, 3))
                nc.scalar.activation(tlin[:, g, :], bank[:, 7, :], ACT.Identity,
                                     bias=par("bias3", 2, 3)).then_inc(sg("kinds_free"), 1)
            act.wait_ge(sg("kinds_free"), 1 + GROUPS)
            nc.scalar.activation(tabs[:, :, :], tabs[:, :, :], ACT.Exp, scale=-1.0).then_inc(a_step, ca.one())
            act.wait_ge(a_step, ca.now)
            nc.scalar.activation(tabs[:, :, :], tabs[:, :, :], ACT.Ln, bias=1.0).then_inc(sg("theta_parts"), 1)
            pair = lambda a: a.rearrange("p (g n) -> p g n", g=2)
            four = lambda a: a.rearrange("p (b n) -> p b n", b=4)
            act.wait_ge(sg("means"), 1)
            nc.scalar.activation(pair(tmp(0)), bank[:, 0:2, :], ACT.Identity, bias=par("affine", 0, 1), scale=0.9)
            nc.scalar.activation(pair(tmp(1)), bank[:, 2:4, :], ACT.Identity, bias=par("affine", 1, 2),
                                 scale=-0.1).then_inc(sg("bd_read"), 1)
            act.wait_ge(sg("means"), 2)
            nc.scalar.activation(four(eta_c), bank[:, 4:8, :], ACT.Identity, bias=par("affine", 0, 1), scale=0.9)
            act.wait_ge(sg("means"), 3)
            nc.scalar.activation(four(keep_c), bank[:, 0:4, :], ACT.Identity, bias=par("affine", 1, 2),
                                 scale=-0.1).then_inc(sg("bank_free"), 1)

        ks = carve("ks", [P, 2, GROUPS, CHUNK])
        vs = carve("vs", [P, 2, GROUPS, CHUNK])
        qx = carve("qx", [P, 2, GROUPS, B4, CHUNK])
        qa = carve("qa", [P, 2, GROUPS, CHUNK])
        qb = carve("qb", [P, 2, GROUPS, CHUNK])
        kh = carve("kh", [P, 2, P])
        vt = carve("vt", [P, P])
        de = carve("de", [P, 2, P])
        dec = carve("dec", [P, 2, 2, P])
        dexy = carve("dexy", [P, 2, 2, P])
        cxy = carve("cxy", [P, 2, B4])
        sq = carve("sq", [P, 2, P])
        sqe = carve("sqe", [P, P])
        skh = carve("skh", [P, 2, B4])
        sde = carve("sde", [P, 2, B4])
        cl = carve("cl", [P, 3, B4])
        sig = carve("sig", [P, P])
        dsilu = carve("dsilu", [P, P])
        hT = carve("hT", [P, 2, GROUPS, CHUNK])
        eT = carve("eT", [P, GROUPS, CHUNK])
        p1 = carve("p1", [P, B4, CHUNK])
        p2 = carve("p2", [P, B4, CHUNK])
        sig2 = carve("sig2", [P, GROUPS, CHUNK])
        h2 = carve("h2", [P, GROUPS, CHUNK])
        h2x = carve("h2x", [P, GROUPS, B4, CHUNK])
        h2a = carve("h2a", [P, GROUPS, CHUNK])
        h2b = carve("h2b", [P, GROUPS, CHUNK])
        wc = carve("wc", [P, GROUPS, 2, D])
        sc = carve("sc", [P, GROUPS, 2, D])
        sd = carve("sd", [P, GROUPS, 2, D])
        wx = carve("wx", [P, 2, GROUPS * 2, B4, D])
        sx = carve("sx", [P, 2, GROUPS * 2, B4, D])
        w2x = carve("w2x", [P, 2, GROUPS, P])
        ret = carve("ret", [P, GROUPS, SEQ])
        A_B, KV_B, SC_B, TR_B, G_B, R_B = 0, 1, 2, 3, 4, 6
        y5 = yco.rearrange("p (b c t) -> p b c t", b=B4, c=CHUNKS)
        x5 = xco.rearrange("p (b c t) -> p b c t", b=B4, c=CHUNKS)
        quad_t = quad4[:, :, 0:1]

        w2_bank = bank[:, KV_B, 256:512]
        pred_at, dh_at = bank[:, TR_B, 256:384], bank[:, TR_B, 384:512]
        r_bank = bank[:, R_B:R_B + 2, 0:128].rearrange("p g (k t) -> p g k t", k=2)

        def grp(a, g):
            return a[64 * g:64 * g + 64]

        def at(i):
            return bass.ds(i * CHUNK, CHUNK)

        def expand(dst, src):
            return nc.vector.tensor_tensor(
                dst, src[:, :, :, :].rearrange("p g k d -> p (g k) d")[:, :, None, :].broadcast_to([P, 4, B4, D]),
                quad4[:, None, :, :].broadcast_to([P, 4, B4, D]), ALU.mult)

        def expand_layer(dst, src, k):
            return nc.vector.tensor_tensor(
                dst.rearrange("p (g k) b d -> p g k b d", k=2)[:, :, k], src[:, :, k, None, :].broadcast_to([P, GROUPS, B4, D]),
                quad4[:, None, :, :].broadcast_to([P, GROUPS, B4, D]), ALU.mult)

        def chunks_on(eng, step):
            step(0, 0, True, False)
            with eng.Fori(0, (CHUNKS - 2) // 2) as r:
                step(2 * r + 1, 1, True, True)
                step(2 * r + 2, 0, True, True)
            step(CHUNKS - 1, 1, True, True)
            step(CHUNKS, 0, False, True)

        def recur_gpsimd(pool):
            pool.wait_ge(sg("coef_ready"), 1)

            def stage(i, p):
                nc.gpsimd.tensor_copy(ks[:, p], kvq[:, 0, :, at(i)])
                nc.gpsimd.tensor_copy(vs[:, p], kvq[:, 1, :, at(i)])
                for g in range(GROUPS):
                    nc.gpsimd.tensor_tensor(qx[:, p, g], kvq[:, 2, g, at(i)][:, None, :].broadcast_to([P, B4, CHUNK]),
                                            quad_t.broadcast_to([P, B4, CHUNK]), ALU.mult)
                nc.gpsimd.tensor_tensor(qa[:, p], kvq[:, 2, :, at(i)], w_st[:, :, at(i)], ALU.mult)
                nc.gpsimd.tensor_tensor(qb[:, p], kvq[:, 2, :, at(i)], b_st[:, :, at(i)],
                                        ALU.mult).then_inc(sg("staged"), 1)

            def step(i, p, chain, back):
                if back:
                    pool.wait_ge(sg("h2_ready"), i)
                    nc.gpsimd.tensor_tensor(h2a[:, :, :], h2[:, :, :], w_st[:, :, at(i - 1)], ALU.mult)
                    nc.gpsimd.tensor_tensor(h2b[:, :, :], h2[:, :, :], b_st[:, :, at(i - 1)],
                                            ALU.mult).then_inc(sg("h2ab"), 1)
                if chain:
                    pool.wait_ge(sg("norm_ready"), i + 1)
                    nc.gpsimd.tensor_tensor(cl[:, 2, :], cl[:, 1, :], pow_c[:, 0:B4], ALU.pow).then_inc(sg("clip_ready"), 1)

            stage(0, 0)

            def both(i, p, chain, back):
                if chain and not (isinstance(i, int) and i == CHUNKS - 1):
                    if back:
                        pool.wait_ge(sg("r1_done"), i)
                    stage(i + 1, 1 - p)
                step(i, p, chain, back)

            chunks_on(pool, both)

        def recur_scalar(act):
            act.wait_ge(sg("coef_ready"), 1)

            def turned_w2(p):
                nc.scalar.activation(w2x[:, p], w2_bank.rearrange("p (g n) -> p g n", g=2),
                                     ACT.Identity).then_inc(sg("w2_ready"), 1)

            def step(i, p, chain, back):
                if chain:
                    act.wait_ge(sg("a_done"), i + 1)
                    nc.scalar.activation(sig[:, :], bank[:, A_B, 0:P], ACT.Sigmoid).then_inc(sg("sig_ready"), 1)
                    act.wait_ge(sg("kv_done"), i + 1)
                    nc.scalar.activation(kh[:, 0, :], bank[:, KV_B, 0:P], ACT.Identity)
                    nc.scalar.activation(vt[:, :], bank[:, KV_B, P:2 * P], ACT.Identity).then_inc(sg("kv_ready"), 1)
                if back:
                    act.wait_ge(sg("r1_done"), i)
                    nc.scalar.activation(sig2[:, :, :], r_bank[:, :, 0, :], ACT.Sigmoid).then_inc(sg("sig2_ready"), 1)
                if chain:
                    act.wait_ge(sg("hT_done"), i + 1)
                    nc.scalar.activation(hT[:, p], bank[:, TR_B, 0:P].rearrange("p (g t) -> p g t", g=2),
                                         ACT.Identity).then_inc(sg("hT_ready"), 1)
                if chain and back:
                    act.wait_ge(sg("w2_done"), i + 1)
                    turned_w2(p)
                if chain:
                    act.wait_ge(sg("eT_done"), i + 1)
                    nc.scalar.activation(eT[:, :, :], bank[:, TR_B, P:2 * P].rearrange("p (g t) -> p g t", g=2),
                                         ACT.Identity).then_inc(sg("eT_ready"), 1)
                if back:
                    act.wait_ge(sg("r3_done"), i)
                    nc.scalar.activation(ret[:, :, at(i - 1)], r_bank[:, :, 1, :], ACT.Identity).then_inc(sg("ret_ready"), 1)

            act.wait_ge(sg("w2_done"), 1)
            turned_w2(0)
            chunks_on(act, step)

        def recur_vector(v):
            for g in range(GROUPS):
                nc.vector.tensor_copy(wc[:, g], par("mem").rearrange("p (k d) -> p k d", k=2)).then_inc(v_step, cv.one())
            nc.vector.memset(sc[:, :, :, :], 0.0).then_inc(v_step, cv.one())
            v.wait_ge(v_step, cv.now)
            v.wait_ge(sg("coef_ready"), 1)
            expand(sx[:, 0], sc)
            expand_layer(wx[:, 0], wc, 0).then_inc(sg("w1x_ready"), 1)
            expand_layer(wx[:, 0], wc, 1).then_inc(sg("w2x_ready"), 1)

            heads = lambda a: a.rearrange("p k (b d) -> p k b d", b=B4)

            def hidden(i, p, first):
                v.wait_ge(sg("sig_ready"), i + 1)
                a = bank[:, A_B, 0:P]
                if not first:
                    v.wait_ge(sg("hT_done"), i)
                nc.vector.tensor_tensor(kh[:, 1, :], a, sig[:, :], ALU.mult).then_inc(sg("h_ready"), 1)
                v.wait_ge(sg("h_ready"), i + 1)
                vdo(v, nc.vector.scalar_tensor_tensor(dsilu[:, :], a, 1.0, kh[:, 1, :], ALU.add, ALU.subtract))
                nc.vector.tensor_tensor(dsilu[:, :], dsilu[:, :], sig[:, :], ALU.mult).then_inc(v_step, cv.one())
                v.wait_ge(sg("kv_ready"), i + 1)
                vdo(v, nc.vector.tensor_tensor(sq[:, :, :], kh[:, :, :], kh[:, :, :], ALU.mult))
                nc.vector.tensor_reduce(skh[:, :, :], heads(sq[:, :, :]), AX, ALU.add).then_inc(v_step, cv.one())
                v.wait_ge(sg("pred_done"), i + 1)
                nc.vector.tensor_tensor(de[:, 1, :], pred_at, vt[:, :], ALU.subtract).then_inc(sg("e_ready"), 1)

            def read_hidden(i):
                v.wait_ge(sg("sig2_ready"), i)
                nc.vector.tensor_tensor(h2[:, :, :], r_bank[:, :, 0, :], sig2[:, :, :], ALU.mult).then_inc(sg("h2_ready"), 1)
                v.wait_ge(sg("h2_ready"), i)
                nc.vector.tensor_tensor(h2x[:, :, :, :], h2[:, :, None, :].broadcast_to([P, GROUPS, B4, CHUNK]),
                                        quad_t[:, None, :, :].broadcast_to([P, GROUPS, B4, CHUNK]),
                                        ALU.mult).then_inc(sg("h2x_ready"), 1)

            def e_norm(i):
                v.wait_ge(sg("e_ready"), i + 1)
                vdo(v, nc.vector.tensor_tensor(sqe[:, :], de[:, 1, :], de[:, 1, :], ALU.mult))
                vdo(v, nc.vector.tensor_reduce(sde[:, 1, :], sqe[:, :].rearrange("p (b d) -> p b d", b=B4), AX, ALU.add))
                vdo(v, nc.vector.tensor_tensor(sde[:, 1, :], sde[:, 1, :], skh[:, 1, :], ALU.mult))

            def norms(i, p):
                v.wait_ge(sg("dh_done"), i + 1)
                vdo(v, nc.vector.tensor_tensor(de[:, 0, :], dh_at, dsilu[:, :], ALU.mult))
                vdo(v, nc.vector.tensor_tensor(sqe[:, :], de[:, 0, :], de[:, 0, :], ALU.mult))
                vdo(v, nc.vector.tensor_reduce(sde[:, 0, :], sqe[:, :].rearrange("p (b d) -> p b d", b=B4), AX, ALU.add))
                vdo(v, nc.vector.tensor_tensor(sde[:, 0, :], sde[:, 0, :], skh[:, 0, :], ALU.mult))
                vdo(v, nc.vector.tensor_tensor(cl[:, 0, :], sde[:, 0, :], sde[:, 1, :], ALU.add))
                nc.vector.tensor_scalar(cl[:, 1, :], cl[:, 0, :], 25.0, None, ALU.max).then_inc(sg("norm_ready"), 1)

            def read_weights(i, chain):
                v.wait_ge(sg("s2_done"), i)
                if chain:
                    v.wait_ge(sg("s1_done"), i + 1)
                nc.vector.tensor_tensor(p2[:, :, :], bank[:, SC_B, 256:512].rearrange("p (b t) -> p b t", b=B4),
                                        y5[:, :, i - 1, :], ALU.mult).then_inc(sg("p2_ready"), 1)

            def update(i, p):
                v.wait_ge(sg("s1_done"), i + 1)
                nc.vector.tensor_tensor(p1[:, :, :], bank[:, SC_B, 0:256].rearrange("p (b t) -> p b t", b=B4),
                                        y5[:, :, i, :], ALU.mult).then_inc(sg("p1_ready"), 1)
                v.wait_ge(sg("clip_ready"), i + 1)
                for w, coef in enumerate((x5, y5)):
                    j = nc.vector.tensor_tensor(cxy[:, w, :, None], coef[:, :, i, CHUNK - 1:CHUNK], cl[:, 2, :, None],
                                                ALU.mult)
                vdo(v, j)
                for k in range(2):
                    j = nc.vector.tensor_tensor(
                        heads(dexy[:, k]), de[:, k, :].rearrange("p (b d) -> p b d", b=B4)[:, None, :, :].broadcast_to([P, 2, B4, D]),
                        cxy[:, :, :, None].broadcast_to([P, 2, B4, D]), ALU.mult)
                j.then_inc(sg("dxy_ready"), 1)
                nc.vector.tensor_tensor(heads(dec[:, p]), heads(de[:, :, :]),
                                        cl[:, 2, :][:, None, :, None].broadcast_to([P, 2, B4, D]),
                                        ALU.mult).then_inc(sg("dec_ready"), 1)
                last = lambda a, g: a[:, g, bass.ds(i * CHUNK + CHUNK - 1, 1)]
                fresh = lambda w: bank[:, G_B:G_B + 2, 0:128].rearrange("p g (k w d) -> p g k w d", k=2, w=2)[:, :, :, w, :]
                for g in range(GROUPS):
                    nc.vector.tensor_scalar(sd[:, g], sc[:, g], last(b_st, g), None, ALU.mult).then_inc(v_step, cv.one())
                for g in range(GROUPS):
                    v.wait_ge(v_step, cv.now - 1)
                    nc.vector.scalar_tensor_tensor(wc[:, g], wc[:, g], last(w_st, g), sd[:, g],
                                                   ALU.mult, ALU.add).then_inc(v_step, cv.one())
                for g in range(GROUPS):
                    nc.vector.tensor_scalar(sc[:, g], sc[:, g], last(e_st, g), None, ALU.mult).then_inc(v_step, cv.one())
                v.wait_ge(v_step, cv.now)
                v.wait_ge(sg("g_done"), i + 1)
                vdo(v, nc.vector.tensor_tensor(wc[:, :, :, :], wc[:, :, :, :], fresh(1), ALU.add))
                expand_layer(wx[:, 1 - p], wc, 0).then_inc(sg("w1x_ready"), 1)
                expand_layer(wx[:, 1 - p], wc, 1).then_inc(sg("w2x_ready"), 1)
                vdo(v, nc.vector.tensor_tensor(sc[:, :, :, :], sc[:, :, :, :], fresh(0), ALU.add))
                expand(sx[:, 1 - p], sc).then_inc(sg("sx_ready"), 1)

            def step(i, p, chain, back):
                if chain:
                    hidden(i, p, not back)
                if back:
                    read_hidden(i)
                if chain:
                    e_norm(i)
                    norms(i, p)
                if back:
                    read_weights(i, chain)
                if chain:
                    update(i, p)

            step(0, 0, True, False)
            with cv.loop(v, (CHUNKS - 2) // 2, 2 * STEPS_V) as r:
                step(2 * r + 1, 1, True, True)
                step(2 * r + 2, 0, True, True)
            step(CHUNKS - 1, 1, True, True)
            step(CHUNKS, 0, False, True)

        def recur_tensor(pe):
            def flip_w2(p):
                for g in range(GROUPS):
                    i = nc.tensor.transpose(w2_bank[:, g * P:(g + 1) * P],
                                            wx[:, p, 2 * g + 1].rearrange("p b d -> p (b d)"), ident)
                i.then_inc(sg("w2_done"), 1)

            def w(p, g, k):
                return wx[:, p, 2 * g + k].rearrange("p b d -> p (b d)")

            def s(p, g, k):
                return sx[:, p, 2 * g + k].rearrange("p b d -> p (b d)")

            def read_state(p, k, a, b):
                for g in range(GROUPS):
                    nc.tensor.matmul(r_bank[:, g, k, :], w(p, g, k), a[:, g, :], start=True, stop=False)
                    nc.tensor.matmul(r_bank[:, g, k, :], s(p, g, k), b[:, g, :], start=False, stop=True)

            def read_steps(p, k, src):
                for g in range(GROUPS):
                    for b4 in range(B4):
                        i = nc.tensor.matmul(r_bank[D * b4:D * b4 + D, g, k, :],
                                             grp(dec[:, p, k, D * b4:D * b4 + D], g), grp(src[:, b4, :], g),
                                             start=False, stop=True, skip_group_check=True)
                return i

            pe.wait_ge(sg("w2x_ready"), 1)
            flip_w2(0)
            pe.wait_ge(sg("w2_ready"), 1)

            def step(i, p, chain, back):
                if chain:
                    pe.wait_ge(sg("staged"), i + 1)
                    pe.wait_ge(sg("w1x_ready"), i + 1)
                    for g in range(GROUPS):
                        j = nc.tensor.matmul(bank[64 * g:64 * g + 64, A_B, 0:P], ks[:, p, g, :], w(p, g, 0),
                                             start=True, stop=True)
                    j.then_inc(sg("a_done"), 1)
                    for k, src in enumerate((ks, vs)):
                        j = nc.tensor.transpose(bank[:, KV_B, k * P:(k + 1) * P],
                                                src[:, p].rearrange("p g t -> p (g t)"), ident)
                    j.then_inc(sg("kv_done"), 1)
                if back:
                    pe.wait_ge(sg("p1_ready"), i)
                    pe.wait_ge(sg("dec_ready"), i)
                    pe.sem_inc(sg("pe_go"), 1)
                    read_steps(1 - p, 0, p1).then_inc(sg("r1_done"), 1)
                if chain:
                    pe.wait_ge(sg("h_ready"), i + 1)
                    nc.tensor.transpose(bank[:, TR_B, 0:P], kh[:, 1, :], ident).then_inc(sg("hT_done"), 1)
                    if back:
                        pe.wait_ge(sg("kv_ready"), i + 1)
                        pe.wait_ge(sg("w2x_ready"), i + 1)
                        flip_w2(p)
                    pe.wait_ge(sg("hT_ready"), i + 1)
                    for g in range(GROUPS):
                        j = nc.tensor.matmul(pred_at[64 * g:64 * g + 64], hT[:, p, g, :], w(p, g, 1),
                                             start=True, stop=True)
                    j.then_inc(sg("pred_done"), 1)
                    pe.wait_ge(sg("e_ready"), i + 1)
                    nc.tensor.transpose(bank[:, TR_B, P:2 * P], de[:, 1, :], ident).then_inc(sg("eT_done"), 1)
                    pe.wait_ge(sg("eT_ready"), i + 1)
                    pe.wait_ge(sg("w2_ready"), i + 1)
                    for g in range(GROUPS):
                        j = nc.tensor.matmul(dh_at[64 * g:64 * g + 64], eT[:, g, :], w2x[:, p, g, :],
                                             start=True, stop=True)
                    j.then_inc(sg("dh_done"), 1)
                if back:
                    pe.wait_ge(sg("h2x_ready"), i)
                    for g in range(GROUPS):
                        j = nc.tensor.matmul(bank[64 * g:64 * g + 64, SC_B, 256:512], hT[:, 1 - p, g, :],
                                             h2x[:, g].rearrange("p b t -> p (b t)"), start=True, stop=True)
                    j.then_inc(sg("s2_done"), 1)
                if chain:
                    for g in range(GROUPS):
                        j = nc.tensor.matmul(bank[64 * g:64 * g + 64, SC_B, 0:256], ks[:, p, g, :],
                                             qx[:, p, g].rearrange("p b t -> p (b t)"), start=True, stop=True)
                    j.then_inc(sg("s1_done"), 1)
                if back:
                    pe.wait_ge(sg("h2ab"), i)
                    read_state(1 - p, 1, h2a, h2b)
                    pe.wait_ge(sg("p2_ready"), i)
                    pe.sem_inc(sg("pe_go"), 1)
                    read_steps(1 - p, 1, p2).then_inc(sg("r3_done"), 1)
                if chain:
                    pe.wait_ge(sg("dxy_ready"), i + 1)
                    pe.sem_inc(sg("pe_go"), 1)
                    for g in range(GROUPS):
                        for k in range(2):
                            for b4 in range(B4):
                                j = nc.tensor.matmul(
                                    bank[D * b4:D * b4 + D, G_B + g, 64 * k:64 * k + 64],
                                    grp(kh[:, k, D * b4:D * b4 + D], g), grp(dexy[:, k, :, D * b4:D * b4 + D], g),
                                    start=True, stop=True)
                    j.then_inc(sg("g_done"), 1)
                    if back:
                        pe.wait_ge(sg("sx_ready"), i)
                        pe.wait_ge(sg("ret_ready"), i)
                    read_state(p, 0, qa[:, p], qb[:, p])

            chunks_on(pe, step)

        def post_tensor(pe):
            pe.wait_ge(sg("ret_ready"), CHUNKS)
            for n in range(GROUPS * TPB):
                g, j = divmod(n, TPB)
                if n >= 2:
                    pe.wait_ge(sg("o_read"), n - 1)
                nc.tensor.matmul(bank[:, n % 2, :], ret[:, g, j * P:(j + 1) * P], par("wo"),
                                 start=True, stop=True).then_inc(sg("o_done"), 1)

        tiles = lambda a: a[:, :].rearrange("p (t c) -> p t c", t=TILES)
        o_all = tiles(big[2])
        carved[0] = 0
        o_sq = kvq[:, :, :, :].rearrange("p k g n -> p (k g) n")

        def post_scalar(act):
            o5 = o_all.rearrange("p (g b j) c -> p g b j c", g=GROUPS, b=B4)
            for n in range(GROUPS * TPB):
                g, j = divmod(n, TPB)
                act.wait_ge(sg("o_done"), n + 1)
                src = bank[:, n % 2, :].rearrange("p (b c) -> p b c", b=B4)
                nc.scalar.activation(o5[:, g, :, j, :], src, ACT.Identity)
                if n >= 2:
                    act.wait_ge(sg("sq_read"), n - 1)
                nc.scalar.activation(o_sq[:, n % 2, :], bank[:, n % 2, :], ACT.Square).then_inc(sg("o_read"), 1)

        def post_vector(v):
            s4 = st[:, :, 0].rearrange("p (g b j) -> p g b j", g=GROUPS, b=B4)
            for n in range(GROUPS * TPB):
                g, j = divmod(n, TPB)
                v.wait_ge(sg("o_read"), n + 1)
                nc.vector.tensor_reduce(s4[:, g, :, j], o_sq[:, n % 2, :].rearrange("p (b c) -> p b c", b=B4),
                                        AX, ALU.add).then_inc(sg("sq_read"), 1)
            v.wait_ge(sg("sq_read"), GROUPS * TPB)
            nc.vector.tensor_scalar(var[:, :], st[:, :, 0], 1.0 / H, 1e-6, ALU.mult, ALU.add).then_inc(sg("var_ready"), 1)
            n_asked[0] += 1
            v.wait_ge(sg("rstd_ready"), n_asked[0])

            def gated(b):
                for t in range(b * TPB, (b + 1) * TPB):
                    i = nc.vector.scalar_tensor_tensor(o_all[:, t, :], o_all[:, t, :], rstd[:, t:t + 1],
                                                       gate_t[:, t, :], ALU.mult, ALU.mult)
                vdo(v, i)
                stats(v, o_all, b)

            flow_vector(v, "memory", o_all, gated, False,
                        lambda s: route_slot_vector(v, 0, lambda b: None, lambda v, h: None, s), ROUTE_LAG)

        def flow_vector(v, name, src, finish, twice, follow, lag):
            branch, fresh = {}, {}
            for s in range(BATCH + 2 + lag):
                if s < BATCH:
                    finish(s)
                    branch[s] = moments(v, s * TPB, (s + 1) * TPB)
                if 0 <= s - 1 < BATCH:
                    b = s - 1
                    four = slice(b * TPB, (b + 1) * TPB)
                    n_normed[0] += 1
                    v.wait_ge(sg("normed"), n_normed[0])
                    vdo(v, nc.vector.tensor_tensor(xres[:, four, :], xres[:, four, :], src[:, four, :], ALU.add))
                    stats(v, xres, b)
                    fresh[b] = moments(v, b * TPB, (b + 1) * TPB, twice)
                if s >= 2:
                    follow(s - 2)
            asked_of[name] = (branch, fresh)

        n_normed = [0]
        asked_of = {}

        def flow_scalar(act, name, src, follow, lag):
            branch, fresh = asked_of[name]
            for s in range(BATCH + 2 + lag):
                if 0 <= s - 1 < BATCH:
                    act.wait_ge(sg("rstd_ready"), branch[s - 1])
                    layer_norm(src, src, s - 1).then_inc(sg("normed"), 1)
                if s >= 2:
                    follow(s - 2, fresh.get(s - 2))

        def layer_norm(dst, src, b, twice=False):
            by, add = (rstd2, shift2) if twice else (rstd, shift)
            for t in range(b * TPB, (b + 1) * TPB):
                i = nc.scalar.activation(dst[:, t, :], src[:, t, :], ACT.Identity, bias=add[:, t:t + 1],
                                         scale=by[:, t:t + 1])
            return i

        def flow_gpsimd(s, twice):
            for lag, both in ((0, False), (1, twice)):
                if 0 <= s - lag < BATCH:
                    rsqrts((s - lag) * TPB, (s - lag + 1) * TPB, both)

        def post_gpsimd(pool):
            rsqrts(0, TILES, shifts=False)
        zeros = sb("zeros", [P, H])
        in_dram = lambda name: [[nc.dram_tensor(f"{name}{n}{h}", (SHARE_SLOTS[h] * P, H), F32).ap()
                                 for h in range(2)] for n in range(2)]
        rows_d, made_d = in_dram("sorted_rows"), in_dram("made_rows")
        xb = carve("xb", [P, 2, SEQ])
        lg = carve("lg", [P, TILES, EXPERTS])
        pr = carve("pr", [P, TILES, EXPERTS])
        key = carve("key", [P, TILES, EXPERTS])
        hot = [carve(f"hot{k}", [P, TILES, EXPERTS]) for k in range(3)]
        t8 = carve("t8", [P, TILES, EXPERTS])
        t8b = carve("t8b", [P, TILES, EXPERTS])
        m32 = carve("m32", [P, 2, TILES])
        gain = sb("gain", [P, 2, TILES])
        csum = carve("csum", [P, EXPERTS, TILES])
        e8 = carve("e8", [P, 4, EXPERTS])
        slot8 = carve("slot8", [P, max(SHARE_SLOTS), EXPERTS])
        slotf = carve("slotf", [P, max(SHARE_SLOTS)])
        rowf = carve("rowf", [P, 2, TILES])
        row_of = sb("row_of", [P, 2, TILES], I32)
        expert_of = sb("expert_of", [P, SLOTS], I32)
        sgs = carve("sgs", [P, 2, SEQ])
        hs = carve("hs", [P, 2, 2, SEQ])
        xr = carve("xr", [P, 2, 4, H])
        xT2 = carve("xT2", [P, 2, P])
        sgb = carve("sgb", [P, 2, MID])
        hb = carve("hb", [P, 2, MID])
        hTb = carve("hTb", [P, 2, MID])
        yb = carve("yb", [P, 2, 4, H])
        rows = tiles(big[0])
        xt_all = big[1][:, :]
        T0, L0B = 0, 2
        ROUTE_LAG = 2
        RANK_AT = SHARES[0] - 1 + ROUTE_LAG
        rows_of = [rows, tiles(big[2])]

        def turned(n, b):
            return xt_all[:, b * SEQ:(b + 1) * SEQ] if n == 0 else xb[:, b % 2]

        def route_slot_vector(v, n, lead, place, s):
            if s < BATCH:
                lead(s)
            if s >= ROUTE_LAG:
                b = s - ROUTE_LAG
                v.wait_ge(sg("lg_done"), n * BATCH + b + 1)
                nc.vector.tensor_copy(lg[:, b * TPB:(b + 1) * TPB, :],
                                      bank[:, L0B + b % 2, 0:TPB * EXPERTS].rearrange("p (j e) -> p j e", j=TPB)
                                      ).then_inc(sg("lg_out"), 1)
                if b + 1 in SHARE_B:
                    v.wait_ge(sg("lg_out"), n * BATCH + b + 1)
                    place(v, SHARE_B.index(b + 1) - 1)

        def route_slot_scalar(act, n, s, asked, share):
            if s < BATCH:
                act.wait_ge(sg("rstd_ready"), asked)
                layer_norm(rows_of[n], xres, s, twice=(n == 1)).then_inc(sg("xa_ready" if n == 0 else "rows_normed"), 1)
            if 1 <= s <= BATCH:
                b = s - 1
                act.wait_ge(sg("xa_turned"), n * BATCH + b + 1)
                if n == 1 and b >= 2:
                    act.wait_ge(sg("lg_done"), n * BATCH + b - 1)
                nc.scalar.activation(turned(n, b), bank[:, T0 + b % 2, :], ACT.Identity).then_inc(sg("xb_ready"), 1)
                if b == RANK_AT - 1:
                    share(0)
                if b == BATCH - 1:
                    share(1)

        def rank(pe, n, h):
            pe.wait_ge(sg("hot_ready"), n * 2 + h + 1)
            for k, w in enumerate(("before", "ones")):
                i = nc.tensor.matmul(bank[:, 6 + k, SHARE_T[h] * EXPERTS:SHARE_T[h + 1] * EXPERTS], par(w),
                                     hot[2][:, SHARE_T[h]:SHARE_T[h + 1], :].rearrange("p t e -> p (t e)"),
                                     start=True, stop=True)
            i.then_inc(sg("ranks"), 1)

        def route_tensor(pe, n):
            pe.wait_ge(sg("o_read"), GROUPS * TPB)

            for s in range(BATCH + 1):
                if s < BATCH:
                    pe.wait_ge(sg("xa_ready"), n * BATCH + s + 1)
                    if s >= 2:
                        pe.wait_ge(sg("xb_ready"), n * BATCH + s - 1)
                    for j in range(TPB):
                        i = nc.tensor.transpose(bank[:, T0 + s % 2, j * P:(j + 1) * P], rows_of[n][:, s * TPB + j, :], ident)
                    i.then_inc(sg("xa_turned"), 1)
                if s >= 1:
                    b = s - 1
                    pe.wait_ge(sg("xb_ready"), n * BATCH + b + 1)
                    if b >= 2:
                        pe.wait_ge(sg("lg_out"), n * BATCH + b - 1)
                    for j in range(TPB):
                        i = nc.tensor.matmul(bank[:, L0B + b % 2, j * EXPERTS:(j + 1) * EXPERTS],
                                             turned(n, b)[:, j * P:(j + 1) * P], par(f"route{n}"), start=True, stop=True)
                    i.then_inc(sg("lg_done"), 1)
                if n == 1 and s == RANK_AT:
                    rank(pe, n, 0)
            if n == 1:
                rank(pe, n, 1)

        def share_of(h):
            tl = slice(SHARE_T[h], SHARE_T[h + 1])
            return tl, (lambda a: a[:, tl, :]), (lambda a: a[:, tl, None].broadcast_to([P, SHARES[h] * TPB, EXPERTS]))

        def choose(v, dst, h):
            tl, of, wide = share_of(h)
            vdo(v, nc.vector.tensor_reduce(m32[:, 0, tl], of(key), AX, ALU.max))
            vdo(v, nc.vector.tensor_tensor(of(t8), of(key), wide(m32[:, 0]), ALU.is_equal))
            vdo(v, nc.vector.tensor_tensor(of(t8), of(t8), par("rank8")[:, None, :].broadcast_to([P, tl.stop - tl.start, EXPERTS]),
                                           ALU.mult))
            vdo(v, nc.vector.tensor_reduce(m32[:, 0, tl], of(t8), AX, ALU.max))
            vdo(v, nc.vector.tensor_tensor(of(dst), of(t8), wide(m32[:, 0]), ALU.is_equal))

        def first_choice(v, n, h):
            choose(v, hot[0], h)

        def second_choice(v, n, h):
            tl, of, wide = share_of(h)
            vdo(v, nc.vector.scalar_tensor_tensor(of(key), of(hot[0]), -3.0e38, of(key), ALU.mult, ALU.add))
            choose(v, hot[1], h)
            nc.vector.tensor_tensor(of(hot[2]), of(hot[0]), of(hot[1]), ALU.add).then_inc(sg("hot_ready"), 1)

        def weights(v, n, h):
            tl, of, wide = share_of(h)
            for k in range(2):
                vdo(v, nc.vector.tensor_tensor(of(t8), of(hot[k]), of(pr), ALU.mult))
                vdo(v, nc.vector.tensor_reduce(gain[:, k, tl], of(t8), AX, ALU.add))

        def ranked(tl, k):
            cols = bank[:, 6 + k, tl.start * EXPERTS:tl.stop * EXPERTS]
            return cols.rearrange("p (t e) -> p t e", e=EXPERTS)

        def count_rows(v, n, h):
            tl, of, wide = share_of(h)
            n_t = SHARES[h] * TPB
            total = ranked(tl, 1)
            v.wait_ge(sg("ranks"), n * 2 + h + 1)
            for e in range(EXPERTS):
                i = nc.vector.tensor_tensor_scan(csum[:, e, 0:n_t], par("ones", 0, n_t), total[:, :, e], 0.0,
                                                 ALU.mult, ALU.add)
            vdo(v, i)
            c8 = of(t8).rearrange("p t e -> p (t e)").rearrange("p (e t) -> p e t", e=EXPERTS)
            vdo(v, nc.vector.tensor_tensor(c8, csum[:, :, n_t - 1:n_t].broadcast_to([P, EXPERTS, n_t]),
                                           par("edge", 0, n_t)[:, None, :].broadcast_to([P, EXPERTS, n_t]), ALU.is_gt))
            vdo(v, nc.vector.tensor_reduce(e8[:, 0, :], c8, AX, ALU.add))
            vdo(v, nc.vector.tensor_tensor_scan(e8[:, 1, :], par("ones", 0, EXPERTS), e8[:, 0, :], 0.0,
                                                ALU.mult, ALU.add))
            vdo(v, nc.vector.tensor_tensor(e8[:, 2, :], e8[:, 1, :], e8[:, 0, :], ALU.subtract))
            vdo(v, nc.vector.tensor_scalar(e8[:, 3, :], e8[:, 2, :], float(P), None, ALU.mult))

        def sorted_places(v, n, h):
            tl, of, wide = share_of(h)
            n_t = SHARES[h] * TPB
            before, total = ranked(tl, 0), ranked(tl, 1)
            vdo(v, nc.vector.tensor_tensor(of(t8b), csum[:, :, 0:n_t].rearrange("p e t -> p t e"), total, ALU.subtract))
            vdo(v, nc.vector.tensor_tensor(of(t8b), of(t8b), before, ALU.add))
            vdo(v, nc.vector.tensor_tensor(of(t8b), of(t8b), e8[:, 3, :][:, None, :].broadcast_to([P, n_t, EXPERTS]),
                                           ALU.add))
            for k in range(2):
                vdo(v, nc.vector.tensor_tensor(of(t8), of(hot[k]), of(t8b), ALU.mult))
                vdo(v, nc.vector.tensor_reduce(rowf[:, k, tl], of(t8), AX, ALU.add))
            nc.vector.tensor_copy(row_of[:, :, tl], rowf[:, :, tl]).then_inc(sg("rows_ready"), 1)

        def tile_experts(v, n, h):
            n_s = SHARE_SLOTS[h]
            vdo(v, nc.vector.tensor_tensor(slot8[:, 0:n_s, :], par("slot", 0, n_s)[:, :, None].broadcast_to([P, n_s, EXPERTS]),
                                           e8[:, 1, :][:, None, :].broadcast_to([P, n_s, EXPERTS]), ALU.is_ge))
            vdo(v, nc.vector.tensor_reduce(slotf[:, 0:n_s], slot8[:, 0:n_s, :], AX, ALU.add))
            vdo(v, nc.vector.tensor_scalar(slotf[:, 0:n_s], slotf[:, 0:n_s], float(EXPERTS - 1), None, ALU.min))
            nc.vector.tensor_copy(expert_of[:, SLOT_AT[h]:SLOT_AT[h] + n_s], slotf[:, 0:n_s]
                                  ).then_inc(sg("experts_ready"), 1)

        PLACING = (first_choice, second_choice, weights, count_rows, sorted_places, tile_experts)

        def scatter_gpsimd(pool, n, src, flow):
            for s in range(BATCH + (n == 0)):
                flow(s)
            pool.wait_ge(sg("zeroed"), 16 * 4)
            for h in range(2):
                pool.wait_ge(sg("rows_ready"), n * 2 + h + 1)
                for t in range(SHARE_T[h], SHARE_T[h + 1]):
                    if n == 1 and t % TPB == 0:
                        for k in range(2):
                            pool.wait_ge(sg(f"xe{k}_ready"), t // TPB + 1)
                    for k in range(2):
                        nc.gpsimd.indirect_dma_start(
                            rows_d[n][h][:, :], bass.IndirectOffsetOnAxis(ap=row_of[:, k, t:t + 1], axis=0),
                            src[k][:, t, :], None).then_inc(sg(f"sorted{h}"), 16)
                    if n == 1 and t == 0:
                        flow(BATCH)

        AHEAD = (1, 4, 7, 10, 12, 14, 16)

        def gather_gpsimd(pool, n, dst, flow):
            def gather(h, t):
                for k in range(2):
                    nc.gpsimd.indirect_dma_start(
                        dst[k][:, t, :], None, made_d[n][h][:, :],
                        bass.IndirectOffsetOnAxis(ap=row_of[:, k, t:t + 1], axis=0)
                    ).then_inc(sg(f"back{t // TPB}"), 16)

            for h in range(2):
                for q in range(2):
                    pool.wait_ge(sg(f"made{q}"), 16 * (n * SLOTS + SLOT_AT[h] + SHARE_SLOTS[h]) // 8)
                for t in range(SHARE_T[h], SHARE_T[h + 1]):
                    gather(h, t)
                    done = t + 1 - SHARE_T[1]
                    if done in AHEAD:
                        flow(AHEAD.index(done))
            for s in range(len(AHEAD), BATCH + 1):
                flow(s)

        def shared_tensor(pe):
            pe.wait_ge(sg("experts_in"), 32)

            def up(b):
                pe.wait_ge(sg("hs_ready"), b + 1)
                for c in range(4):
                    i = nc.tensor.matmul(bank[:, c, :], experts_up[:, EXPERTS, c * P:(c + 1) * P],
                                         xt_all[:, bass.ds(b * SEQ, SEQ)], start=True, stop=True)
                i.then_inc(sg("su_done"), 1)

            def down(b, p):
                pe.wait_ge(sg("hs_ready"), b + 2)
                pe.wait_ge(sg("acc_ready"), b + 1)
                for j in range(TPB):
                    for m in range(2):
                        i = nc.tensor.matmul(bank[:, 4 + p, j * P:(j + 1) * P], hs[:, p, m, j * P:(j + 1) * P],
                                             experts_down[:, EXPERTS, m, :], start=(m == 0), stop=(m == 1))
                i.then_inc(sg("sd_done"), 1)

            up(0)
            for b in range(BATCH):
                if b + 1 < BATCH:
                    up(b + 1)
                down(b, b % 2)
                if b in (0, 3):
                    rank(pe, 0, b // 3)

        def shared_scalar(act):
            act.sem_inc(sg("acc_ready"), 2)
            silu(act, 0)
            with act.Fori(0, (BATCH - 2) // 2) as r:
                silu(act, 2 * r + 1)
                out_shared(act, 2 * r, 0)
                silu(act, 2 * r + 2)
                out_shared(act, 2 * r + 1, 1)
            silu(act, BATCH - 1)
            out_shared(act, BATCH - 2, 0)
            out_shared(act, BATCH - 1, 1)

        def silu(act, b):
            act.wait_ge(sg("su_done"), b + 1)
            act.wait_ge(sg("hs_ready"), b + 1)
            nc.scalar.activation(sgs[:, :, :], bank[:, 0:2, :], ACT.Silu).then_inc(sg("sgs_ready"), 1)

        def out_shared(act, b, p):
            act.wait_ge(sg("sd_done"), b + 1)
            nc.scalar.activation(o_all[:, bass.ds(b * TPB, TPB), :],
                                 bank[:, 4 + p, :].rearrange("p (j c) -> p j c", j=TPB), ACT.Identity
                                 ).then_inc(sg("acc_ready"), 1)

        def shared_vector(v):
            v.sem_inc(sg("hs_ready"), 1)
            steps = [(h, step) for h in range(2) for step in PLACING]
            upto = (0, 2, 5, 7, 8, 10, 12, 12, 12)
            for b in range(BATCH):
                v.wait_ge(sg("sgs_ready"), b + 1)
                v.wait_ge(sg("acc_ready"), b + 1)
                nc.vector.tensor_tensor(hs[:, b % 2], sgs[:, :, :], bank[:, 2:4, :], ALU.mult).then_inc(sg("hs_ready"), 1)
                for h, step in steps[upto[b]:upto[b + 1]]:
                    if step is first_choice:
                        place0_keys(v, h)
                    step(v, 0, h)

        LAG = 3
        ROUND = 16
        XT, GU, HT, YB = 0, 2, 4, 6

        def tiles_on(eng, slot):
            for m in range(ROUND):
                slot(m, m, 0)
            with eng.Fori(1, SLOTS // ROUND) as r:
                for m in range(ROUND):
                    slot(r * ROUND + m, m, r)
            for m in range(LAG):
                slot(SLOTS + m, m, SLOTS // ROUND)

        def has(s, lag):
            return not isinstance(s, int) or 0 <= s - lag < SLOTS

        def need(eng, name, value, base=0):
            if not isinstance(value, int) or value > 0:
                eng.wait_ge(sg(name), base + value)

        def experts_tensor(pe, n):
            at0 = n * SLOTS
            dma0 = n * 16 * (SLOTS // 8)
            pe.wait_ge(sg("experts_ready"), 2 * (n + 1))
            pe.wait_ge(sg("experts_in"), 32 * (n + 1))

            def expert(tile):
                return pe.value_load(expert_of[0:1, bass.ds(tile, 1)], min_val=0, max_val=EXPERTS - 1)

            loaded = {}

            def slot(s, m, r):
                if m == 0:
                    loaded.clear()
                    if has(s, 1) and has(s, 3):
                        loaded[-1] = expert(s - 1)
                if has(s, 0):
                    if m % 4 == 0:
                        pe.wait_ge(sg(f"rows_in{m // 4 % 2}"), dma0 + 16 * (r * (ROUND // 8) + m // 8 + 1))
                    nc.tensor.transpose(bank[:, XT + m % 2, 0:P], xr[:, m // 4 % 2, m % 4, :], ident).then_inc(sg("x_turned"), 1)
                if has(s, 1):
                    o = (m - 1) % 2
                    e = loaded[m - 1]
                    need(pe, "xT_in", s, at0)
                    nc.tensor.matmul(bank[:, GU + o, :], xT2[:, o, :], experts_up[:, e, :], start=True,
                                     stop=True).then_inc(sg("gu_done"), 1)
                if has(s, 0) and m < ROUND - 1:
                    loaded[m] = expert(s)
                if has(s, 3) and m - 3 not in loaded:
                    loaded[m - 3] = expert(s - 3)
                if has(s, 2):
                    o = m % 2
                    need(pe, "hb_ready", s - 1, at0)
                    for c in range(2):
                        i = nc.tensor.transpose(bank[:, HT + o, c * P:(c + 1) * P], hb[:, o, c * P:(c + 1) * P], ident)
                    i.then_inc(sg("h_turned"), 1)
                if has(s, 3):
                    o = (m - 3) % 2
                    e = loaded[m - 3]
                    need(pe, "hT_in", s - 2, at0)
                    need(pe, "y_out", s - 4, at0)
                    for c in range(2):
                        i = nc.tensor.matmul(bank[:, YB + o, 0:H], hTb[:, o, c * P:(c + 1) * P], experts_down[:, e, c, :],
                                             start=(c == 0), stop=(c == 1))
                    i.then_inc(sg("y_done"), 1)

            tiles_on(pe, slot)

        def experts_scalar(act, n):
            at0 = n * SLOTS

            def slot(s, m, r):
                if has(s, 0):
                    need(act, "x_turned", s + 1, at0)
                    need(act, "gu_done", s - 1, at0)
                    nc.scalar.activation(xT2[:, m % 2, :], bank[:, XT + m % 2, 0:P], ACT.Identity).then_inc(sg("xT_in"), 1)
                if has(s, 1):
                    o = (m - 1) % 2
                    need(act, "gu_done", s, at0)
                    need(act, "hb_ready", s - 2, at0)
                    nc.scalar.activation(sgb[:, o, :], bank[:, GU + o, 0:MID], ACT.Silu).then_inc(sg("silu_ready"), 1)
                if has(s, 2):
                    o = m % 2
                    need(act, "h_turned", s - 1, at0)
                    need(act, "y_done", s - 3, at0)
                    nc.scalar.activation(hTb[:, o, :], bank[:, HT + o, 0:MID], ACT.Identity).then_inc(sg("hT_in"), 1)

            tiles_on(act, slot)

        def experts_vector(v, n):
            at0 = n * SLOTS
            dma0 = n * 16 * (SLOTS // 8)

            def slot(s, m, r):
                if has(s, 1):
                    o = (m - 1) % 2
                    need(v, "silu_ready", s, at0)
                    need(v, "h_turned", s - 2, at0)
                    nc.vector.tensor_tensor(hb[:, o, :], sgb[:, o, :], bank[:, GU + o, MID:2 * MID],
                                            ALU.mult).then_inc(sg("hb_ready"), 1)
                if has(s, 3):
                    o = (m - 3) % 2
                    k = (m - 3) % ROUND
                    need(v, "y_done", s - 2, at0)
                    if k % 4 == 0 and not (isinstance(r, int) and r == 0 and k < 8):
                        v.wait_ge(sg(f"made{k // 4 % 2}"), dma0 + 16 * (r * (ROUND // 8) + k // 8))
                    nc.vector.tensor_copy(yb[:, k // 4 % 2, k % 4, :], bank[:, YB + o, 0:H]).then_inc(sg("y_out"), 1)

            tiles_on(v, slot)

        def experts_sync(sync, n):
            at0 = n * SLOTS
            four = lambda d, k: d.rearrange("(a j p) c -> p a j c", j=4, p=P)[:, k]

            def load(h, k, o):
                sync.dma_start(xr[:, o], four(rows_d[n][h], k)).then_inc(sg(f"rows_in{o}"), 16)

            def store(h, k, o):
                sync.wait_ge(sg("y_out"), at0 + SLOT_AT[h] + 4 * k + 4)
                sync.dma_start(four(made_d[n][h], k), yb[:, o]).then_inc(sg(f"made{o}"), 16)

            def sorted_rows(h):
                sync.wait_ge(sg(f"sorted{h}"), 16 * 2 * SHARES[h] * TPB * (n + 1))

            sorted_rows(0)
            load(0, 0, 0)
            load(0, 1, 1)
            for h in range(2):
                with sync.Fori(0, SHARE_SLOTS[h] // 8 - 1) as r:
                    for o in range(2):
                        k = 2 * r + o
                        sync.wait_ge(sg("x_turned"), at0 + SLOT_AT[h] + 4 * k + 4)
                        load(h, k + 2, o)
                        store(h, k, o)
                if h == 0:
                    sorted_rows(1)
                for o in range(2):
                    k = SHARE_SLOTS[h] // 4 - 2 + o
                    if h == 0:
                        sync.wait_ge(sg("x_turned"), at0 + 4 * k + 4)
                        load(1, o, o)
                    store(h, k, o)

        def place0_keys(v, h):
            tl, of, _ = share_of(h)
            vdo(v, nc.vector.tensor_tensor(of(key), of(lg), par("beta0")[:, None, :].broadcast_to([P, SHARES[h] * TPB, EXPERTS]),
                                           ALU.add))
            v.wait_ge(sg("pr_ready"), h + 1)

        def moe0_vector(v):
            shared_vector(v)
            experts_vector(v, 0)
            v.wait_ge(sg("acc_ready"), 2 + BATCH)

            def combine(b):
                v.wait_ge(sg(f"back{b}"), 16 * 2 * TPB)
                for k in range(2):
                    for t in range(b * TPB, (b + 1) * TPB):
                        i = nc.vector.scalar_tensor_tensor(o_all[:, t, :], got[k][:, t, :], gain[:, k, t:t + 1],
                                                           o_all[:, t, :], ALU.mult, ALU.add)
                    vdo(v, i)
                stats(v, o_all, b)

            flow_vector(v, "mixture", o_all, combine, True, lambda s: ssm_slot_vector(v, s), SSM_LAG)

        got = [tiles(big[0]), tiles(big[1])]

        def moe0_scalar(act):
            def share(h):
                tl, of, _ = share_of(h)
                act.wait_ge(sg("lg_out"), SHARE_B[h + 1])
                nc.scalar.activation(of(pr), of(lg), ACT.Sigmoid).then_inc(sg("pr_ready"), 1)

            flow_scalar(act, "memory", o_all,
                        lambda s, asked: route_slot_scalar(act, 0, s, asked, share), ROUTE_LAG)
            shared_scalar(act)
            experts_scalar(act, 0)
            flow_scalar(act, "mixture", o_all, lambda s, asked: ssm_slot_scalar(act, s, asked), SSM_LAG)

        def moe0_tensor(pe):
            route_tensor(pe, 0)
            shared_tensor(pe)
            experts_tensor(pe, 0)

        def moe0_gpsimd(pool):
            scatter_gpsimd(pool, 0, [rows, rows], lambda s: flow_gpsimd(s, False))

            gather_gpsimd(pool, 0, got, lambda s: flow_gpsimd(s, True))

        dt, xc, sz = big[0], big[1], big[2]
        f_res = tiles(big[3])
        end_of_moe = carved[0]
        carved[0] = 0
        xf = carve("xf", [P, 2, TPB, H])
        xfT = carve("xfT", [P, 2, SEQ])
        xxp = carve("xxp", [P, 2, SEQ + 2])
        cvd = carve("cvd", [P, 2, SEQ])
        bcr = carve("bcr", [P, 2, SEQ])
        bc3 = carve("bc3", [P, TOKENS], BF16)
        pick = carve("pick", [P, 2 * STATE, P], BF16)
        neg_a = carve("neg_a", [P, 2, STATE])
        da = carve("da", [P, 2, SEQ])
        db = carve("db", [P, 4, SEQ])
        sta = carve("sta", [P, 2, SEQ])
        cs = carve("cs", [P, 2, SEQ])
        yc = carve("yc", [P, 4, SEQ])
        yf = carve("yf", [P, 2, SEQ])
        lnx = carve("lnx", [P, TPB, H])
        ROWS = 3 * 2 * STATE

        def at_b(a, b):
            return a[:, bass.ds(b * SEQ, SEQ)]

        SSM_LAG = 2

        def ssm_slots(eng, slot):
            slot(0, 0)
            slot(1, 1)
            with eng.Fori(1, BATCH // 2) as r:
                slot(2 * r, 0)
                slot(2 * r + 1, 1)
            for s in range(SSM_LAG):
                slot(BATCH + s, s % 2)

        def in_batch(s, lag):
            return not isinstance(s, int) or 0 <= s - lag < BATCH

        def ssm_start(v):
            nc.vector.memset(xxp[:, :, 0:SEQ + 2], 0.0).then_inc(sg("xxp_zero"), 1)
            nc.vector.tensor_copy(pick[0:ROWS], par("pick")[0:ROWS, :, None].broadcast_to([ROWS, 2 * STATE, P])
                                  ).then_inc(sg("pick_ready"), 1)
            v.sem_inc(sg("cv_free"), 2)

        def ssm_slot_vector(v, s):
            if s == 0:
                ssm_start(v)
            if in_batch(s, 2):
                b, p = s - 2, s % 2
                v.wait_ge(sg("bc_first"), b + 1)
                nc.vector.tensor_scalar(at_b(dt, b), bank[:, 6, :], par("b_dt"), None, ALU.add)
                nc.vector.tensor_tensor(bcr[0:64, p], bank[0:64, 7, :], at_b(bc3, b)[0:64], ALU.subtract).then_inc(sg("bc_rest"), 1)
            if in_batch(s, 1):
                b, p = s - 1, (s - 1) % 2
                v.wait_ge(sg("xx_ready"), b + 1)
                v.wait_ge(sg("xc_ready"), b + 1)
                w = lambda k: par("sconv", k, k + 1)
                vdo(v, nc.vector.tensor_scalar(cvd[:, p], xxp[:, p, 0:SEQ], w(0), None, ALU.mult))
                vdo(v, nc.vector.scalar_tensor_tensor(cvd[:, p], xxp[:, p, 1:SEQ + 1], w(1), cvd[:, p], ALU.mult, ALU.add))
                nc.vector.scalar_tensor_tensor(cvd[:, p], xxp[:, p, 2:SEQ + 2], w(2), cvd[:, p],
                                               ALU.mult, ALU.add).then_inc(sg("cv_done"), 1)
            if in_batch(s, 2):
                b, p = s - 2, s % 2
                v.wait_ge(sg("bc_second"), b + 1)
                nc.vector.tensor_tensor(at_b(bc3, b)[0:32], bcr[0:32, p], at_b(bc3, b)[0:32], ALU.subtract).then_inc(sg("bc_third"), 1)

        def quarter(a, q):
            return a[:, q * TOKENS // 4:(q + 1) * TOKENS // 4]

        def ssm_prep_vector(v):
            v.wait_ge(sg("dt_parts"), 1)
            nc.vector.tensor_scalar(neg_a[:, 1, :], neg_a[:, 0, :], -1.0, None, ALU.mult).then_inc(sg("dt_ready"), 1)
            for q in range(4):
                v.wait_ge(sg("dt_parts"), q + 2)
                nc.vector.scalar_tensor_tensor(quarter(dt, q), quarter(dt, q), 0.0, quarter(big[3], q),
                                               ALU.max, ALU.add).then_inc(sg("dt_ready"), 1)

        def ssm_prep_tensor(pe):
            pe.sem_inc(sg("f_turned"), 2)

            def head(b, p):
                pe.wait_ge(sg("f_rows"), b + 1)
                for j in range(TPB):
                    i = nc.tensor.transpose(bank[:, p, j * P:(j + 1) * P], xf[:, p, j, :], ident)
                i.then_inc(sg("f_turned"), 1)
                pe.wait_ge(sg("fT_ready"), b + 1)
                pe.wait_ge(sg("z_ready"), b + 1)
                nc.tensor.matmul(bank[:, 2 + p, :], par("w_in", 0, H), xfT[:, p], start=True, stop=True)
                nc.tensor.matmul(bank[:, 4 + p, :], par("w_in", H, 2 * H), xfT[:, p], start=True,
                                 stop=True).then_inc(sg("xz_done"), 1)

            def tail(b, p):
                pe.wait_ge(sg("xc_ready"), b + 3)
                pe.wait_ge(sg("bc_read"), b + 1)
                nc.tensor.matmul(bank[:, 6, :], par("w_dt"), at_b(xc, b), start=True, stop=True)
                nc.tensor.matmul(bank[0:ROWS, 7, :], par("w_bc"), at_b(xc, b), start=True,
                                 stop=True).then_inc(sg("dtbc_done"), 1)

            def slot(s, p):
                if in_batch(s, 0):
                    head(s, p)
                if in_batch(s, 1):
                    tail(s - 1, 1 - p)

            ssm_slots(pe, slot)

        def ssm_prep_scalar(act):
            act.wait_ge(sg("bc_second"), BATCH)
            nc.scalar.activation(big[3][:, :], big[3][:, :], ACT.Exp, scale=-1.0).then_inc(a_step, ca.one())
            nc.scalar.activation(neg_a[:, 0, :], par("a_log"), ACT.Exp).then_inc(sg("dt_parts"), 1)
            act.wait_ge(a_step, ca.now)
            for q in range(4):
                nc.scalar.activation(quarter(big[3], q), quarter(big[3], q), ACT.Ln, bias=1.0).then_inc(sg("dt_parts"), 1)

        def ssm_slot_scalar(act, s, asked):
            p = s % 2
            if s == 0:
                act.sem_inc(sg("z_ready"), 2)
                act.sem_inc(sg("xz_free"), 2)
                act.sem_inc(sg("xc_ready"), 2)
                act.sem_inc(sg("bc_read"), 1)
                act.wait_ge(sg("xxp_zero"), 1)
            if in_batch(s, 0):
                act.wait_ge(sg("rstd_ready"), asked)
                act.wait_ge(sg("f_turned"), s + 1)
                for k in range(TPB):
                    t = s * TPB + k
                    i = nc.scalar.activation(xf[:, p, k, :], xres[:, t, :], ACT.Identity, bias=shift2[:, t:t + 1],
                                             scale=rstd2[:, t:t + 1])
                i.then_inc(sg("f_rows"), 1)
            if in_batch(s, 2):
                b = s - 2
                act.wait_ge(sg("dtbc_done"), b + 1)
                nc.scalar.activation(at_b(bc3, b)[0:ROWS], bank[0:ROWS, 7, :], ACT.Identity)
                nc.scalar.activation(at_b(big[3], b), bank[:, 6, :], ACT.Abs, bias=par("b_dt")).then_inc(sg("bc_first"), 1)
            if in_batch(s, 0):
                act.wait_ge(sg("f_turned"), s + 3)
                act.wait_ge(sg("xz_free"), s + 1)
                nc.scalar.activation(xfT[:, p], bank[:, p, :], ACT.Identity, bias=par("beta"),
                                     scale=par("gamma")).then_inc(sg("fT_ready"), 1)
            if in_batch(s, 2):
                b = s - 2
                act.wait_ge(sg("bc_rest"), b + 1)
                act.sem_inc(sg("bc_read"), 1)
                nc.scalar.activation(at_b(bc3, b)[0:64], bcr[0:64, p], ACT.Identity).then_inc(sg("bc_second"), 1)
            if in_batch(s, 1):
                b = s - 1
                act.wait_ge(sg("cv_done"), b + 1)
                act.sem_inc(sg("cv_free"), 1)
                nc.scalar.activation(at_b(xc, b), cvd[:, 1 - p], ACT.Silu).then_inc(sg("xc_ready"), 1)
            if in_batch(s, 0):
                act.wait_ge(sg("xz_done"), s + 1)
                act.sem_inc(sg("xz_free"), 1)
                act.wait_ge(sg("cv_free"), s + 1)
                nc.scalar.activation(xxp[:, p, 1:SEQ + 1], bank[:, 2 + p, :], ACT.Identity).then_inc(sg("xx_ready"), 1)
                nc.scalar.activation(at_b(sz, s), bank[:, 4 + p, :], ACT.Silu).then_inc(sg("z_ready"), 1)

        BB, CB, Y_B, O_B = 0, 2, 4, 5

        Y_LAG = 3

        def batches_on(eng, batch):
            batch(0, False)
            with eng.Fori(1, BATCH) as b:
                batch(b, True)

        def scan_vector(v):
            v.wait_ge(sg("dt_ready"), 5)

            def scan(u, s):
                p = s % 2
                v.wait_ge(sg("da_ready"), u + 1)
                v.wait_ge(sg("db_ready"), u + 1)
                need(v, "yc_ready", u - 1)
                nc.vector.tensor_tensor_scan(sta[:, p], da[:, p], db[:, s % 4], 0.0, ALU.mult, ALU.add).then_inc(sg("state_ready"), 1)

            def final(b):
                v.wait_ge(sg("y_summed"), 16 * b + 16)
                nc.vector.scalar_tensor_tensor(yf[:, 0], at_b(xc, b), par("skip_d"), bank[:, Y_B, :],
                                               ALU.mult, ALU.add).then_inc(sg("y_read"), 1)

            def result(b):
                v.wait_ge(sg("lnx"), b + 1)
                v.wait_ge(sg("out_done_f"), b + 1)
                nc.vector.tensor_tensor(f_res[:, bass.ds(b * TPB, TPB), :], lnx[:, :, :],
                                        bank[:, O_B, :].rearrange("p (k c) -> p k c", k=TPB), ALU.add).then_inc(sg("res_ready"), 1)
                v.wait_ge(sg("res_ready"), b + 1)
                for k in range(TPB):
                    i = nc.vector.bn_stats(st[:, b * TPB + k, :], f_res[:, b * TPB + k, :])
                i.then_inc(sg("f_stats"), 1)

            def batch(b, back):
                for s in range(STATE):
                    u = b * STATE + s
                    if back and s == Y_LAG:
                        final(b - 1)
                    if back and s == 8:
                        result(b - 1)
                    v.wait_ge(sg("b_done"), u + 1)
                    need(v, "state_ready", u - 3)
                    nc.vector.tensor_tensor(db[:, s % 4], at_b(dt, b), bank[:, BB + s % 2, :], ALU.mult).then_inc(sg("db_ready"), 1)
                    if s > 0 or back:
                        scan(u - 1, (s - 1) % STATE)

            batches_on(v, batch)
            scan(BATCH * STATE - 1, STATE - 1)
            final(BATCH - 1)
            result(BATCH - 1)
            v.wait_ge(sg("f_stats"), BATCH)
            flow_vector(v, "scan", f_res, lambda b: None, True,
                        lambda s: route_slot_vector(v, 1, lead1, place1, s), ROUTE_LAG)

        def scan_scalar(act):
            act.wait_ge(sg("dt_ready"), 2)

            def batch(b, back):
                for s in range(STATE):
                    u = b * STATE + s
                    need(act, "state_ready", u - 1)
                    act.sem_inc(sg("act_go"), 1)
                    nc.scalar.activation(da[:, s % 2], at_b(dt, b), ACT.Exp, scale=neg_a[:, 1, s:s + 1]).then_inc(sg("da_ready"), 1)
                    act.wait_ge(sg("c_done"), u + 1)
                    need(act, "yc_ready", u - 1)
                    nc.scalar.activation(cs[:, s % 2], bank[:, CB + s % 2, :], ACT.Identity).then_inc(sg("cs_ready"), 1)
                    if back and s == 4:
                        residual_rows(b - 1)

            def residual_rows(b):
                for k in range(TPB):
                    t = b * TPB + k
                    i = nc.scalar.activation(lnx[:, k, :], xres[:, t, :], ACT.Identity, bias=shift[:, bass.ds(t, 1)],
                                             scale=rstd[:, bass.ds(t, 1)])
                i.then_inc(sg("lnx"), 1)

            batches_on(act, batch)
            residual_rows(BATCH - 1)

        def scan_gpsimd(pool):
            def batch(b, back):
                for s in range(STATE):
                    u = b * STATE + s
                    if back and s == Y_LAG - 1:
                        gate(b - 1)
                    pool.wait_ge(sg("state_ready"), u + 1)
                    pool.wait_ge(sg("cs_ready"), u + 1)
                    need(pool, "y_summed", u - 3)
                    nc.gpsimd.tensor_tensor(yc[:, s % 4], sta[:, s % 2], cs[:, s % 2], ALU.mult).then_inc(sg("yc_ready"), 1)

            def gate(b):
                pool.wait_ge(sg("y_read"), b + 1)
                nc.gpsimd.tensor_tensor(yf[:, 1], yf[:, 0], at_b(sz, b), ALU.mult).then_inc(sg("yf_ready"), 1)

            batches_on(pool, batch)
            gate(BATCH - 1)
        def scan_tensor(pe):
            pe.wait_ge(sg("pick_ready"), 1)
            pe.wait_ge(sg("bc_third"), BATCH)
            pe.wait_ge(sg("dt_ready"), 1)

            def summed(b, s):
                u = b * STATE + s
                if s == 0:
                    need(pe, "y_read", b)
                pe.wait_ge(sg("yc_ready"), u + 1)
                nc.tensor.matmul(bank[:, Y_B, :], ident, yc[:, s % 4], start=(s == 0), stop=(s == STATE - 1)
                                 ).then_inc(sg("y_summed"), 1)

            def output(b):
                pe.wait_ge(sg("yf_ready"), b + 1)
                need(pe, "res_ready", b)
                for k in range(TPB):
                    i = nc.tensor.matmul(bank[:, O_B, k * H:(k + 1) * H], yf[:, 1, k * P:(k + 1) * P], par("w_out"),
                                         start=True, stop=True)
                i.then_inc(sg("out_done_f"), 1)

            def batch(b, back):
                for s in range(STATE):
                    u = b * STATE + s
                    need(pe, "db_ready", u - 1)
                    nc.tensor.matmul(bank[:, BB + s % 2, :], pick[0:ROWS, s, :], at_b(bc3, b)[0:ROWS],
                                     start=True, stop=True).then_inc(sg("b_done"), 1)
                    need(pe, "cs_ready", u - 1)
                    nc.tensor.matmul(bank[:, CB + s % 2, :], pick[0:ROWS, STATE + s, :], at_b(bc3, b)[0:ROWS],
                                     start=True, stop=True).then_inc(sg("c_done"), 1)
                    if s >= Y_LAG:
                        summed(b, s - Y_LAG)
                    elif back:
                        summed(b - 1, STATE - Y_LAG + s)
                    if back and s == 4:
                        output(b - 1)

            batches_on(pe, batch)
            for s in range(STATE - Y_LAG, STATE):
                summed(BATCH - 1, s)
            output(BATCH - 1)

        carved[0] = end_of_moe
        xe = [tiles(big[0]), tiles(big[1])]
        rows1 = tiles(big[2])

        def lead1(b):
            four = slice(b * TPB, (b + 1) * TPB)
            nc.vector.wait_ge(sg("rows_normed"), b + 1)
            over = lambda a: a[:, None, :].broadcast_to([P, TPB, H])
            vdo(nc.vector, nc.vector.tensor_tensor(rows1[:, four, :], rows1[:, four, :], over(par("ln_g")), ALU.mult))
            nc.vector.tensor_tensor(rows1[:, four, :], rows1[:, four, :], over(par("ln_b")),
                                    ALU.add).then_inc(sg("xa_ready"), 1)

        def place1(v, h):
            tl, of, wide = share_of(h)
            m1 = lambda k: m32[:, k, tl]
            vdo(v, nc.vector.tensor_scalar(of(lg), of(lg), -10000.0, 10000.0, ALU.max, ALU.min))
            vdo(v, nc.vector.tensor_reduce(m1(0), of(lg), AX, ALU.max))
            nc.vector.tensor_tensor(of(key), of(lg), wide(m32[:, 0]), ALU.subtract).then_inc(sg("key_ready"), 1)
            v.wait_ge(sg("pr_ready"), 2 + h + 1)
            vdo(v, nc.vector.tensor_reduce(m1(0), of(pr), AX, ALU.add))
            vdo(v, nc.vector.tensor_scalar(m1(0), m1(0), 1e-8, None, ALU.add))
            vdo(v, nc.vector.reciprocal(m1(1), m1(0)))
            vdo(v, nc.vector.tensor_tensor(of(pr), of(pr), wide(m32[:, 1]), ALU.mult))
            vdo(v, nc.vector.tensor_scalar(of(pr), of(pr), 1e-8, 1.0, ALU.max, ALU.min))
            vdo(v, nc.vector.tensor_copy(of(key), of(pr)))
            for step in PLACING:
                step(v, 1, h)
            for b in share_batches(h):
                for t in range(b * TPB, (b + 1) * TPB):
                    i = nc.vector.tensor_scalar(xe[0][:, t, :], rows1[:, t, :], gain[:, 0, t:t + 1], None, ALU.mult)
                i.then_inc(sg("xe0_ready"), 1)

        last_asked = {}

        def share_batches(h):
            return range(SHARE_B[h], SHARE_B[h + 1])

        def moe1_vector(v):
            experts_vector(v, 1)
            for s in range(BATCH + 2):
                if s < BATCH:
                    four = slice(s * TPB, (s + 1) * TPB)
                    v.wait_ge(sg(f"back{s}"), 2 * 16 * 2 * TPB)
                    v.wait_ge(sg("x_normed"), s + 1)
                    for k in range(2):
                        vdo(v, nc.vector.tensor_tensor(f_res[:, four, :], f_res[:, four, :], xe[k][:, four, :], ALU.add))
                    stats(v, f_res, s)
                    last_asked[s] = moments(v, s * TPB, (s + 1) * TPB)
                if 0 <= s - 1 < BATCH:
                    four = slice((s - 1) * TPB, s * TPB)
                    v.wait_ge(sg("std_ready"), s)
                    vdo(v, nc.vector.reciprocal(rstd[:, four], var2[:, four]))
                    nc.vector.tensor_tensor(shift[:, four], neg_mean[:, four], rstd[:, four], ALU.mult
                                            ).then_inc(sg("last_scale"), 1)
                if s >= 2:
                    four = slice((s - 2) * TPB, (s - 1) * TPB)
                    n_normed[0] += 1
                    v.wait_ge(sg("normed"), n_normed[0])
                    nc.vector.tensor_tensor(xres[:, four, :], xres[:, four, :], f_res[:, four, :], ALU.add).then_inc(sg("x_out"), 1)

        def moe1_scalar(act):
            def share(h):
                tl, of, _ = share_of(h)
                act.wait_ge(sg("key_ready"), h + 1)
                nc.scalar.activation(of(pr), of(key), ACT.Exp).then_inc(sg("pr_ready"), 1)
                act.wait_ge(sg("rows_ready"), 2 + h + 1)
                for b in share_batches(h):
                    for t in range(b * TPB, (b + 1) * TPB):
                        i = nc.scalar.activation(xe[1][:, t, :], rows1[:, t, :], ACT.Identity, scale=gain[:, 1, t:t + 1])
                    i.then_inc(sg("xe1_ready"), 1)

            flow_scalar(act, "scan", f_res,
                        lambda s, asked: route_slot_scalar(act, 1, s, asked, share), ROUTE_LAG)
            experts_scalar(act, 1)
            for s in range(-1, BATCH + 1):
                if s + 1 < BATCH:
                    layer_norm(f_res, xres, s + 1).then_inc(sg("x_normed"), 1)
                if 0 <= s < BATCH:
                    four = slice(s * TPB, (s + 1) * TPB)
                    act.wait_ge(sg("var_ready"), last_asked[s])
                    nc.scalar.activation(var2[:, four], var[:, four], ACT.Sqrt).then_inc(sg("std_ready"), 1)
                if s >= 1:
                    act.wait_ge(sg("last_scale"), s)
                    layer_norm(f_res, f_res, s - 1).then_inc(sg("normed"), 1)

        def moe1_tensor(pe):
            route_tensor(pe, 1)
            experts_tensor(pe, 1)

        def moe1_gpsimd(pool):
            scatter_gpsimd(pool, 1, xe, lambda s: flow_gpsimd(s, True))
            gather_gpsimd(pool, 1, xe, lambda s: None)

        def moe1_sync(sync):
            sync.wait_ge(sg("y_out"), SLOTS)
            sync.dma_start(experts_up[:, 0:EXPERTS, :], up1_d).then_inc(sg("experts_in"), 16)
            sync.dma_start(experts_down[:, 0:EXPERTS, :, :], down1_d).then_inc(sg("experts_in"), 16)
            experts_sync(sync, 1)
            for b in range(BATCH):
                sync.wait_ge(sg("x_out"), b + 1)
                sync.dma_start(out_d.rearrange("(t p) c -> p t c", p=P)[:, b * TPB:(b + 1) * TPB, :],
                               xres[:, b * TPB:(b + 1) * TPB, :]).then_inc(sg("stored"), 16)
            sync.wait_ge(sg("stored"), 16 * BATCH)

        block = ctx.enter_context(nc.Block())

        @block.sync
        def _(sync):
            prep_sync(sync)
            experts_sync(sync, 0)
            moe1_sync(sync)

        @block.gpsimd
        def _(pool):
            prep_gpsimd(pool)
            recur_gpsimd(pool)
            post_gpsimd(pool)
            moe0_gpsimd(pool)
            scan_gpsimd(pool)
            moe1_gpsimd(pool)

        @block.vector
        def _(v):
            prep_vector(v)
            recur_vector(v)
            post_vector(v)
            moe0_vector(v)
            ssm_prep_vector(v)
            scan_vector(v)
            moe1_vector(v)

        @block.tensor
        def _(pe):
            prep_tensor(pe)
            recur_tensor(pe)
            post_tensor(pe)
            moe0_tensor(pe)
            ssm_prep_tensor(pe)
            scan_tensor(pe)
            moe1_tensor(pe)

        @block.scalar
        def _(act):
            prep_scalar(act)
            recur_scalar(act)
            post_scalar(act)
            moe0_scalar(act)
            ssm_prep_scalar(act)
            scan_scalar(act)
            moe1_scalar(act)


def _packed(x):
    def rows(v):
        return np.broadcast_to(v[None, :], (P, v.shape[0]))

    def bd(v):
        return np.tile(v, (B4, 1))

    part = {}
    part["proj"] = np.concatenate([x["L0_attn_W" + n].T for n in "kvq"] +
                                  [x["L0_attn_" + n + "W"].T for n in "aet"], axis=1)
    part["gate"] = x["L0_attn_gW"].T
    part["gate_b"] = rows(x["L0_attn_gb"])
    part["norm_g"] = rows(x["L0_attn_norm_g"])
    wo = np.zeros((B4, D, B4, H), np.float32)
    for b in range(B4):
        wo[b, :, b, :] = x["L0_attn_Wo"].T
    part["wo"] = wo.reshape(P, B4 * H)
    part["conv_w"] = np.concatenate([bd(x[f"L0_attn_c{n}w"]) for n in "kvq"], axis=1)
    part["conv_b"] = np.concatenate([bd(x[f"L0_attn_c{n}b"][:, None]) for n in "kvq"], axis=1)
    part["bias3"] = np.concatenate([bd(x[f"L0_attn_{n}b"][:, None]) for n in "aet"], axis=1)
    part["mem"] = np.concatenate([bd(x["L0_attn_mW1"].T), bd(x["L0_attn_mW2"].T)], axis=1)
    part["route0"] = x["L0_ffn_gate_w"].T
    part["beta0"] = rows(x["L0_ffn_beta"])
    part["route1"] = x["L1_ffn_router_w"].T
    part["ln_g"] = rows(x["L1_ffn_ln_gamma"])
    part["ln_b"] = rows(x["L1_ffn_ln_beta"])
    part["w_in"] = x["L1_attn_W_in"].T
    part["w_bc"] = np.tile(x["L1_attn_W_x"].T, (1, 3))
    part["w_dt"] = x["L1_attn_W_dt"].T
    part["w_out"] = x["L1_attn_W_out"].T
    part["sconv"] = x["L1_attn_conv_w"][:, 0, :]
    part["b_dt"] = x["L1_attn_b_dt"][:, None]
    part["a_log"] = x["L1_attn_A_log"]
    part["skip_d"] = x["L1_attn_D_param"][:, None]
    part["gamma"] = x["L1_attn_gamma"][:, None]
    part["beta"] = x["L1_attn_beta"][:, None]
    p = np.arange(P)
    part["ident"] = np.eye(P)
    part["quad"] = (p[:, None] // D == p[None, :] // D)
    part["neg_i"] = -(p[:, None] % CHUNK == np.arange(CHUNK)[None, :]).astype(np.float32)
    part["mean_bd"] = (p[:, None] // D == p[None, :] // D) / D
    part["mean_sel"] = (p[:, None] // D == np.arange(B4 * 64)[None, :] // 64) / D
    part["before"] = (p[:, None] < p[None, :])
    part["ones"] = np.ones((P, P))
    part["rank8"] = rows(np.arange(EXPERTS, 0, -1))
    part["edge"] = rows(np.arange(TILES) * P)
    part["slot"] = rows(np.arange(max(SHARE_SLOTS)))
    part["pick"] = (p[:, None] % (2 * STATE) == np.arange(2 * STATE)[None, :])
    part["affine"] = rows(np.array([0.05, 1.0]))
    packed = np.zeros((P, PACKED), np.float32)
    for name, (at, width) in AT.items():
        assert part[name].shape == (P, width), (name, part[name].shape)
        packed[:, at:at + width] = part[name]
    return packed


def _experts(up, down):
    n = up.shape[0]
    return (np.ascontiguousarray(up.transpose(1, 0, 2)),
            np.ascontiguousarray(down.reshape(n, 2, P, H).transpose(2, 0, 1, 3)))


def kernel(**inputs):
    import concourse.bacc as _bacc
    from concourse.bass_utils import run_bass_kernel_spmd as _run

    x = {k: np.asarray(v) for k, v in inputs.items()}
    up0 = np.concatenate([np.concatenate([x["L0_ffn_gate_proj_w"], x["L0_ffn_shared_gate_w"]]),
                          np.concatenate([x["L0_ffn_up_proj_w"], x["L0_ffn_shared_up_w"]])], axis=2)
    down0 = np.concatenate([x["L0_ffn_down_proj_w"], x["L0_ffn_shared_down_w"]])
    up0, down0 = _experts(up0, down0)
    up1, down1 = _experts(x["L1_ffn_gate_up_w"].transpose(0, 2, 1), x["L1_ffn_down_w"].transpose(0, 2, 1))
    arrays = {"x": np.ascontiguousarray(x["L0_attn_hidden"]).reshape(TOKENS, H), "packed": _packed(x),
              "up0": up0, "down0": down0, "up1": up1, "down1": down1}
    nc = _bacc.Bacc("TRN2", target_bir_lowering=False, num_devices=1)
    args = [nc.dram_tensor(n, a.shape, F32, kind="ExternalInput").ap() for n, a in arrays.items()]
    out = nc.dram_tensor("out", (TOKENS, H), F32, kind="ExternalOutput").ap()
    build(nc, *args, out)
    r = _run(nc, [arrays], core_ids=[0])
    return r.results[0]["out"].reshape(BATCH, SEQ, H)
```
